# Optimizing a Trainium2 kernel written in Bass

```python
import numpy as np
import jax
import jax.numpy as jnp

def _softmax(x, axis=-1):
    return jax.nn.softmax(x, axis=axis)

def _gelu(x):
    return jax.nn.gelu(x, approximate=True)

def _silu(x):
    return jax.nn.silu(x)

def _sigmoid(x):
    return jax.nn.sigmoid(x)

def _layernorm(x, axis=-1, eps=1e-05):
    m = jnp.mean(x, axis=axis, keepdims=True)
    v = jnp.var(x, axis=axis, keepdims=True)
    return (x - m) / jnp.sqrt(v + eps)

def _scatter_add(tgt, idx, src, axis=0):
    return tgt.at[idx].add(src)

def _segment_sum(src, seg, n):
    return jax.ops.segment_sum(src, seg, n)
kernel_name = 'mk_gnn_resnorm_d4_gnn_r8_825189'

def setup_inputs(seed: int=0):
    np.random.seed(seed)
    _w = jnp.asarray

    def _rec_inputs():
        import jax
        import jax.numpy as jnp
        _gk = jax.random.key(seed)
        x = -8.776e-05 + 1 * jax.random.normal(jax.random.fold_in(_gk, 1), (6250, 256), jnp.float32)
        src = jax.random.randint(jax.random.fold_in(_gk, 2), (100000,), 0, 6250, jnp.int32)
        dst = jnp.minimum((6250 * jax.random.uniform(jax.random.fold_in(_gk, 3), (100000,)) ** 2.0).astype(jnp.int32), 49999)
        _o = jnp.argsort(dst, stable=True)
        src = src[_o]
        dst = dst[_o]
        edge_attr_12 = -1.02531e-05 + 0.999808 * jax.random.normal(jax.random.fold_in(_gk, 12), (100000, 12), jnp.float32)
        edge_attr_16 = 0.000130101 + 1.00012 * jax.random.normal(jax.random.fold_in(_gk, 13), (100000, 16), jnp.float32)
        edge_type_7 = jax.random.randint(jax.random.fold_in(_gk, 15), (100000,), 0, 7, jnp.int32)
        edge_type_8 = jax.random.randint(jax.random.fold_in(_gk, 16), (100000,), 0, 8, jnp.int32)
        edge_weight = jax.random.uniform(jax.random.fold_in(_gk, 17), (100000,), jnp.float32, 0.0, 0.999998)
        return (x, src, dst, edge_attr_12, edge_attr_16, edge_type_7, edge_type_8, edge_weight)
    x, src, dst, edge_attr_12, edge_attr_16, edge_type_7, edge_type_8, edge_weight = _rec_inputs()

    def _L0_gnn_setup():
        import jax, jax.numpy as jnp
        import numpy as np
        H, C = (8, 32)
        D = H * C
        NEG_SLOPE = 0.2
        SELF_LOOP_TYPE = 6
        EPS_LN = 1e-05
        EPS_BN = 1e-05

        def _gat_layer(x, src, dst, ea, et, Ws, Wd, a_s, a_d, We, ae, te, Wo, bo, b, lg, lb):
            N = x.shape[0]
            xs = (x @ Ws).reshape(N, H, C)
            xd = (x @ Wd).reshape(N, H, C)
            a_i = jnp.einsum('nhc,hc->nh', xd, a_s)
            a_j = jnp.einsum('nhc,hc->nh', xs, a_d)
            alpha = a_i[dst] + a_j[src]
            ef = (ea @ We).reshape(-1, H, C)
            alpha = alpha + jnp.einsum('ehc,hc->eh', ef, ae)
            tf = te[et].reshape(-1, H, C)
            alpha = alpha + jnp.einsum('ehc,hc->eh', tf, ae)
            alpha = jnp.where(alpha >= 0, alpha, NEG_SLOPE * alpha)
            m = jax.ops.segment_max(alpha, dst, num_segments=N)
            e = jnp.exp(alpha - m[dst])
            s = jax.ops.segment_sum(e, dst, num_segments=N)
            alpha = e / (s[dst] + 1e-16)
            msg = xs[src] * alpha[:, :, None]
            out = jax.ops.segment_sum(msg, dst, num_segments=N).reshape(N, D)
            out = out @ Wo + bo + b
            mu = out.mean(-1, keepdims=True)
            var = out.var(-1, keepdims=True)
            out = (out - mu) / jnp.sqrt(var + EPS_LN) * lg + lb
            return out + x

        def _bn_relu(x, g, bvec, relu=True):
            mu = x.mean(0)
            var = x.var(0)
            x = (x - mu) / jnp.sqrt(var + EPS_BN) * g + bvec
            return jnp.maximum(x, 0.0) if relu else x

        def _forward(x, edge_index, edge_attr, edge_types, Ws1, Wd1, as1, ad1, We1, ae1, te1, Wo1, bo1, b1, lg1, lb1, Ws2, Wd2, as2, ad2, We2, ae2, te2, Wo2, bo2, b2, lg2, lb2, bng1, bnb1, bng2, bnb2):
            N = x.shape[0]
            loops = jnp.arange(N, dtype=edge_index.dtype)
            src = jnp.concatenate([edge_index[0], loops])
            dst = jnp.concatenate([edge_index[1], loops])
            ea = jnp.concatenate([edge_attr, jnp.ones((N, edge_attr.shape[1]), edge_attr.dtype)])
            et = jnp.concatenate([edge_types, jnp.full((N,), SELF_LOOP_TYPE, edge_types.dtype)])
            residual = x
            out = _gat_layer(x, src, dst, ea, et, Ws1, Wd1, as1, ad1, We1, ae1, te1, Wo1, bo1, b1, lg1, lb1)
            out = _bn_relu(out, bng1, bnb1, relu=True)
            out = _gat_layer(out, src, dst, ea, et, Ws2, Wd2, as2, ad2, We2, ae2, te2, Wo2, bo2, b2, lg2, lb2)
            out = _bn_relu(out, bng2, bnb2, relu=False)
            return jnp.maximum(out + residual, 0.0)
        key = jax.random.key(seed)
        ks = jax.random.split(key, 32)
        N, E, EDIM, NTYPES = (2500, 40000, 16, 7)
        d = {}
        d['x'] = jax.random.normal(ks[0], (N, D), jnp.float32)
        d['edge_index'] = jax.random.randint(ks[1], (2, E), 0, N, jnp.int64)
        d['edge_attr'] = jax.random.normal(ks[2], (E, EDIM), jnp.float32)
        d['edge_types'] = jax.random.randint(ks[3], (E,), 0, NTYPES, jnp.int64)

        def glorot(k, shape):
            fan = shape[-2] + shape[-1] if len(shape) >= 2 else shape[-1] + 1
            return jax.random.uniform(k, shape, jnp.float32, -1.0, 1.0) * np.sqrt(6.0 / fan)
        i = 4
        for L in ('1', '2'):
            d['Ws' + L] = glorot(ks[i], (D, D))
            i += 1
            d['Wd' + L] = glorot(ks[i], (D, D))
            i += 1
            d['as' + L] = glorot(ks[i], (H, C))
            i += 1
            d['ad' + L] = glorot(ks[i], (H, C))
            i += 1
            d['We' + L] = glorot(ks[i], (EDIM, D))
            i += 1
            d['ae' + L] = glorot(ks[i], (H, C))
            i += 1
            d['te' + L] = glorot(ks[i], (NTYPES, D))
            i += 1
            d['Wo' + L] = glorot(ks[i], (D, D))
            i += 1
            d['bo' + L] = jnp.zeros((D,), jnp.float32)
            d['b' + L] = jnp.zeros((D,), jnp.float32)
            d['lg' + L] = jnp.ones((D,), jnp.float32)
            d['lb' + L] = jnp.zeros((D,), jnp.float32)
        d['bng1'] = jnp.ones((D,), jnp.float32)
        d['bnb1'] = jnp.zeros((D,), jnp.float32)
        d['bng2'] = jnp.ones((D,), jnp.float32)
        d['bnb2'] = jnp.zeros((D,), jnp.float32)
        return d
    _L0_gnn_all = _L0_gnn_setup()
    _L0_gnn_in = {k: v for k, v in _L0_gnn_all.items() if k in ('Ws1', 'Wd1', 'as1', 'ad1', 'We1', 'ae1', 'te1', 'Wo1', 'bo1', 'b1', 'lg1', 'lb1', 'Ws2', 'Wd2', 'as2', 'ad2', 'We2', 'ae2', 'te2', 'Wo2', 'bo2', 'b2', 'lg2', 'lb2', 'bng1', 'bnb1', 'bng2', 'bnb2')}
    del _L0_gnn_all

    def _L1_gnn_setup():
        import jax, jax.numpy as jnp
        import numpy as np
        PI = float(np.pi)
        CUTOFF = 5.0
        N_NODES = 6250
        N_EDGES = 100000
        HIDDEN = 256
        FILT = 64
        RADIAL = 12
        key = jax.random.key(seed)
        ks = jax.random.split(key, 10)
        x = jax.random.normal(ks[0], (N_NODES, HIDDEN), dtype=jnp.float32)
        rbf = jax.random.normal(ks[1], (N_EDGES, RADIAL), dtype=jnp.float32)
        dists = jax.random.uniform(ks[2], (N_EDGES,), dtype=jnp.float32)
        edge_index = jax.random.randint(ks[3], (2, N_EDGES), 0, N_NODES, dtype=jnp.int64)
        batch = jnp.zeros((N_NODES,), dtype=jnp.int64)
        s = 0.05
        W_node_to_message = jax.random.normal(ks[4], (FILT, HIDDEN), dtype=jnp.float32) * s
        W_radial_to_message = jax.random.normal(ks[5], (FILT, RADIAL), dtype=jnp.float32) * s
        W_lin1 = jax.random.normal(ks[6], (FILT, FILT), dtype=jnp.float32) * s
        W_lin2 = jax.random.normal(ks[7], (FILT, FILT), dtype=jnp.float32) * s
        b_lin2 = jax.random.normal(ks[8], (FILT,), dtype=jnp.float32) * s
        W_message_to_node = jax.random.normal(ks[9], (HIDDEN, FILT), dtype=jnp.float32) * s
        return {'x': x, 'rbf': rbf, 'dists': dists, 'edge_index': edge_index, 'batch': batch, 'W_node_to_message': W_node_to_message, 'W_radial_to_message': W_radial_to_message, 'W_lin1': W_lin1, 'W_lin2': W_lin2, 'b_lin2': b_lin2, 'W_message_to_node': W_message_to_node}
    _L1_gnn_all = _L1_gnn_setup()
    _L1_gnn_in = {k: v for k, v in _L1_gnn_all.items() if k in ('W_node_to_message', 'W_radial_to_message', 'W_lin1', 'W_lin2', 'b_lin2', 'W_message_to_node')}
    del _L1_gnn_all

    def _L2_gnn_setup():
        import jax, jax.numpy as jnp
        import numpy as np
        N = 6250
        E = 100000
        DIN = 256
        DOUT = 256
        R = 8
        key = jax.random.key(seed)
        k1, k2, k3, k4, k5, k6 = jax.random.split(key, 6)
        h = jax.random.normal(k1, (N, DIN), dtype=jnp.float32)
        weight = jax.random.normal(k2, (R, DIN, DOUT), dtype=jnp.float32) * (1.0 / np.sqrt(DIN))
        sl_w = jax.random.normal(k3, (DOUT, DIN), dtype=jnp.float32) * (1.0 / np.sqrt(DIN))
        sl_b = jax.random.normal(k4, (DOUT,), dtype=jnp.float32) * 0.01
        edge_index = jax.random.randint(k5, (2, E), 0, N, dtype=jnp.int32)
        edge_type = jax.random.randint(k6, (E,), 0, R, dtype=jnp.int32)
        return {'h': h, 'weight': weight, 'sl_w': sl_w, 'sl_b': sl_b, 'edge_index': edge_index, 'edge_type': edge_type, 'num_nodes': N}
    _L2_gnn_all = _L2_gnn_setup()
    _L2_gnn_in = {k: v for k, v in _L2_gnn_all.items() if k in ('weight', 'sl_w', 'sl_b')}
    del _L2_gnn_all

    def _L3_gnn_setup():
        import jax, jax.numpy as jnp
        import numpy as np
        N = 6250
        E = 100000
        F_IN = 256
        F_OUT = 256
        key = jax.random.key(seed)
        k1, k2, k3, k4, k5, k6 = jax.random.split(key, 6)
        x = jax.random.normal(k1, (N, F_IN), dtype=jnp.float32)
        edge_index = jax.random.randint(k2, (2, E), 0, N, dtype=jnp.int64)
        edge_values = jax.random.uniform(k3, (E,), dtype=jnp.float32)
        s_w = float(np.sqrt(6.0 / (F_IN + F_OUT)))
        s_a = float(np.sqrt(6.0 / (F_OUT + 1)))
        W = jax.random.uniform(k4, (F_IN, F_OUT), dtype=jnp.float32, minval=-s_w, maxval=s_w)
        a1 = jax.random.uniform(k5, (F_OUT, 1), dtype=jnp.float32, minval=-s_a, maxval=s_a)
        a2 = jax.random.uniform(k6, (F_OUT, 1), dtype=jnp.float32, minval=-s_a, maxval=s_a)
        return {'x': x, 'edge_index': edge_index, 'edge_values': edge_values, 'W': W, 'a1': a1, 'a2': a2}
    _L3_gnn_all = _L3_gnn_setup()
    _L3_gnn_in = {k: v for k, v in _L3_gnn_all.items() if k in ('W', 'a1', 'a2')}
    del _L3_gnn_all
    return {'x': x, 'src': src, 'dst': dst, 'edge_attr_12': edge_attr_12, 'edge_attr_16': edge_attr_16, 'edge_type_7': edge_type_7, 'edge_type_8': edge_type_8, 'edge_weight': edge_weight, 'L0_gnn_Ws1': _L0_gnn_in['Ws1'], 'L0_gnn_Wd1': _L0_gnn_in['Wd1'], 'L0_gnn_as1': _L0_gnn_in['as1'], 'L0_gnn_ad1': _L0_gnn_in['ad1'], 'L0_gnn_We1': _L0_gnn_in['We1'], 'L0_gnn_ae1': _L0_gnn_in['ae1'], 'L0_gnn_te1': _L0_gnn_in['te1'], 'L0_gnn_Wo1': _L0_gnn_in['Wo1'], 'L0_gnn_bo1': _L0_gnn_in['bo1'], 'L0_gnn_b1': _L0_gnn_in['b1'], 'L0_gnn_lg1': _L0_gnn_in['lg1'], 'L0_gnn_lb1': _L0_gnn_in['lb1'], 'L0_gnn_Ws2': _L0_gnn_in['Ws2'], 'L0_gnn_Wd2': _L0_gnn_in['Wd2'], 'L0_gnn_as2': _L0_gnn_in['as2'], 'L0_gnn_ad2': _L0_gnn_in['ad2'], 'L0_gnn_We2': _L0_gnn_in['We2'], 'L0_gnn_ae2': _L0_gnn_in['ae2'], 'L0_gnn_te2': _L0_gnn_in['te2'], 'L0_gnn_Wo2': _L0_gnn_in['Wo2'], 'L0_gnn_bo2': _L0_gnn_in['bo2'], 'L0_gnn_b2': _L0_gnn_in['b2'], 'L0_gnn_lg2': _L0_gnn_in['lg2'], 'L0_gnn_lb2': _L0_gnn_in['lb2'], 'L0_gnn_bng1': _L0_gnn_in['bng1'], 'L0_gnn_bnb1': _L0_gnn_in['bnb1'], 'L0_gnn_bng2': _L0_gnn_in['bng2'], 'L0_gnn_bnb2': _L0_gnn_in['bnb2'], 'L1_gnn_W_node_to_message': _L1_gnn_in['W_node_to_message'], 'L1_gnn_W_radial_to_message': _L1_gnn_in['W_radial_to_message'], 'L1_gnn_W_lin1': _L1_gnn_in['W_lin1'], 'L1_gnn_W_lin2': _L1_gnn_in['W_lin2'], 'L1_gnn_b_lin2': _L1_gnn_in['b_lin2'], 'L1_gnn_W_message_to_node': _L1_gnn_in['W_message_to_node'], 'L2_gnn_weight': _L2_gnn_in['weight'], 'L2_gnn_sl_w': _L2_gnn_in['sl_w'], 'L2_gnn_sl_b': _L2_gnn_in['sl_b'], 'L3_gnn_W': _L3_gnn_in['W'], 'L3_gnn_a1': _L3_gnn_in['a1'], 'L3_gnn_a2': _L3_gnn_in['a2']}

def reference(x, src, dst, edge_attr_12, edge_attr_16, edge_type_7, edge_type_8, edge_weight, L0_gnn_Ws1, L0_gnn_Wd1, L0_gnn_as1, L0_gnn_ad1, L0_gnn_We1, L0_gnn_ae1, L0_gnn_te1, L0_gnn_Wo1, L0_gnn_bo1, L0_gnn_b1, L0_gnn_lg1, L0_gnn_lb1, L0_gnn_Ws2, L0_gnn_Wd2, L0_gnn_as2, L0_gnn_ad2, L0_gnn_We2, L0_gnn_ae2, L0_gnn_te2, L0_gnn_Wo2, L0_gnn_bo2, L0_gnn_b2, L0_gnn_lg2, L0_gnn_lb2, L0_gnn_bng1, L0_gnn_bnb1, L0_gnn_bng2, L0_gnn_bnb2, L1_gnn_W_node_to_message, L1_gnn_W_radial_to_message, L1_gnn_W_lin1, L1_gnn_W_lin2, L1_gnn_b_lin2, L1_gnn_W_message_to_node, L2_gnn_weight, L2_gnn_sl_w, L2_gnn_sl_b, L3_gnn_W, L3_gnn_a1, L3_gnn_a2):
    import jax
    import jax.numpy as jnp

    def _L0_gnn_ref(x, edge_index, edge_attr, edge_types, Ws1, Wd1, as1, ad1, We1, ae1, te1, Wo1, bo1, b1, lg1, lb1, Ws2, Wd2, as2, ad2, We2, ae2, te2, Wo2, bo2, b2, lg2, lb2, bng1, bnb1, bng2, bnb2):
        import jax, jax.numpy as jnp
        import numpy as np
        H, C = (8, 32)
        D = H * C
        NEG_SLOPE = 0.2
        SELF_LOOP_TYPE = 6
        EPS_LN = 1e-05
        EPS_BN = 1e-05

        def _gat_layer(x, src, dst, ea, et, Ws, Wd, a_s, a_d, We, ae, te, Wo, bo, b, lg, lb):
            N = x.shape[0]
            xs = (x @ Ws).reshape(N, H, C)
            xd = (x @ Wd).reshape(N, H, C)
            a_i = jnp.einsum('nhc,hc->nh', xd, a_s)
            a_j = jnp.einsum('nhc,hc->nh', xs, a_d)
            alpha = a_i[dst] + a_j[src]
            ef = (ea @ We).reshape(-1, H, C)
            alpha = alpha + jnp.einsum('ehc,hc->eh', ef, ae)
            tf = te[et].reshape(-1, H, C)
            alpha = alpha + jnp.einsum('ehc,hc->eh', tf, ae)
            alpha = jnp.where(alpha >= 0, alpha, NEG_SLOPE * alpha)
            m = jax.ops.segment_max(alpha, dst, num_segments=N)
            e = jnp.exp(alpha - m[dst])
            s = jax.ops.segment_sum(e, dst, num_segments=N)
            alpha = e / (s[dst] + 1e-16)
            msg = xs[src] * alpha[:, :, None]
            out = jax.ops.segment_sum(msg, dst, num_segments=N).reshape(N, D)
            out = out @ Wo + bo + b
            mu = out.mean(-1, keepdims=True)
            var = out.var(-1, keepdims=True)
            out = (out - mu) / jnp.sqrt(var + EPS_LN) * lg + lb
            return out + x

        def _bn_relu(x, g, bvec, relu=True):
            mu = x.mean(0)
            var = x.var(0)
            x = (x - mu) / jnp.sqrt(var + EPS_BN) * g + bvec
            return jnp.maximum(x, 0.0) if relu else x

        def _forward(x, edge_index, edge_attr, edge_types, Ws1, Wd1, as1, ad1, We1, ae1, te1, Wo1, bo1, b1, lg1, lb1, Ws2, Wd2, as2, ad2, We2, ae2, te2, Wo2, bo2, b2, lg2, lb2, bng1, bnb1, bng2, bnb2):
            N = x.shape[0]
            loops = jnp.arange(N, dtype=edge_index.dtype)
            src = jnp.concatenate([edge_index[0], loops])
            dst = jnp.concatenate([edge_index[1], loops])
            ea = jnp.concatenate([edge_attr, jnp.ones((N, edge_attr.shape[1]), edge_attr.dtype)])
            et = jnp.concatenate([edge_types, jnp.full((N,), SELF_LOOP_TYPE, edge_types.dtype)])
            residual = x
            out = _gat_layer(x, src, dst, ea, et, Ws1, Wd1, as1, ad1, We1, ae1, te1, Wo1, bo1, b1, lg1, lb1)
            out = _bn_relu(out, bng1, bnb1, relu=True)
            out = _gat_layer(out, src, dst, ea, et, Ws2, Wd2, as2, ad2, We2, ae2, te2, Wo2, bo2, b2, lg2, lb2)
            out = _bn_relu(out, bng2, bnb2, relu=False)
            return jnp.maximum(out + residual, 0.0)
        return _forward(x, edge_index, edge_attr, edge_types, Ws1, Wd1, as1, ad1, We1, ae1, te1, Wo1, bo1, b1, lg1, lb1, Ws2, Wd2, as2, ad2, We2, ae2, te2, Wo2, bo2, b2, lg2, lb2, bng1, bnb1, bng2, bnb2)

    def _L1_gnn_ref(x, rbf, dists, edge_index, batch, W_node_to_message, W_radial_to_message, W_lin1, W_lin2, b_lin2, W_message_to_node):
        import jax, jax.numpy as jnp
        import numpy as np
        PI = float(np.pi)
        CUTOFF = 5.0
        N_NODES = 6250
        N_EDGES = 100000
        HIDDEN = 256
        FILT = 64
        RADIAL = 12
        h = x @ W_node_to_message.T
        edge_attr = rbf @ W_radial_to_message.T
        C = 0.5 * (jnp.cos(dists * (PI / CUTOFF)) + 1.0)
        W = edge_attr * C[:, None]
        h = h @ W_lin1.T
        src, dst = (edge_index[0], edge_index[1])
        m = h[src] * W
        agg = jax.ops.segment_sum(m, dst, num_segments=h.shape[0])
        h = agg @ W_lin2.T + b_lin2
        out = h @ W_message_to_node.T
        return out

    def _L2_gnn_ref(h, weight, sl_w, sl_b, edge_index, edge_type, num_nodes):
        import jax, jax.numpy as jnp
        import numpy as np
        N = 6250
        E = 100000
        DIN = 256
        DOUT = 256
        R = 8
        src, dst = (edge_index[0], edge_index[1])
        hW = jnp.einsum('nd,rde->rne', h, weight)
        msg = hW[edge_type, src]
        m = jax.ops.segment_sum(msg, dst, num_segments=num_nodes)
        deg = jax.ops.segment_sum(jnp.ones_like(dst, dtype=h.dtype), dst, num_segments=num_nodes)
        deg = jnp.maximum(deg, 1.0)[:, None]
        return h @ sl_w.T + sl_b + m / deg

    def _L3_gnn_ref(x, edge_index, edge_values, W, a1, a2):
        import jax, jax.numpy as jnp
        import numpy as np
        N = 6250
        E = 100000
        F_IN = 256
        F_OUT = 256
        n = x.shape[0]
        row, col = (edge_index[0], edge_index[1])
        support = x @ W
        r_D = jax.nn.sigmoid(support @ a2)
        gated = r_D * support
        msg = gated[col] * edge_values[:, None]
        out = jax.ops.segment_sum(msg, row, num_segments=n)
        sumnorm = jax.ops.segment_sum(edge_values * r_D[col, 0], row, num_segments=n)
        out = out / sumnorm[:, None]
        l_D = jax.nn.softplus(out @ a1)
        out = jnp.maximum(out, 0.0) + l_D * jnp.minimum(out, 0.0)
        out = jax.nn.elu(out)
        return out
    edge_index = jnp.stack([src, dst])
    batch0 = jnp.zeros((6250,), jnp.int32)
    x = _layernorm(x + _L0_gnn_ref(x, edge_index, edge_attr_16, edge_type_7, L0_gnn_Ws1, L0_gnn_Wd1, L0_gnn_as1, L0_gnn_ad1, L0_gnn_We1, L0_gnn_ae1, L0_gnn_te1, L0_gnn_Wo1, L0_gnn_bo1, L0_gnn_b1, L0_gnn_lg1, L0_gnn_lb1, L0_gnn_Ws2, L0_gnn_Wd2, L0_gnn_as2, L0_gnn_ad2, L0_gnn_We2, L0_gnn_ae2, L0_gnn_te2, L0_gnn_Wo2, L0_gnn_bo2, L0_gnn_b2, L0_gnn_lg2, L0_gnn_lb2, L0_gnn_bng1, L0_gnn_bnb1, L0_gnn_bng2, L0_gnn_bnb2), axis=-1)
    x = _layernorm(x + _L1_gnn_ref(x, edge_attr_12, edge_weight, edge_index, batch0, L1_gnn_W_node_to_message, L1_gnn_W_radial_to_message, L1_gnn_W_lin1, L1_gnn_W_lin2, L1_gnn_b_lin2, L1_gnn_W_message_to_node), axis=-1)
    x = _layernorm(x + _L2_gnn_ref(x, L2_gnn_weight, L2_gnn_sl_w, L2_gnn_sl_b, edge_index, edge_type_8, 6250), axis=-1)
    x = _layernorm(x + _L3_gnn_ref(x, edge_index, edge_weight, L3_gnn_W, L3_gnn_a1, L3_gnn_a2), axis=-1)
    return x

_drawn_inputs = setup_inputs


def setup_inputs(seed=0):
    import zlib

    import numpy as np

    out = dict(_drawn_inputs(seed))
    spreads = {'L0_gnn_bo1': (0.0, 0.421),
     'L0_gnn_b1': (0.0, 0.426),
     'L0_gnn_lg1': (1.0, 0.2),
     'L0_gnn_lb1': (0.0, 2.0),
     'L0_gnn_bo2': (0.0, 2.0),
     'L0_gnn_b2': (0.0, 2.0),
     'L0_gnn_lg2': (1.0, 0.6),
     'L0_gnn_lb2': (0.0, 2.0),
     'L0_gnn_bng1': (1.0, 0.6),
     'L0_gnn_bnb1': (0.0, 0.316),
     'L0_gnn_bng2': (1.0, 0.2),
     'L0_gnn_bnb2': (0.0, 0.1)}
    factors = {'L0_gnn_te1': 2.69,
     'L0_gnn_te2': 13.555,
     'L2_gnn_sl_b': 7.263,
     'L0_gnn_Wd2': 3.757,
     'L0_gnn_as2': 11.307,
     'L0_gnn_We2': 3.105}
    for name, (base, spread) in spreads.items():
        noise = np.random.default_rng([zlib.crc32(name.encode()), seed]).standard_normal(out[name].shape)
        drawn = base * np.exp(spread * noise) if base else spread * noise
        out[name] = jnp.asarray(drawn.astype(out[name].dtype))
    for name, factor in factors.items():
        out[name] = (out[name] * factor).astype(out[name].dtype)
    return out
```

```python
from contextlib import ExitStack

import numpy as np
import concourse.bass as bass
from concourse import mybir

F32 = mybir.dt.float32
I32 = mybir.dt.int32
ALU = mybir.AluOpType
ACT = mybir.ActivationFunctionType
AX_X = mybir.AxisListType.X

P = 128
N_NODES = 6250
N_EDGES = 100000
D = 256
H = 8
C = D // H
N_TYPES = 7
SELF_TYPE = 6
N_REL = 8
EDIM = 16
RADIAL = 12
FILT = 64
NEG_SLOPE = 0.2
EPS = 1e-5
BIG = 1e30
CUTOFF = 5.0

NPT = P - 1
NT = -(-N_NODES // NPT)
NR = NT * P
LAST_ROWS = N_NODES - (NT - 1) * NPT + 1
assert NT % 2 == 0

TE = -(-N_EDGES // P)
TCH = 7
TCP = 112
TP = TCH * TCP
assert TP >= TE + 1
GROUP = 8
SETS = 4
BODY = GROUP * SETS
S = -(-(TE + NT - 1) // BODY) * BODY
NG = S // GROUP
SH = S // 2
SCH = -(-S // P)
assert SH <= 512
PAD_DST = NT * NPT - 1

AGG = D + 2 * H + 1
XW = AGG + 1
TABW = D + H

CT = 5
NCK = NT // CT
assert NT % CT == 0 and NCK % 2 == 0
NORM_STEPS = 2 * CT + 1
K_ACC = 4
assert GROUP % K_ACC == 0


class Mem:
    pass


class Chain:

    def __init__(self, eng, sem, per=0):
        self.eng, self.sem, self.per = eng, sem, per
        self.base, self.k = 0, 0

    def turn(self, n):
        self.base, self.k = n * self.per, 0

    def do(self, ins):
        ins.then_inc(self.sem, 1)
        self.k += 1

    def wait(self):
        self.eng.wait_ge(self.sem, self.base + self.k)

    def link(self, ins):
        self.do(ins)
        self.wait()

    def close(self):
        assert self.k == self.per, (self.k, self.per)


def buf_maker(nc, ctx, prefix):
    def sb(name, shape, dt=F32):
        return ctx.enter_context(nc.sbuf_tensor(f"{prefix}_{name}", shape, dt))

    def ps(name, shape):
        return ctx.enter_context(nc.psum_tensor(f"{prefix}_{name}", shape, F32))
    return sb, ps


def phase_constants(nc, m, sem):
    ready = sem("iota_ready")
    step = sem("const_step")
    with nc.Block() as block:
        @block.gpsimd
        def _(pool):
            nc.gpsimd.iota(m.iota_i[:], pattern=[[1, S]], base=0, channel_multiplier=0).then_inc(ready, 1)
            nc.gpsimd.iota(m.pidx_i[:], pattern=[[1, 1]], base=0, channel_multiplier=1).then_inc(ready, 1)

        @block.vector
        def _(dve):
            ch = Chain(dve, step)
            dve.wait_ge(ready, 2)
            ch.do(nc.vector.tensor_copy(m.iota[:], m.iota_i[:]))
            ch.do(nc.vector.tensor_copy(m.pidx[:], m.pidx_i[:]))
            ch.do(nc.vector.memset(m.ones[:], 1.0))
            ch.do(nc.vector.memset(m.minus_one[:], -1.0))
            ch.link(nc.vector.memset(m.zeros[:], 0.0))
            ch.do(nc.vector.tensor_scalar(m.ident[:], m.iota[:, 0:P], m.pidx[:, 0:1], None, ALU.is_equal))
            ch.do(nc.vector.tensor_scalar(m.mask[:, 0:1], m.pidx[:], 0.0, None, ALU.is_gt))
            ch.do(nc.vector.tensor_scalar(m.is_p0[:], m.pidx[:], 0.0, None, ALU.is_equal))
            ch.link(nc.vector.tensor_scalar(m.mask[:, 1:2], m.pidx[:], float(LAST_ROWS), None, ALU.is_lt))
            ch.link(nc.vector.tensor_tensor(m.mask[:, 1:2], m.mask[:, 1:2], m.mask[:, 0:1], ALU.mult))
            ch.do(nc.vector.tensor_scalar(m.node_mask[:, 0, :], m.ones[:], m.mask[:, 0:1], None, ALU.mult))
            ch.link(nc.vector.tensor_scalar(m.node_mask[:, 1, :], m.ones[:], m.mask[:, 1:2], None, ALU.mult))


def phase_index(nc, m, d, sem):
    loaded = sem("edges_loaded")
    tiles_ready = sem("edge_rows_ready")
    step = sem("index_step")
    moved = sem("slot_moved")
    taken = sem("slot_taken")
    qrow_ready = sem("carried_row_ready")
    qb_ready = sem("carried_spread")
    n_ready = sem("node_tile_ready")
    stored = sem("carried_stored")
    with ExitStack() as ctx:
        sb, ps = buf_maker(nc, ctx, "ix")
        raw = {n: sb(f"{n}_raw", [TCP, TCH, P], I32) for n in ("dst", "dprev", "src", "rel")}
        dnext_raw = sb("dnext_raw", [TCP, TCH], I32)
        rows = sb("rows", [TCP, 6, TCH, P])
        wide = sb("wide", [TCP, 3, TCH * P])
        wide_i = sb("wide_i", [TCP, TCH * P], I32)
        q = sb("q", [TCP, TCH, P])
        qn = sb("qn", [TCP, TCH])
        small = sb("small", [TCP, 4, TCH])
        small_i = sb("small_i", [TCP, TCH], I32)
        tcol = sb("tcol", [TCP, TCH])
        sel = m.sel
        slot = sb("slot", [P, 6, S])
        qrow = sb("qrow", [1, 3, S])
        tmp = sb("tmp", [P, S])
        psum = [ps(f"ps{b}", [P, 2, 512]) for b in range(2)]

        with nc.Block() as block:
            @block.sync
            def _(sp):
                flat = d.dst_ext.rearrange("t p -> (t p)")
                for name, at in (("dst", P), ("dprev", P - 1)):
                    sp.dma_start(raw[name][:], flat[at:at + TP * P].rearrange("(c t p) -> t c p", c=TCH, p=P)).then_inc(loaded, 16)
                sp.dma_start(raw["src"][:], d.src.rearrange("(c t) p -> t c p", c=TCH)).then_inc(loaded, 16)
                sp.dma_start(raw["rel"][:], d.type8.rearrange("(c t) p -> t c p", c=TCH)).then_inc(loaded, 16)
                sp.dma_start(rows[:, 3, :, :], d.weight.rearrange("(c t) p -> t c p", c=TCH)).then_inc(loaded, 16)
                with nc.allow_non_contiguous_dma(reason="one word per edge tile"):
                    sp.dma_start(dnext_raw[:], d.dst_ext[2:2 + TP, 0:1].rearrange("(c t) p -> t (c p)", c=TCH)).then_inc(loaded, 16)

            @block.vector
            def _(dve):
                ch = Chain(dve, step)

                def floor_npt(out, x, t0, t1, ti):
                    ch.link(nc.vector.tensor_scalar(t0, x, float(NPT // 2), 1.0 / NPT, ALU.subtract, ALU.mult))
                    ch.link(nc.vector.tensor_copy(ti, t0))
                    ch.link(nc.vector.tensor_copy(out, ti))
                    ch.link(nc.vector.scalar_tensor_tensor(out=t0, in0=out, scalar=-float(NPT), in1=x, op0=ALU.mult, op1=ALU.add))
                    ch.do(nc.vector.tensor_scalar(t1, t0, float(NPT), None, ALU.is_ge))
                    ch.link(nc.vector.tensor_scalar(t0, t0, 0.0, None, ALU.is_lt))
                    ch.link(nc.vector.tensor_tensor(t1, t1, t0, ALU.subtract))
                    ch.link(nc.vector.tensor_tensor(out, out, t1, ALU.add))

                def flat(a):
                    return a.rearrange("t c p -> t (c p)")
                for v, pad in ((m.src_slot, 0), (m.rel_slot, 0), (m.w_slot, 0.0), (m.trow, 0), (m.nrow, 0), (m.first, 0.0), (m.loc, -1.0), (m.loc_m, -1.0)):
                    ch.do(nc.vector.memset(v[:, S:S + GROUP], pad))
                dve.wait_ge(loaded, 6 * 16)
                t0, t1, x = wide[:, 0, :], wide[:, 1, :], wide[:, 2, :]
                for name, to in (("src", 1), ("dst", 0)):
                    ch.link(nc.vector.tensor_copy(x, flat(raw[name][:])))
                    floor_npt(flat(q[:]), x, t0, t1, wide_i[:])
                    ch.link(nc.vector.scalar_tensor_tensor(out=flat(rows[:, to, :, :]), in0=x, scalar=1.0, in1=flat(q[:]), op0=ALU.add, op1=ALU.add))
                ch.link(nc.vector.tensor_copy(t0, flat(raw["rel"][:])))
                ch.link(nc.vector.scalar_tensor_tensor(out=flat(rows[:, 2, :, :]), in0=t0, scalar=float(NR), in1=flat(rows[:, 1, :, :]), op0=ALU.mult, op1=ALU.add))
                ch.link(nc.vector.tensor_copy(t0, flat(raw["dprev"][:])))
                ch.link(nc.vector.tensor_tensor(flat(rows[:, 4, :, :]), x, t0, ALU.not_equal))
                ch.link(nc.vector.tensor_copy(small[:, 2, :], dnext_raw[:]))
                floor_npt(qn[:], small[:, 2, :], small[:, 0, :], small[:, 1, :], small_i[:])
                for c in range(TCH):
                    ch.do(nc.vector.tensor_scalar(tcol[:, c:c + 1], m.pidx[0:TCP, :], float(c * TCP), None, ALU.add))
                ch.wait()
                ch.link(nc.vector.tensor_tensor(small[:, 0, :], qn[:], tcol[:], ALU.add))
                ch.link(nc.vector.scalar_tensor_tensor(out=small[:, 1, :], in0=tcol[:], scalar=-1.0, in1=q[:, :, 0], op0=ALU.add, op1=ALU.add))
                ch.link(nc.vector.memset(small[0:1, 1, 0:1], -1.0))
                for c in range(TCH):
                    ch.do(nc.vector.tensor_scalar(rows[:, 5, c, :], m.ones[0:TCP, :], tcol[:, c:c + 1], None, ALU.mult))
                    ch.do(nc.vector.tensor_scalar(sel[:, c, :], m.iota[0:TCP, :], small[:, 0, c:c + 1], None, ALU.is_le))
                ch.wait()
                for c in range(TCH):
                    ins = nc.vector.scalar_tensor_tensor(out=sel[:, c, :], in0=m.iota[0:TCP, :], scalar=small[:, 1, c:c + 1], in1=sel[:, c, :], op0=ALU.is_gt, op1=ALU.mult)
                ins.then_inc(tiles_ready, 1)
                for a in range(6):
                    dve.wait_ge(moved, a + 1)
                    nc.vector.tensor_copy(slot[:, a, :].rearrange("p (h s) -> p h s", h=2), psum[a % 2][:, :, 0:SH]).then_inc(taken, 1)
                dve.wait_ge(taken, 6)
                ch.do(nc.vector.tensor_copy(m.src_slot[:, 0:S], slot[:, 1, :]))
                ch.do(nc.vector.tensor_copy(m.rel_slot[:, 0:S], slot[:, 2, :]))
                ch.do(nc.vector.tensor_copy(m.w_slot[:, 0:S], slot[:, 3, :]))
                ch.do(nc.vector.tensor_copy(m.trow[:, 0:S], slot[0:1, 5, :]))
                ch.do(nc.vector.tensor_scalar(m.first[:, 0:S], slot[:, 4, :], m.is_p0[:, 0:1], None, ALU.max))
                ch.link(nc.vector.tensor_tensor(tmp[:], m.iota[:], slot[:, 5, :], ALU.subtract))
                ch.do(nc.vector.tensor_copy(m.nrow[:, 0:S], tmp[0:1, :]))
                ch.link(nc.vector.scalar_tensor_tensor(out=m.loc[:, 0:S], in0=tmp[:], scalar=-float(P), in1=slot[:, 0, :], op0=ALU.mult, op1=ALU.add))
                ch.link(nc.vector.tensor_scalar(qrow[:, 0, :], m.loc[0:1, 0:S], 1.0, None, ALU.is_ge))
                ch.link(nc.vector.tensor_scalar(qrow[:, 1, :], m.loc[0:1, 0:S], float(P), None, ALU.is_lt))
                ch.link(nc.vector.tensor_tensor(qrow[:, 0, :], qrow[:, 0, :], qrow[:, 1, :], ALU.mult))
                ch.link(nc.vector.tensor_scalar(qrow[:, 1, :], slot[0:1, 4, :], 0.0, None, ALU.is_equal))
                ch.link(nc.vector.tensor_tensor(qrow[:, 0, :], qrow[:, 0, :], qrow[:, 1, :], ALU.mult))
                ch.link(nc.vector.scalar_tensor_tensor(out=qrow[:, 1, :], in0=slot[0:1, 0, :], scalar=1.0, in1=qrow[:, 0, :], op0=ALU.add, op1=ALU.mult))
                ch.link(nc.vector.scalar_tensor_tensor(out=qrow[:, 2, :], in0=m.loc[0:1, 0:S], scalar=0.5, in1=qrow[:, 0, :], op0=ALU.add, op1=ALU.mult))
                ch.do(nc.vector.tensor_scalar(qrow[:, 1, :], qrow[:, 1, :], 1.0, None, ALU.subtract))
                ch.do(nc.vector.tensor_scalar(qrow[:, 2, :], qrow[:, 2, :], 0.5, None, ALU.subtract))
                ch.wait()
                nc.vector.memset(tmp[0:1, 0:1], 0.0).then_inc(qrow_ready, 1)
                dve.wait_ge(qb_ready, 2)
                psq = psum[1][:, :, 0:SH]
                ch.link(nc.vector.tensor_tensor(tmp[:].rearrange("p (h s) -> p h s", h=2), m.loc[:, 0:S].rearrange("p (h s) -> p h s", h=2), psq, ALU.is_equal))
                ch.do(nc.vector.tensor_copy(m.carry_b[:].rearrange("p (h s) -> p h s", h=2), psum[0][0:H, :, 0:SH]))
                ch.link(nc.vector.tensor_tensor(tmp[:], tmp[:], m.loc[:, 0:S], ALU.mult))
                ch.link(nc.vector.tensor_tensor(m.loc_m[:, 0:S], m.loc[:, 0:S], tmp[:], ALU.subtract))

            @block.tensor
            def _(pe):
                pe.wait_ge(tiles_ready, 1)
                for a in range(6):
                    if a >= 2:
                        pe.wait_ge(taken, a - 1)
                    for h in range(2):
                        for c in range(TCH):
                            ins = nc.tensor.matmul(psum[a % 2][:, h, 0:SH], rows[:, a, c, :], sel[:, c, h * SH:(h + 1) * SH], start=(c == 0), stop=(c == TCH - 1))
                    ins.then_inc(moved, 1)
                pe.wait_ge(qrow_ready, 1)
                for a in range(2):
                    for h in range(2):
                        ins = nc.tensor.matmul(psum[a][:, h, 0:SH], m.ones[0:1, :], qrow[:, 1 + a, h * SH:(h + 1) * SH], start=True, stop=True)
                    ins.then_inc(qb_ready, 1)

            @block.scalar
            def _(act):
                act.wait_ge(qrow_ready, 1)
                act.dma_start(d.carry_rows[:, 0:S], qrow[:, 1, :]).then_inc(stored, 16)
                act.dma_start(d.carry_rows[:, S:SCH * P], m.minus_one[0:1, 0:SCH * P - S]).then_inc(stored, 16)
                act.wait_ge(stored, 32)
                with nc.allow_non_contiguous_dma(reason="832 words, once"):
                    act.dma_start(m.carry_col[:], d.carry_rows.rearrange("o (c p) -> p (o c)", p=P)).then_inc(stored, 16)
                act.wait_ge(stored, 48)


def phase_edge_weights(nc, m, d, w, sem):
    loaded = sem("weights_loaded")
    zeroed = sem("zeroed")
    step = sem("ew_step")
    folded = sem("folded")
    self_ready = sem("self_ready")
    with ExitStack() as ctx:
        sb, ps = buf_maker(nc, ctx, "ew")
        wt = sb("wt", [39, 2, D])
        ae = sb("ae", [39, 2, D])
        pick = sb("pick", [39, P])
        pk = sb("pk", [39, 3])
        psum = ps("self", [P, 2 * H])
        with nc.Block() as block:
            @block.sync
            def _(sp):
                sp.wait_ge(zeroed, 1)
                for l in range(2):
                    sp.dma_start(wt[0:EDIM, l, :], w[f"We{l + 1}"]).then_inc(loaded, 16)
                    sp.dma_start(wt[32:39, l, :], w[f"te{l + 1}"]).then_inc(loaded, 16)
                    sp.dma_start(ae[:, l, :], w[f"ae{l + 1}"].rearrange("h (o c) -> o (h c)", o=1).to_broadcast([39, D])).then_inc(loaded, 16)

            @block.vector
            def _(dve):
                ch = Chain(dve, step)
                nc.vector.memset(wt[:], 0.0).then_inc(zeroed, 1)
                dve.wait_ge(zeroed, 1)
                dve.wait_ge(loaded, 6 * 16)
                ch.link(nc.vector.tensor_tensor(wt[:], wt[:], ae[:], ALU.mult))
                ch.do(nc.vector.tensor_reduce(m.fold[:], wt[:].rearrange("p l (h c) -> p (l h) c", c=C), AX_X, ALU.add))
                ch.do(nc.vector.tensor_scalar(pk[:, 0:1], m.pidx[0:39, :], float(EDIM), None, ALU.is_lt))
                ch.link(nc.vector.tensor_scalar(pk[:, 1:2], m.pidx[0:39, :], float(32 + SELF_TYPE), None, ALU.is_equal))
                ch.link(nc.vector.tensor_tensor(pk[:, 2:3], pk[:, 0:1], pk[:, 1:2], ALU.add))
                ch.link(nc.vector.tensor_scalar(pick[:], m.ones[0:39, :], pk[:, 2:3], None, ALU.mult))
                nc.vector.tensor_scalar(m.type_row[:], m.pidx[:], 32.0, None, ALU.subtract).then_inc(folded, 1)
                dve.wait_ge(self_ready, 1)
                ch.link(nc.vector.tensor_copy(m.self_term[:], psum[:]))

            @block.tensor
            def _(pe):
                pe.wait_ge(folded, 1)
                nc.tensor.matmul(psum[:], pick[:], m.fold[:], start=True, stop=True).then_inc(self_ready, 1)


def phase_edge_terms(nc, m, d, sem):
    CH = 8
    NCH = TP // CH
    in_ready = [sem(f"attr_loaded{b}") for b in range(2)]
    hot_ready = sem("type_onehot_ready")
    used = sem("attr_used")
    mm_ready = sem("terms_ready")
    copied = sem("terms_copied")
    stored = [sem(f"terms_stored{b}") for b in range(2)]
    with ExitStack() as ctx:
        sb, ps = buf_maker(nc, ctx, "et")
        attr = [sb(f"attr{b}", [39, CH * P]) for b in range(2)]
        ty = [sb(f"ty{b}", [39, CH * P], I32) for b in range(2)]
        out = [sb(f"out{b}", [P, CH, 2 * H]) for b in range(2)]
        psum = [ps(f"ps{b}", [P, CH, 2 * H]) for b in range(2)]
        zeroed = sem("attr_zeroed")
        with nc.Block() as block:
            @block.sync
            def _(sp):
                sp.wait_ge(zeroed, 2)
                with sp.Fori(0, NCH // 2) as it:
                    for b in range(2):
                        n = it * 2 + b
                        sp.wait_ge(used, n + 1)
                        sp.dma_start(attr[b][0:EDIM, :], d.attr16_T[:, bass.ds(n * (CH * P), CH * P)]).then_inc(in_ready[b], 16)
                        sp.dma_start(ty[b][32:39, :], d.type7[0:1, bass.ds(n * (CH * P), CH * P)].to_broadcast([N_TYPES, CH * P])).then_inc(in_ready[b], 16)

            @block.vector
            def _(dve):
                for b in range(2):
                    nc.vector.memset(attr[b][:], 0.0).then_inc(zeroed, 1)
                with dve.Fori(0, NCH // 2) as it:
                    for b in range(2):
                        dve.wait_ge(in_ready[b], it * 32 + 32)
                        nc.vector.tensor_scalar(attr[b][32:39, :], ty[b][32:39, :], m.type_row[32:39, 0:1], None, ALU.is_equal).then_inc(hot_ready, 1)

            @block.tensor
            def _(pe):
                pe.sem_inc(used, 2)
                with pe.Fori(0, NCH // 2) as it:
                    for b in range(2):
                        n = it * 2 + b
                        pe.wait_ge(hot_ready, n + 1)
                        pe.wait_ge(copied, n + 1)
                        for j in range(CH):
                            ins = nc.tensor.matmul(psum[b][:, j, :], attr[b][:, j * P:(j + 1) * P], m.fold[:], start=True, stop=True)
                        ins.then_inc(mm_ready, 1)
                        pe.wait_ge(mm_ready, n + 1)
                        pe.sem_inc(used, 1)

            @block.scalar
            def _(act):
                act.sem_inc(copied, 2)
                for b in range(2):
                    act.sem_inc(stored[b], 16)
                with act.Fori(0, NCH // 2) as it:
                    for b in range(2):
                        n = it * 2 + b
                        act.wait_ge(mm_ready, n + 1)
                        act.wait_ge(stored[b], it * 16 + 16)
                        nc.scalar.copy(out[b][:], psum[b][:]).then_inc(copied, 1)
                        act.wait_ge(copied, n + 3)
                        act.dma_start(d.edge_terms[bass.ds(n * CH, CH), :, :].rearrange("t p k -> p t k"), out[b][:]).then_inc(stored[b], 16)
                for b in range(2):
                    act.wait_ge(stored[b], 16 * (NCH // 2 + 1))


def phase_slot_terms(nc, m, d, sem):
    loaded = sem("terms_loaded")
    moved = sem("terms_moved")
    taken = sem("terms_taken")
    stored = sem("layer_stored")
    zeroed = sem("pad_zeroed")
    with ExitStack() as ctx:
        sb, ps = buf_maker(nc, ctx, "st")
        terms = sb("terms", [TCP, TCH, P, 2 * H])
        slot_terms = sb("slot_terms", [P, H, S + GROUP])
        psum = [ps(f"ps{b}", [P, 2, 512]) for b in range(2)]
        with nc.Block() as block:
            @block.sync
            def _(sp):
                sp.dma_start(terms[:], d.edge_terms.rearrange("(c t) p k -> t c p k", c=TCH)).then_inc(loaded, 16)
                for l in range(2):
                    sp.wait_ge(taken, H * (l + 1))
                    sp.dma_start(d.terms[l], slot_terms[:]).then_inc(stored, 16)
                    sp.wait_ge(stored, 16 * (l + 1))

            @block.tensor
            def _(pe):
                pe.wait_ge(loaded, 16)
                for a in range(2 * H):
                    if a >= 2:
                        pe.wait_ge(taken, a - 1)
                    k = a
                    for h in range(2):
                        for c in range(TCH):
                            ins = nc.tensor.matmul(psum[a % 2][:, h, 0:SH], terms[:, c, :, k], m.sel[:, c, h * SH:(h + 1) * SH], start=(c == 0), stop=(c == TCH - 1))
                    ins.then_inc(moved, 1)

            @block.vector
            def _(dve):
                nc.vector.memset(slot_terms[:, :, S:S + GROUP], 0.0).then_inc(zeroed, 1)
                dve.wait_ge(zeroed, 1)
                for a in range(2 * H):
                    if a == H:
                        dve.wait_ge(stored, 16)
                    dve.wait_ge(moved, a + 1)
                    nc.vector.tensor_copy(slot_terms[:, a % H, 0:S].rearrange("p (h s) -> p h s", h=2), psum[a % 2][:, :, 0:SH]).then_inc(taken, 1)


def phase_table_weights(nc, m, w, l, sem):
    loaded = sem("weights_loaded")
    step = sem("tw_step")
    with ExitStack() as ctx:
        sb, ps = buf_maker(nc, ctx, f"tw{l}")
        wd = sb("wd", [P, 2, D])
        av = sb("av", [P, 2, D])
        prod = sb("prod", [P, 2, 2, D])
        with nc.Block() as block:
            @block.sync
            def _(sp):
                sp.dma_start(m.w_table[:, :, 0:D], w[f"Ws{l}"].rearrange("(k p) n -> p k n", p=P)).then_inc(loaded, 16)
                sp.dma_start(wd[:], w[f"Wd{l}"].rearrange("(k p) n -> p k n", p=P)).then_inc(loaded, 16)
                sp.dma_start(av[:, 0, :], w[f"ad{l}"].rearrange("h (o c) -> o (h c)", o=1).to_broadcast([P, D])).then_inc(loaded, 16)
                sp.dma_start(av[:, 1, :], w[f"as{l}"].rearrange("h (o c) -> o (h c)", o=1).to_broadcast([P, D])).then_inc(loaded, 16)

            @block.vector
            def _(dve):
                ch = Chain(dve, step)
                dve.wait_ge(loaded, 4 * 16)
                for k in range(2):
                    ch.do(nc.vector.tensor_tensor(prod[:, k, 0, :], m.w_table[:, k, 0:D], av[:, 0, :], ALU.mult))
                    ch.do(nc.vector.tensor_tensor(prod[:, k, 1, :], wd[:, k, :], av[:, 1, :], ALU.mult))
                ch.wait()
                for k in range(2):
                    ch.do(nc.vector.tensor_reduce(m.w_table[:, k, D:D + 2 * H], prod[:, k, :, :].rearrange("p a (h c) -> p (a h) c", c=C), AX_X, ALU.add))
                ch.wait()


def tile_of(dram, n):
    return dram[bass.ds(n, 1), :, :].rearrange("o p k -> p (o k)")


def load_and_store(eng, load, store):
    half = NT // 2
    load(0, 0, 0)
    with eng.Fori(0, half - 1) as it:
        load(it * 2 + 1, 1, it)
        store(it * 2, 0, it)
        load(it * 2 + 2, 0, it + 1)
        store(it * 2 + 1, 1, it)
    load(NT - 1, 1, half - 1)
    store(NT - 2, 0, half - 1)
    store(NT - 1, 1, half - 1)


def phase_table(nc, m, d, h_dram, l, sem):
    in_ready = [sem(f"h_loaded{b}") for b in range(2)]
    in_free = sem("h_free")
    t_ready = sem("hT_ready")
    t_copied = sem("hT_copied")
    o_ready = sem("row_ready")
    o_copied = sem("row_copied")
    stored = [sem(f"row_stored{b}") for b in range(2)]
    with ExitStack() as ctx:
        sb, ps = buf_maker(nc, ctx, f"tb{l}")
        h = [sb(f"h{b}", [P, D]) for b in range(2)]
        hT = [sb(f"hT{b}", [P, 2, P]) for b in range(2)]
        row = [sb(f"row{b}", [P, TABW]) for b in range(2)]
        psT = [ps(f"psT{b}", [P, 2, P]) for b in range(2)]
        psO = [ps(f"psO{b}", [P, D + 2 * H]) for b in range(2)]
        with nc.Block() as block:
            @block.sync
            def _(sp):
                for b in range(2):
                    sp.sem_inc(stored[b], 16)

                def load(n, b, turn):
                    sp.wait_ge(in_free, n + 1)
                    sp.dma_start(h[b][:], tile_of(h_dram, n)).then_inc(in_ready[b], 16)

                def store(n, b, turn):
                    sp.wait_ge(o_copied, n + 3)
                    sp.dma_start(d.table[bass.ds(n * P, P), :], row[b][:]).then_inc(stored[b], 16)
                load_and_store(sp, load, store)
                for b in range(2):
                    sp.wait_ge(stored[b], 16 * (NT // 2 + 1))

            @block.tensor
            def _(pe):
                pe.sem_inc(in_free, 2)
                with pe.Fori(0, NT // 2) as it:
                    for b in range(2):
                        n = it * 2 + b
                        pe.wait_ge(in_ready[b], it * 16 + 16)
                        pe.wait_ge(t_copied, n + 1)
                        for k in range(2):
                            ins = nc.tensor.transpose(psT[b][:, k, :], h[b][:, k * P:(k + 1) * P], m.ident[:])
                        ins.then_inc(t_ready, 1)
                        pe.wait_ge(t_ready, n + 1)
                        pe.sem_inc(in_free, 1)
                        pe.wait_ge(t_copied, n + 3)
                        pe.wait_ge(o_copied, n + 1)
                        for k in range(2):
                            ins = nc.tensor.matmul(psO[b][:], hT[b][:, k, :], m.w_table[:, k, :], start=(k == 0), stop=(k == 1))
                        ins.then_inc(o_ready, 1)

            @block.scalar
            def _(act):
                act.sem_inc(t_copied, 2)
                with act.Fori(0, NT // 2) as it:
                    for b in range(2):
                        n = it * 2 + b
                        act.wait_ge(t_ready, n + 1)
                        act.wait_ge(o_copied, n + 1)
                        nc.scalar.copy(hT[b][:], psT[b][:]).then_inc(t_copied, 1)

            @block.vector
            def _(dve):
                dve.sem_inc(o_copied, 2)
                with dve.Fori(0, NT // 2) as it:
                    for b in range(2):
                        n = it * 2 + b
                        dve.wait_ge(o_ready, n + 1)
                        dve.wait_ge(stored[b], it * 16 + 16)
                        nc.vector.tensor_copy(row[b][:], psO[b][:, 0:TABW])
                        nc.vector.tensor_copy(m.a_j[:, bass.ds(n * H, H)], psO[b][:, D:D + H])
                        nc.vector.tensor_copy(m.a_i[:, bass.ds(n * H, H)], psO[b][:, TABW:TABW + H]).then_inc(o_copied, 1)


def phase_attention(nc, m, d, l, sem):
    x_ready = [sem(f"rows_gathered{b}") for b in range(SETS)]
    idx_ready = sem("index_ready")
    idx_pass = sem("index_pass")
    full_ready = sem("onehot_full")
    first_ready = sem("first_spread")
    t_ready = sem("onehotT")
    t_copied = sem("onehotT_copied")
    ai_ready = sem("a_dst")
    z_ready = sem("logit_sum")
    al_ready = sem("logits")
    al_step = sem("logit_step")
    xT_ready = sem("logitsT")
    mT_step = sem("maxT_step")
    mT_ready = sem("maxT")
    m_ready = sem("max_back")
    shift_ready = sem("shifted")
    cols_ready = sem("max_columns")
    ex_ready = sem("exps")
    rhs_ready = sem("messages")
    o_ready = sem("slot_sums")
    acc_done = sem("added")
    row_copied = sem("carry_copied")
    row_stored = [sem(f"carry_stored{b}") for b in range(2)]
    zeroed = sem("agg_zeroed")
    with ExitStack() as ctx:
        sb, ps = buf_maker(nc, ctx, f"at{l}")
        x = [sb(f"x{b}", [P, GROUP, XW]) for b in range(SETS)]
        idx = [sb(f"idx{b}", [P, GROUP], I32) for b in range(SETS)]
        full = sb("full", [P, GROUP, P])
        main = [sb(f"main{b}", [P, GROUP, P]) for b in range(2)]
        fullT = sb("fullT", [P, GROUP, P])
        crow = [sb(f"crow{b}", [1, GROUP, AGG]) for b in range(2)]
        first = sb("first", [P, GROUP, H])
        z = sb("z", [P, GROUP, H])
        al = sb("al", [P, GROUP, H])
        shifted = sb("shifted", [P, GROUP, H])
        flag = sb("flag", [GROUP * H, P + 1])
        fwd = sb("fwd", [GROUP * H, P])
        mx = sb("mx", [GROUP * H, P])
        psT = [ps(f"psT{b}", [P, GROUP // 2, P]) for b in range(2)]
        psA = ps("psA", [P, GROUP, H])
        psX = ps("psX", [GROUP * H, 2, P])
        psM = ps("psM", [P, GROUP, H])
        psO = [ps(f"psO{b}", [P, 512]) for b in range(2)]
        NTURN = NG // SETS

        with nc.Block() as block:
            @block.gpsimd
            def _(pool):
                def gather(g, b, reused):
                    if reused:
                        pool.wait_ge(o_ready, (g - SETS + 1) * GROUP)
                    nc.gpsimd.tensor_copy(idx[b][:], m.src_slot[:, bass.ds(g * GROUP, GROUP)]).then_inc(idx_ready, 1)
                    pool.wait_ge(idx_ready, g + 1)
                    pool.sem_inc(idx_pass, 1)
                    for j in range(GROUP):
                        pool.indirect_dma_start(x[b][:, j, 0:TABW], None, d.table[0:NR, :],
                                                bass.IndirectOffsetOnAxis(ap=idx[b][:, j:j + 1], axis=0)).then_inc(x_ready[b], 16)
                for b in range(SETS):
                    gather(b, b, False)
                with pool.Fori(1, NTURN) as it:
                    for b in range(SETS):
                        gather(it * SETS + b, b, True)
                gather(NG, 0, True)
                pool.wait_ge(x_ready[0], 16 * GROUP * (NTURN + 1))

            @block.tensor
            def _(pe):
                regs = [pe.alloc_register(f"pe_n{l}_{j}") for j in range(GROUP)]
                pe.sem_inc(t_ready, 2)
                pe.sem_inc(ai_ready, 1)

                def transposes(g, b):
                    pe.wait_ge(full_ready, g + 1)
                    for h in range(2):
                        pe.wait_ge(t_copied, g * 2 + h + 1)
                        for j in range(GROUP // 2):
                            ins = nc.tensor.transpose(psT[h][:, j, :], full[:, h * (GROUP // 2) + j, :], m.ident[:])
                        ins.then_inc(t_ready, 1)

                def dst_terms(g, b):
                    pe.load(regs, m.nrow[0:1, bass.ds(g * GROUP, GROUP)])
                    ns = [pe.snap(r, min_val=0, max_val=NT - 1) for r in regs]
                    pe.wait_ge(z_ready, g + 1)
                    for h in range(2):
                        pe.wait_ge(t_copied, g * 2 + h + 3)
                        for j in range(h * (GROUP // 2), (h + 1) * (GROUP // 2)):
                            ins = nc.tensor.matmul(psA[:, j, :], fullT[:, j, :], m.a_i[:, bass.ds(ns[j] * H, H)], start=True, stop=True)
                    ins.then_inc(ai_ready, 1)

                def turn_logits(g, b):
                    pe.wait_ge(al_ready, g + 1)
                    pe.wait_ge(first_ready, g + 1)
                    pe.wait_ge(mT_ready, g + 1)
                    nc.tensor.matmul(psX[:, 0, :], al[:].rearrange("p j h -> p (j h)"), m.ident[:], start=True, stop=True)
                    nc.tensor.matmul(psX[:, 1, :], first[:].rearrange("p j h -> p (j h)"), m.ident[:], start=True, stop=True).then_inc(xT_ready, 1)

                def turn_max(g, b):
                    pe.wait_ge(mT_ready, g + 2)
                    pe.wait_ge(cols_ready, g + 1)
                    nc.tensor.matmul(psM[:].rearrange("p j h -> p (j h)"), mx[:], m.ident[0:GROUP * H, 0:GROUP * H], start=True, stop=True).then_inc(m_ready, 1)

                def sums(g, b, j):
                    i = g * GROUP + j
                    pe.wait_ge(rhs_ready, i + 1)
                    pe.wait_ge(acc_done, i + 1)
                    ins = nc.tensor.matmul(psO[(b * GROUP + j) % 2][:, 0:AGG], main[b % 2][:, j, :], x[b][:, j, 0:AGG], start=True, stop=True)
                    ins.then_inc(o_ready, 1)

                def chain(g, b):
                    transposes(g, b)
                    dst_terms(g, b)
                    turn_logits(g, b)
                    turn_max(g, b)
                chain(0, 0)
                with pe.Fori(0, NTURN) as it:
                    for b in range(SETS):
                        g = it * SETS + b
                        g1, b1 = g + 1, (b + 1) % SETS
                        sums(g, b, 0)
                        transposes(g1, b1)
                        sums(g, b, 1)
                        dst_terms(g1, b1)
                        sums(g, b, 2)
                        sums(g, b, 3)
                        turn_logits(g1, b1)
                        sums(g, b, 4)
                        sums(g, b, 5)
                        turn_max(g1, b1)
                        sums(g, b, 6)
                        sums(g, b, 7)

            @block.scalar
            def _(act):
                act.sem_inc(t_copied, 2)
                act.sem_inc(row_copied, 2)
                for b in range(2):
                    act.sem_inc(row_stored[b], 16)

                def copy_T(g, b):
                    for h in range(2):
                        act.wait_ge(t_ready, g * 2 + h + 3)
                        act.wait_ge(ai_ready, g + 1)
                        nc.scalar.copy(fullT[:, h * (GROUP // 2):(h + 1) * (GROUP // 2), :], psT[h][:]).then_inc(t_copied, 1)

                def exps(g, b):
                    act.wait_ge(shift_ready, g + 1)
                    nc.scalar.activation(x[b][:, :, D:D + H], shifted[:], ACT.Exp).then_inc(ex_ready, 1)

                def carry(g, b, j):
                    i = g * GROUP + j
                    act.wait_ge(o_ready, i + 1)
                    nc.scalar.copy(crow[b % 2][:, j, :], psO[(b * GROUP + j) % 2][0:1, 0:AGG]).then_inc(row_copied, 1)

                copy_T(0, 0)
                exps(0, 0)
                with act.Fori(0, NTURN) as it:
                    for b in range(SETS):
                        g = it * SETS + b
                        g1, b1 = g + 1, (b + 1) % SETS
                        act.wait_ge(row_stored[b % 2], it * 32 + (b // 2) * 16 + 16)
                        carry(g, b, 0)
                        copy_T(g1, b1)
                        for j in range(1, GROUP - 1):
                            carry(g, b, j)
                        exps(g1, b1)
                        carry(g, b, GROUP - 1)

            @block.sync
            def _(sp):
                with sp.Fori(0, NTURN) as it:
                    for b in range(SETS):
                        g = it * SETS + b
                        sp.wait_ge(row_copied, g * GROUP + GROUP + 2)
                        sp.dma_start(d.carry[bass.ds(g * GROUP, GROUP), :].rearrange("(o j) k -> o (j k)", o=1),
                                     crow[b % 2][:].rearrange("o j k -> o (j k)")).then_inc(row_stored[b % 2], 16)
                for b in range(2):
                    sp.wait_ge(row_stored[b], 16 * (NG // 2 + 1))

            @block.vector
            def _(dve):
                regs = [dve.alloc_register(f"dve_n{l}_{j}") for j in range(GROUP)]
                nc.vector.memset(m.agg[:], 0.0).then_inc(zeroed, 1)
                nc.vector.memset(flag[:], 0.0).then_inc(zeroed, 1)
                dve.sem_inc(z_ready, 1)
                dve.sem_inc(mT_ready, 1)
                dve.sem_inc(cols_ready, 1)
                dve.sem_inc(acc_done, 2)
                mT_ch = Chain(dve, mT_step, 2)
                dve.wait_ge(zeroed, 2)

                def onehots(g, b):
                    at = bass.ds(g * GROUP, GROUP)
                    iota = m.iota[:, 0:P].unsqueeze(1).to_broadcast([P, GROUP, P])
                    dve.wait_ge(t_ready, g * 2 + 2)
                    dve.wait_ge(cols_ready, g + 1)
                    nc.vector.tensor_tensor(full[:], iota, m.loc[:, at].unsqueeze(2).to_broadcast([P, GROUP, P]), ALU.is_equal).then_inc(full_ready, 1)
                    nc.vector.tensor_tensor(main[b % 2][:], iota, m.loc_m[:, at].unsqueeze(2).to_broadcast([P, GROUP, P]), ALU.is_equal)
                    nc.vector.tensor_copy(first[:], m.first[:, at].unsqueeze(2).to_broadcast([P, GROUP, H])).then_inc(first_ready, 1)

                def logits(g, b, turn):
                    dve.wait_ge(ai_ready, g + 2)
                    nc.vector.tensor_tensor(z[:], psA[:], m.slot_terms[:, :, bass.ds(g * GROUP, GROUP)].rearrange("p h j -> p j h"), ALU.add).then_inc(z_ready, 1)
                    dve.wait_ge(z_ready, g + 2)
                    dve.wait_ge(x_ready[b], turn * (16 * GROUP) + 16 * GROUP)
                    nc.vector.tensor_tensor(z[:], z[:], x[b][:, :, D:D + H], ALU.add).then_inc(al_step, 1)
                    dve.wait_ge(al_step, g + 1)
                    nc.vector.scalar_tensor_tensor(out=al[:], in0=z[:], scalar=NEG_SLOPE, in1=z[:], op0=ALU.mult, op1=ALU.max).then_inc(al_ready, 1)

                def scans(g, b):
                    mT_ch.turn(g)
                    dve.wait_ge(xT_ready, g + 1)
                    mT_ch.link(nc.vector.tensor_scalar(flag[:, 0:P], psX[:, 1, :], -BIG, None, ALU.mult))
                    mT_ch.link(nc.vector.tensor_tensor_scan(fwd[:], flag[:, 0:P], psX[:, 0, :], -BIG, ALU.add, ALU.max))
                    nc.vector.tensor_tensor_scan(mx[:, ::-1], flag[:, P:0:-1], fwd[:, ::-1], -BIG, ALU.add, ALU.max).then_inc(mT_ready, 1)
                    mT_ch.close()

                def shifts(g, b):
                    dve.wait_ge(m_ready, g + 1)
                    nc.vector.tensor_tensor(shifted[:], al[:], psM[:], ALU.subtract).then_inc(shift_ready, 1)
                    nc.vector.tensor_copy(x[b][:, :, D + 2 * H:AGG], first[:, :, 0:1])
                    nc.vector.tensor_tensor(x[b][:, :, D + H:D + 2 * H], psM[:], first[:], ALU.mult).then_inc(cols_ready, 1)

                def message(g, b, j):
                    if j == 0:
                        dve.wait_ge(ex_ready, g + 1)
                    v = x[b][:, j, 0:D].rearrange("p (h c) -> p h c", c=C)
                    nc.vector.tensor_tensor(v, v, x[b][:, j, D:D + H].unsqueeze(2).to_broadcast([P, H, C]), ALU.mult).then_inc(rhs_ready, 1)

                def add(g, b, j, ns):
                    i = g * GROUP + j
                    dve.wait_ge(row_copied, i + 3)
                    dve.wait_ge(acc_done, i + 2)
                    to = m.agg[:, bass.ds(ns[j] * AGG, AGG)]
                    nc.vector.tensor_tensor(to, to, psO[(b * GROUP + j) % 2][:, 0:AGG], ALU.add).then_inc(acc_done, 1)

                onehots(0, 0)
                logits(0, 0, 0)
                scans(0, 0)
                shifts(0, 0)
                with dve.Fori(0, NTURN) as it:
                    for b in range(SETS):
                        g = it * SETS + b
                        g1, b1 = g + 1, (b + 1) % SETS
                        t1 = it + 1 if b1 == 0 else it
                        dve.load(regs, m.nrow[0:1, bass.ds(g * GROUP, GROUP)])
                        ns = [dve.snap(r, min_val=0, max_val=NT - 1) for r in regs]
                        message(g, b, 0)
                        message(g, b, 1)
                        onehots(g1, b1)
                        message(g, b, 2)
                        add(g, b, 0, ns)
                        message(g, b, 3)
                        add(g, b, 1, ns)
                        logits(g1, b1, t1)
                        message(g, b, 4)
                        add(g, b, 2, ns)
                        message(g, b, 5)
                        add(g, b, 3, ns)
                        scans(g1, b1)
                        message(g, b, 6)
                        add(g, b, 4, ns)
                        message(g, b, 7)
                        add(g, b, 5, ns)
                        add(g, b, 6, ns)
                        shifts(g1, b1)
                        add(g, b, 7, ns)


def phase_load_terms(nc, m, d, l, sem):
    loaded = sem("terms_loaded")
    with nc.Block() as block:
        @block.sync
        def _(sp):
            sp.dma_start(m.slot_terms[:], d.terms[l - 1]).then_inc(loaded, 16)
            sp.wait_ge(loaded, 16)


def phase_carry(nc, m, d, l, cagg, sem):
    zeroed = sem("tail_zeroed")
    loaded = sem("carry_loaded")
    step = sem("carry_step")
    turned = sem("maxima_turned")
    mT_ready = sem("node_maxima")
    back = sem("maxima_back")
    diff_ready = sem("diff_ready")
    ex_ready = sem("factors_ready")
    rows_ready = sem("rows_scaled")
    hot_ready = sem("onehot_ready")
    hot_step = sem("tile_step")
    o_ready = sem("tile_summed")
    o_copied = sem("tile_copied")
    W = SCH * P
    FULL = S // P
    with ExitStack() as ctx:
        sb, ps = buf_maker(nc, ctx, f"cy{l}")
        rows = sb("rows", [P, SCH, AGG])
        mT = sb("mT", [H, W])
        flag = sb("flag", [H, W + 1])
        firstT = sb("firstT", [H, W])
        f8 = sb("f8", [P, SCH, H])
        diff = sb("diff", [P, SCH, H])
        ex = sb("ex", [P, SCH, H])
        rel = sb("rel", [P, SCH])
        hot = [sb(f"hot{b}", [P, SCH, P]) for b in range(2)]
        psT = [ps(f"psT{b}", [H, 4, P]) for b in range(2)]
        psB = [ps(f"psB{b}", [P, SCH, H]) for b in range(2)]
        psO = [ps(f"psO{b}", [P, 512]) for b in range(2)]
        with nc.Block() as block:
            @block.sync
            def _(sp):
                sp.wait_ge(zeroed, 1)
                sp.dma_start(rows[:, 0:FULL, :], d.carry[0:FULL * P, :].rearrange("(c p) k -> p c k", p=P)).then_inc(loaded, 16)
                if S % P:
                    sp.dma_start(rows[0:S % P, FULL, :], d.carry[FULL * P:S, :]).then_inc(loaded, 16)

            @block.tensor
            def _(pe):
                pe.wait_ge(loaded, 16 * (1 + (S % P > 0)))
                for c in range(SCH):
                    ins = nc.tensor.transpose(psT[c // 4][:, c % 4, :], rows[:, c, D + H:D + 2 * H], m.ident[:])
                ins.then_inc(turned, 1)
                pe.wait_ge(mT_ready, 1)
                for c in range(SCH):
                    nc.tensor.transpose(psB[0][:, c, :], mT[:, c * P:(c + 1) * P], m.ident[0:H, 0:H])
                    ins = nc.tensor.transpose(psB[1][:, c, :], firstT[:, c * P:(c + 1) * P], m.ident[0:H, 0:H])
                ins.then_inc(back, 1)
                pe.wait_ge(rows_ready, 1)
                pe.sem_inc(o_ready, 2)
                with pe.Fori(0, NT // 2) as it:
                    for b in range(2):
                        n = it * 2 + b
                        pe.wait_ge(hot_ready, n + 3)
                        pe.wait_ge(o_copied, n + 1)
                        for c in range(SCH):
                            ins = nc.tensor.matmul(psO[b][:, 0:AGG], hot[b][:, c, :], rows[:, c, :], start=(c == 0), stop=(c == SCH - 1))
                        ins.then_inc(o_ready, 1)

            @block.scalar
            def _(act):
                act.wait_ge(diff_ready, 1)
                nc.scalar.activation(ex[:], diff[:], ACT.Exp).then_inc(ex_ready, 1)
                act.sem_inc(o_copied, 2)
                with act.Fori(0, NT // 2) as it:
                    for b in range(2):
                        n = it * 2 + b
                        act.wait_ge(o_ready, n + 3)
                        nc.scalar.copy(cagg[:, bass.ds(n * AGG, AGG)], psO[b][:, 0:AGG]).then_inc(o_copied, 1)

            @block.vector
            def _(dve):
                ch = Chain(dve, step)
                nc.vector.memset(rows[:, FULL:SCH, :], 0.0).then_inc(zeroed, 1)
                ch.do(nc.vector.memset(flag[:], 0.0))
                ch.do(nc.vector.memset(mT[:], 0.0))
                ch.link(nc.vector.memset(firstT[:], 1.0))
                ch.link(nc.vector.tensor_tensor(firstT[:, 1:S], m.carry_b[:, 1:S], m.carry_b[:, 0:S - 1], ALU.not_equal))
                ch.link(nc.vector.tensor_scalar(flag[:, 0:S], firstT[:, 0:S], -BIG, None, ALU.mult))
                dve.wait_ge(turned, 1)
                for b, (c0, c1) in enumerate(((0, 4), (4, SCH))):
                    ch.do(nc.vector.tensor_copy(mT[:, c0 * P:c1 * P].rearrange("p (c q) -> p c q", q=P), psT[b][:, 0:c1 - c0, :]))
                ch.wait()
                ch.link(nc.vector.tensor_tensor_scan(mT[:, 0:S], flag[:, 0:S], mT[:, 0:S], -BIG, ALU.add, ALU.max))
                nc.vector.tensor_tensor_scan(mT[:, S - 1::-1], flag[:, S:0:-1], mT[:, S - 1::-1], -BIG, ALU.add, ALU.max).then_inc(mT_ready, 1)
                dve.wait_ge(back, 1)
                ch.do(nc.vector.tensor_copy(f8[:], psB[1][:]))
                nc.vector.tensor_tensor(diff[:], rows[:, :, D + H:D + 2 * H], psB[0][:], ALU.subtract).then_inc(diff_ready, 1)
                dve.wait_ge(ex_ready, 1)
                ch.wait()
                dve.wait_ge(diff_ready, 1)
                for c in range(SCH):
                    v = rows[:, c, 0:D].rearrange("p (h k) -> p h k", k=C)
                    ch.do(nc.vector.tensor_tensor(v, v, ex[:, c, :].unsqueeze(2).to_broadcast([P, H, C]), ALU.mult))
                ch.do(nc.vector.tensor_tensor(rows[:, :, D:D + H], rows[:, :, D:D + H], ex[:], ALU.mult))
                ch.do(nc.vector.tensor_tensor(rows[:, :, D + H:D + 2 * H], psB[0][:], f8[:], ALU.mult))
                ch.do(nc.vector.tensor_copy(rows[:, :, D + 2 * H:AGG], f8[:, :, 0:1]))
                ch.wait()
                nc.vector.tensor_scalar(rel[:], m.carry_col[:], float(P), None, ALU.add).then_inc(rows_ready, 1)
                dve.wait_ge(rows_ready, 1)
                per = Chain(dve, hot_step, 1)
                dve.sem_inc(hot_ready, 2)
                with dve.Fori(0, NT // 2) as it:
                    for b in range(2):
                        n = it * 2 + b
                        per.turn(n)
                        dve.wait_ge(hot_ready, n + 2)
                        dve.wait_ge(o_ready, n + 1)
                        per.link(nc.vector.tensor_scalar(rel[:], rel[:], float(P), None, ALU.subtract))
                        nc.vector.tensor_tensor(hot[b][:], m.iota[:, 0:P].unsqueeze(1).to_broadcast([P, SCH, P]), rel[:].unsqueeze(2).to_broadcast([P, SCH, P]), ALU.is_equal).then_inc(hot_ready, 1)
                        per.close()


def phase_factors(nc, m, d, l, cagg, fac, sem):
    step = sem("factor_step")
    diff_ready = sem("diff_ready")
    ex_ready = sem("exp_ready")
    with ExitStack() as ctx:
        sb, ps = buf_maker(nc, ctx, f"fa{l}")
        a = sb("self", [P, NT, H])
        mm = sb("max", [P, 3, NT, H])
        t = sb("t", [P, NT, H])
        den = sb("den", [P, NT, H])
        agg = m.agg[:].rearrange("p (n k) -> p n k", k=AGG)
        cg = cagg[:].rearrange("p (n k) -> p n k", k=AGG)

        def bc(v):
            return v.to_broadcast([P, NT, H])
        with nc.Block() as block:
            @block.vector
            def _(dve):
                ch = Chain(dve, step)
                v = nc.vector
                ch.link(v.tensor_tensor(a[:].rearrange("p n h -> p (n h)"), m.a_i[:], m.a_j[:], ALU.add))
                ch.link(v.tensor_tensor(a[:], a[:], bc(m.self_term[:, (l - 1) * H:l * H].unsqueeze(1)), ALU.add))
                ch.link(v.scalar_tensor_tensor(out=mm[:, 2, :, :], in0=a[:], scalar=NEG_SLOPE, in1=a[:], op0=ALU.mult, op1=ALU.max))
                for k, src in enumerate((agg, cg)):
                    ch.link(v.tensor_scalar(t[:], bc(src[:, :, D + 2 * H:AGG]), 1.0, BIG, ALU.subtract, ALU.mult))
                    ch.link(v.tensor_tensor(mm[:, k, :, :], t[:], src[:, :, D + H:D + 2 * H], ALU.add))
                ch.link(v.tensor_tensor(a[:], mm[:, 0, :, :], mm[:, 1, :, :], ALU.max))
                ch.link(v.tensor_tensor(a[:], a[:], mm[:, 2, :, :], ALU.max))
                for k in range(3):
                    ins = v.tensor_tensor(mm[:, k, :, :], mm[:, k, :, :], a[:], ALU.subtract)
                ins.then_inc(diff_ready, 1)
                dve.wait_ge(ex_ready, 1)
                ch.do(v.tensor_tensor(den[:], agg[:, :, D:D + H], fac[:, 0, :, :], ALU.mult))
                ch.link(v.tensor_tensor(t[:], cg[:, :, D:D + H], fac[:, 1, :, :], ALU.mult))
                ch.link(v.tensor_tensor(den[:], den[:], t[:], ALU.add))
                ch.link(v.scalar_tensor_tensor(out=den[:], in0=den[:], scalar=1e-16, in1=fac[:, 2, :, :], op0=ALU.add, op1=ALU.add))
                ch.link(v.reciprocal(t[:], den[:]))
                for k in range(3):
                    ch.do(v.tensor_tensor(fac[:, k, :, :], fac[:, k, :, :], t[:], ALU.mult))
                ch.wait()

            @block.scalar
            def _(act):
                act.wait_ge(diff_ready, 1)
                nc.scalar.activation(fac[:].rearrange("p a n h -> p (a n h)"), mm[:].rearrange("p a n h -> p (a n h)"), ACT.Exp).then_inc(ex_ready, 1)


def phase_project(nc, m, d, w, l, cagg, fac, mv, sem):
    w_ready = sem("wo_loaded")
    bias_ready = sem("bias_ready")
    in_ready = [sem(f"xs_loaded{b}") for b in range(2)]
    step = sem("weigh_step")
    sum_ready = sem("weighed")
    t_ready = sem("turned")
    t_copied = sem("turned_copied")
    o_ready = sem("projected")
    kept = sem("kept")
    stat = sem("row_stats")
    stat_read = sem("stats_read")
    held = sem("held")
    PER = 5
    with ExitStack() as ctx:
        sb, ps = buf_maker(nc, ctx, f"pj{l}")
        wo = sb("wo", [P, 2, D])
        bias = sb("bias", [1, 2, D])
        x = [sb(f"x{b}", [P, D]) for b in range(2)]
        s1 = [sb(f"s1{b}", [P, D]) for b in range(2)]
        s2 = sb("s2", [P, D])
        sT = [sb(f"sT{b}", [P, 2, P]) for b in range(2)]
        st = [sb(f"st{b}", [P, 6]) for b in range(2)]
        mv1 = [sb(f"mv1{b}", [P, 2]) for b in range(2)]
        psT = [ps(f"psT{b}", [P, 2, P]) for b in range(2)]
        psO = [ps(f"psO{b}", [P, D]) for b in range(2)]
        with nc.Block() as block:
            @block.sync
            def _(sp):
                sp.dma_start(wo[:], w[f"Wo{l}"].rearrange("(k p) n -> p k n", p=P)).then_inc(w_ready, 16)
                sp.dma_start(bias[:, 0, :], w[f"bo{l}"].rearrange("(o n) -> o n", o=1)).then_inc(w_ready, 16)
                sp.dma_start(bias[:, 1, :], w[f"b{l}"].rearrange("(o n) -> o n", o=1)).then_inc(w_ready, 16)
                with sp.Fori(0, NT // 2) as it:
                    for b in range(2):
                        n = it * 2 + b
                        sp.wait_ge(sum_ready, n + 1)
                        sp.dma_start(x[b][:], d.table[bass.ds(n * P, P), 0:D]).then_inc(in_ready[b], 16)

            @block.vector
            def _(dve):
                v = nc.vector
                ch = Chain(dve, step, PER)
                dve.wait_ge(w_ready, 48)
                v.tensor_tensor(bias[:, 0, :], bias[:, 0, :], bias[:, 1, :], ALU.add).then_inc(bias_ready, 1)
                dve.sem_inc(sum_ready, 2)

                def weigh(n, b, turn):
                    ch.turn(n)
                    dve.wait_ge(in_ready[b], turn * 16 + 16)
                    dve.wait_ge(t_ready, n + 1)
                    dve.wait_ge(sum_ready, n + 2)

                    def hv(a):
                        return a.rearrange("p (h c) -> p h c", c=C)

                    def f(k):
                        return fac[:, k, bass.ds(n, 1), :].rearrange("p o h -> p h o").to_broadcast([P, H, C])
                    ch.do(v.tensor_tensor(hv(s1[b][:]), hv(m.agg[:, bass.ds(n * AGG, D)]), f(0), ALU.mult))
                    ch.link(v.tensor_tensor(hv(s2[:]), hv(cagg[:, bass.ds(n * AGG, D)]), f(1), ALU.mult))
                    ch.do(v.tensor_tensor(s1[b][:], s1[b][:], s2[:], ALU.add))
                    ch.do(v.tensor_tensor(hv(x[b][:]), hv(x[b][:]), f(2), ALU.mult))
                    ch.wait()
                    v.tensor_tensor(s1[b][:], s1[b][:], x[b][:], ALU.add).then_inc(sum_ready, 1)

                def stats(n, b):
                    dve.wait_ge(o_ready, n + 1)
                    v.bn_stats(st[b][:], psO[b][:]).then_inc(stat_read, 1)
                    dve.wait_ge(stat_read, n + 1)
                    dve.sem_inc(held, 1)
                    ch.link(v.bn_aggr(mv1[b][:], st[b][:]))
                    v.tensor_copy(mv[:, bass.ds(n * 2, 2)], mv1[b][:]).then_inc(stat, 1)
                    ch.close()
                with dve.Fori(0, NT // 2) as it:
                    for b in range(2):
                        n = it * 2 + b
                        weigh(n, b, it)
                        stats(n, b)
                dve.wait_ge(stat, NT)

            @block.tensor
            def _(pe):
                pe.wait_ge(bias_ready, 1)
                pe.sem_inc(t_ready, 2)
                with pe.Fori(0, NT // 2) as it:
                    for b in range(2):
                        n = it * 2 + b
                        pe.wait_ge(sum_ready, n + 3)
                        pe.wait_ge(t_copied, n + 1)
                        for k in range(2):
                            ins = nc.tensor.transpose(psT[b][:, k, :], s1[b][:, k * P:(k + 1) * P], m.ident[:])
                        ins.then_inc(t_ready, 1)
                        pe.wait_ge(t_copied, n + 3)
                        pe.wait_ge(kept, n + 1)
                        nc.tensor.matmul(psO[b][:], m.ones[0:1, :], bias[0:1, 0, :], start=True, stop=False)
                        for k in range(2):
                            ins = nc.tensor.matmul(psO[b][:], sT[b][:, k, :], wo[:, k, :], start=False, stop=(k == 1))
                        ins.then_inc(o_ready, 1)

            @block.scalar
            def _(act):
                act.sem_inc(t_copied, 2)
                act.sem_inc(kept, 2)
                with act.Fori(0, NT // 2) as it:
                    for b in range(2):
                        n = it * 2 + b
                        act.wait_ge(t_ready, n + 3)
                        nc.scalar.copy(sT[b][:], psT[b][:]).then_inc(t_copied, 1)
                        act.wait_ge(stat_read, n + 1)
                        nc.scalar.copy(m.agg[:, bass.ds(n * AGG, D)], psO[b][:]).then_inc(kept, 1)


def phase_norm(nc, m, d, w, l, h_dram, mv, bn, sem):
    w_ready = sem("rows_loaded")
    in_ready = [sem(f"h_loaded{b}") for b in range(2)]
    step = sem("norm_step")
    eps_ready = sem("var_eps")
    sd_ready = sem("deviation")
    y_step = sem("y_step")
    y_ready = sem("y_ready")
    sq_ready = sem("squared")
    summed = sem("summed")
    bn_step = sem("bn_step")
    var_ready = sem("bn_var")
    bsd_ready = sem("bn_deviation")
    PER = 3
    with ExitStack() as ctx:
        sb, ps = buf_maker(nc, ctx, f"nm{l}")
        par = sb("par", [P, 4, D])
        h = [sb(f"h{b}", [P, D]) for b in range(2)]
        sd = sb("sd", [P, NT])
        rs = sb("rs", [P, NT])
        sq = [sb(f"sq{b}", [P, D]) for b in range(2)]
        mean = sb("mean", [P, D])
        var = sb("var", [P, D])
        psS = [ps(f"psS{b}", [P, D]) for b in range(2)]
        mvv = mv[:].rearrange("p (n k) -> p n k", k=2)

        def tiles(eng, body):
            body(0, 0, 0, "first")
            body(1, 1, 0, "mid")
            with eng.Fori(1, NT // 2 - 1) as it:
                for b in range(2):
                    body(it * 2 + b, b, it, "mid")
            body(NT - 2, 0, NT // 2 - 1, "mid")
            body(NT - 1, 1, NT // 2 - 1, "last")
        with nc.Block() as block:
            @block.sync
            def _(sp):
                for k, name in enumerate((f"lg{l}", f"lb{l}", f"bng{l}", f"bnb{l}")):
                    sp.dma_start(par[:, k, :], w[name].rearrange("(o n) -> o n", o=1).to_broadcast([P, D])).then_inc(w_ready, 16)
                with sp.Fori(0, NT // 2) as it:
                    for b in range(2):
                        n = it * 2 + b
                        sp.wait_ge(y_ready, n + 1)
                        sp.dma_start(h[b][:], tile_of(h_dram, n)).then_inc(in_ready[b], 16)

            @block.scalar
            def _(act):
                act.wait_ge(eps_ready, 1)
                nc.scalar.activation(sd[:], rs[:], ACT.Sqrt).then_inc(sd_ready, 1)
                act.sem_inc(sq_ready, 2)

                def square(n, b, turn, kind):
                    act.wait_ge(y_ready, n + 3)
                    act.wait_ge(summed, n + 1)
                    nc.scalar.activation(sq[b][:], m.agg[:, bass.ds(n * AGG, D)], ACT.Square).then_inc(sq_ready, 1)
                tiles(act, square)
                act.wait_ge(var_ready, 1)
                nc.scalar.activation(var[:], var[:], ACT.Sqrt).then_inc(bsd_ready, 1)

            @block.tensor
            def _(pe):
                pe.sem_inc(summed, 2)

                def sums(n, b, turn, kind):
                    mask = m.node_mask[:, 1 if kind == "last" else 0, :]
                    pe.wait_ge(sq_ready, n + 3)
                    nc.tensor.matmul(psS[0][:], mask, m.agg[:, bass.ds(n * AGG, D)], start=(kind == "first"), stop=(kind == "last"), skip_group_check=True)
                    nc.tensor.matmul(psS[1][:], mask, sq[b][:], start=(kind == "first"), stop=(kind == "last"), skip_group_check=True).then_inc(summed, 1)
                tiles(pe, sums)

            @block.vector
            def _(dve):
                v = nc.vector
                ch = Chain(dve, step)
                ych = Chain(dve, y_step, PER)
                dve.sem_inc(y_ready, 2)
                v.tensor_scalar(rs[:], mvv[:, :, 1], EPS, None, ALU.add).then_inc(eps_ready, 1)
                dve.wait_ge(sd_ready, 1)
                ch.link(v.reciprocal(rs[:], sd[:]))
                dve.wait_ge(w_ready, 64)

                def norm_tile(n, b, turn, kind):
                    ych.turn(n)
                    y = m.agg[:, bass.ds(n * AGG, D)]
                    ych.link(v.tensor_scalar(y, y, mvv[:, bass.ds(n, 1), 0], None, ALU.subtract))
                    ych.link(v.scalar_tensor_tensor(out=y, in0=y, scalar=rs[:, bass.ds(n, 1)], in1=par[:, 0, :], op0=ALU.mult, op1=ALU.mult))
                    ych.link(v.tensor_tensor(y, y, par[:, 1, :], ALU.add))
                    dve.wait_ge(in_ready[b], turn * 16 + 16)
                    v.tensor_tensor(y, y, h[b][:], ALU.add).then_inc(y_ready, 1)
                    ych.close()
                tiles(dve, norm_tile)
                dve.wait_ge(summed, NT + 2)
                ch.do(v.tensor_scalar(mean[:], psS[0][:], 1.0 / N_NODES, None, ALU.mult))
                ch.link(v.tensor_scalar(var[:], psS[1][:], 1.0 / N_NODES, None, ALU.mult))
                ch.link(v.tensor_tensor(bn[:, 0, :], mean[:], mean[:], ALU.mult))
                ch.link(v.tensor_tensor(var[:], var[:], bn[:, 0, :], ALU.subtract))
                v.tensor_scalar(var[:], var[:], 0.0, EPS, ALU.max, ALU.add).then_inc(var_ready, 1)
                dve.wait_ge(bsd_ready, 1)
                ch.link(v.reciprocal(var[:], var[:]))
                ch.link(v.tensor_tensor(bn[:, 0, :], var[:], par[:, 2, :], ALU.mult))
                ch.link(v.tensor_tensor(mean[:], mean[:], bn[:, 0, :], ALU.mult))
                ch.link(v.tensor_tensor(bn[:, 1, :], par[:, 3, :], mean[:], ALU.subtract))


def phase_apply(nc, m, d, l, bn, sem):
    in_ready = [sem(f"x_loaded{b}") for b in range(2)]
    step = sem("apply_step")
    y_done = sem("y_done")
    stored = [sem(f"h_stored{b}") for b in range(2)]
    eps_ready = sem("var_eps")
    sd_ready = sem("deviation")
    held = sem("held")
    PER = 2 if l == 1 else 7
    with ExitStack() as ctx:
        sb, ps = buf_maker(nc, ctx, f"ap{l}")
        x = [sb(f"x{b}", [P, D]) for b in range(2)]
        y = [sb(f"y{b}", [P, D]) for b in range(2)]
        st = sb("st", [P, 6])
        mv = sb("mv", [P, 2])
        sd = sb("sd", [P, 2])
        with nc.Block() as block:
            @block.sync
            def _(sp):
                for b in range(2):
                    sp.sem_inc(stored[b], 16)

                def load(n, b, turn):
                    if l == 2:
                        sp.wait_ge(y_done, n + 1)
                        sp.dma_start(x[b][:], tile_of(d.x, n)).then_inc(in_ready[b], 16)

                def store(n, b, turn):
                    sp.wait_ge(y_done, n + 3)
                    sp.dma_start(tile_of(d.h, n), y[b][:]).then_inc(stored[b], 16)
                load_and_store(sp, load, store)
                for b in range(2):
                    sp.wait_ge(stored[b], 16 * (NT // 2 + 1))

            @block.scalar
            def _(act):
                if l == 2:
                    with act.Fori(0, NT) as n:
                        act.wait_ge(eps_ready, n + 1)
                        nc.scalar.activation(sd[:, 1:2], sd[:, 0:1], ACT.Sqrt).then_inc(sd_ready, 1)

            @block.vector
            def _(dve):
                v = nc.vector
                ch = Chain(dve, step, PER)
                dve.sem_inc(y_done, 2)
                with dve.Fori(0, NT // 2) as it:
                    for b in range(2):
                        n = it * 2 + b
                        ch.turn(n)
                        dve.wait_ge(stored[b], it * 16 + 16)
                        ch.link(v.tensor_tensor(y[b][:], m.agg[:, bass.ds(n * AGG, D)], bn[:, 0, :], ALU.mult))
                        ch.link(v.tensor_tensor(y[b][:], y[b][:], bn[:, 1, :], ALU.add))
                        if l == 1:
                            v.tensor_scalar(y[b][:], y[b][:], 0.0, None, ALU.max).then_inc(y_done, 1)
                            ch.close()
                            continue
                        dve.wait_ge(in_ready[b], it * 16 + 16)
                        ch.link(v.tensor_tensor(y[b][:], y[b][:], x[b][:], ALU.add))
                        ch.link(v.scalar_tensor_tensor(out=y[b][:], in0=y[b][:], scalar=0.0, in1=x[b][:], op0=ALU.max, op1=ALU.add))
                        layer_norm(v, dve, ch, y[b], st, mv, sd, eps_ready, sd_ready, y_done, held, n)
                        ch.close()


def layer_norm(v, dve, ch, y, st, mv, sd, eps_ready, sd_ready, done, held, n):
    ch.link(v.bn_stats(st[:], y[:]))
    dve.sem_inc(held, 1)
    ch.link(v.bn_aggr(mv[:], st[:]))
    v.tensor_scalar(sd[:, 0:1], mv[:, 1:2], EPS, None, ALU.add).then_inc(eps_ready, 1)
    dve.wait_ge(sd_ready, n + 1)
    ch.link(v.reciprocal(sd[:, 1:2], sd[:, 1:2]))
    v.tensor_scalar(y[:], y[:], mv[:, 0:1], sd[:, 1:2], ALU.subtract, ALU.mult).then_inc(done, 1)


def phase_conv_weights(nc, m, w, sem):
    loaded = sem("weights_loaded")
    ready = sem("joined")
    step = sem("copied")
    with ExitStack() as ctx:
        sb, ps = buf_maker(nc, ctx, "cw")
        wn = sb("wn", [FILT, D])
        l1T = sb("l1T", [FILT, FILT])
        l2 = sb("l2", [FILT, FILT])
        b2 = sb("b2", [FILT, 1])
        wmT = sb("wmT", [FILT, D])
        psI = ps("psI", [P, 2, FILT])
        psO = ps("psO", [FILT, D])
        psB = ps("psB", [1, D])
        with nc.Block() as block:
            @block.sync
            def _(sp):
                sp.dma_start(wn[:], w["c_W_node_to_message"]).then_inc(loaded, 16)
                sp.dma_start(l1T[:], w["c_W_lin1_T"]).then_inc(loaded, 16)
                sp.dma_start(l2[:], w["c_W_lin2"]).then_inc(loaded, 16)
                sp.dma_start(b2[:], w["c_b_lin2"].rearrange("(k o) -> k o", o=1)).then_inc(loaded, 16)
                sp.dma_start(wmT[:], w["c_W_message_to_node_T"]).then_inc(loaded, 16)
                sp.dma_start(m.w_radial[:], w["c_W_radial_to_message_T"]).then_inc(loaded, 16)

            @block.tensor
            def _(pe):
                pe.wait_ge(loaded, 6 * 16)
                for k in range(2):
                    nc.tensor.matmul(psI[:, k, :], wn[:, k * P:(k + 1) * P], l1T[:], start=True, stop=True)
                nc.tensor.matmul(psB[:], b2[:], wmT[:], start=True, stop=True)
                nc.tensor.matmul(psO[:], l2[:], wmT[:], start=True, stop=True).then_inc(ready, 1)

            @block.vector
            def _(dve):
                ch = Chain(dve, step)
                dve.wait_ge(ready, 1)
                ch.do(nc.vector.tensor_copy(m.w_conv_in[:], psI[:]))
                ch.do(nc.vector.tensor_copy(m.w_conv_out[:], psO[:]))
                ch.do(nc.vector.tensor_copy(m.b_conv_out[:], psB[:]))
                dve.wait_ge(loaded, 6 * 16)
                ch.wait()


def phase_cutoff(nc, m, sem):
    step = sem("cut_step")
    arg_ready = sem("argument")
    sin_ready = sem("sine")
    turn = 2.0 * np.pi
    with ExitStack() as ctx:
        sb, _ = buf_maker(nc, ctx, "cut")
        u = sb("u", [P, S])
        r = sb("r", [P, S])
        whole = sb("whole", [P, S], I32)
        with nc.Block() as block:
            @block.vector
            def _(dve):
                ch = Chain(dve, step)
                v = nc.vector
                ch.do(v.memset(m.cut[:, S:S + GROUP], 0.0))
                ch.link(v.tensor_scalar(u[:], m.w_slot[:, 0:S], 0.5 / CUTOFF, None, ALU.mult))
                ch.link(v.tensor_copy(whole[:], u[:]))
                ch.link(v.tensor_copy(r[:], whole[:]))
                ch.link(v.tensor_tensor(r[:], u[:], r[:], ALU.subtract))
                ch.link(v.scalar_tensor_tensor(out=u[:], in0=r[:], scalar=-1.0, in1=r[:], op0=ALU.mult, op1=ALU.max))
                ch.link(v.tensor_scalar(r[:], u[:], -1.0, 1.0, ALU.mult, ALU.add))
                ch.link(v.tensor_tensor(r[:], u[:], r[:], ALU.min))
                v.tensor_scalar(u[:], r[:], -turn, turn / 4, ALU.mult, ALU.add).then_inc(arg_ready, 1)
                dve.wait_ge(sin_ready, 1)
                ch.link(v.tensor_scalar(m.cut[:, 0:S], r[:], 0.5, 0.5, ALU.mult, ALU.add))

            @block.scalar
            def _(act):
                act.wait_ge(arg_ready, 1)
                nc.scalar.activation(r[:], u[:], ACT.Sin).then_inc(sin_ready, 1)


def phase_conv_table(nc, m, d, sem):
    in_ready = [sem(f"h_loaded{b}") for b in range(2)]
    t_ready = sem("hT_ready")
    t_copied = sem("hT_copied")
    o_ready = sem("row_ready")
    o_copied = sem("row_copied")
    stored = [sem(f"row_stored{b}") for b in range(2)]
    with ExitStack() as ctx:
        sb, ps = buf_maker(nc, ctx, "ct")
        h = [sb(f"h{b}", [P, D]) for b in range(2)]
        hT = [sb(f"hT{b}", [P, 2, P]) for b in range(2)]
        row = [sb(f"row{b}", [P, FILT]) for b in range(2)]
        psT = [ps(f"psT{b}", [P, 2, P]) for b in range(2)]
        psO = [ps(f"psO{b}", [P, FILT]) for b in range(2)]
        with nc.Block() as block:
            @block.sync
            def _(sp):
                for b in range(2):
                    sp.sem_inc(stored[b], 16)

                def load(n, b, turn):
                    sp.wait_ge(t_ready, n + 1)
                    sp.dma_start(h[b][:], tile_of(d.h, n)).then_inc(in_ready[b], 16)

                def store(n, b, turn):
                    sp.wait_ge(o_copied, n + 3)
                    sp.dma_start(d.conv_table[bass.ds(n * P, P), :], row[b][:]).then_inc(stored[b], 16)
                load_and_store(sp, load, store)
                for b in range(2):
                    sp.wait_ge(stored[b], 16 * (NT // 2 + 1))

            @block.tensor
            def _(pe):
                pe.sem_inc(t_ready, 2)
                with pe.Fori(0, NT // 2) as it:
                    for b in range(2):
                        n = it * 2 + b
                        pe.wait_ge(in_ready[b], it * 16 + 16)
                        pe.wait_ge(t_copied, n + 1)
                        for k in range(2):
                            ins = nc.tensor.transpose(psT[b][:, k, :], h[b][:, k * P:(k + 1) * P], m.ident[:])
                        ins.then_inc(t_ready, 1)
                        pe.wait_ge(t_copied, n + 3)
                        pe.wait_ge(o_copied, n + 1)
                        for k in range(2):
                            ins = nc.tensor.matmul(psO[b][:], hT[b][:, k, :], m.w_conv_in[:, k, :], start=(k == 0), stop=(k == 1))
                        ins.then_inc(o_ready, 1)

            @block.scalar
            def _(act):
                act.sem_inc(t_copied, 2)
                with act.Fori(0, NT // 2) as it:
                    for b in range(2):
                        n = it * 2 + b
                        act.wait_ge(t_ready, n + 3)
                        act.wait_ge(o_copied, n + 1)
                        nc.scalar.copy(hT[b][:], psT[b][:]).then_inc(t_copied, 1)

            @block.vector
            def _(dve):
                dve.sem_inc(o_copied, 2)
                with dve.Fori(0, NT // 2) as it:
                    for b in range(2):
                        n = it * 2 + b
                        dve.wait_ge(o_ready, n + 1)
                        dve.wait_ge(stored[b], it * 16 + 16)
                        nc.vector.tensor_copy(row[b][:], psO[b][:]).then_inc(o_copied, 1)


def phase_sum_messages(nc, m, d, kind, table, slot_rows, sem):
    K = FILT if kind == "conv" else D + 1
    WIDE = FILT if kind == "conv" else D
    BANKS = 4
    x_ready = [sem(f"rows_gathered{b}") for b in range(SETS)]
    idx_ready = sem("index_ready")
    idx_pass = sem("index_pass")
    hot_ready = sem("onehot_ready")
    attr_ready = [sem(f"attr_loaded{b}") for b in range(2)]
    f_ready = sem("filters_ready")
    prod_ready = sem("products")
    msg_ready = sem("messages")
    o_ready = sem("slot_sums")
    acc_done = sem("added")
    zeroed = sem("zeroed")
    acc_zeroed = sem("tables_zeroed")
    NTURN = NG // SETS
    with ExitStack() as ctx:
        sb, ps = buf_maker(nc, ctx, kind)
        x = [sb(f"x{b}", [P, GROUP, K]) for b in range(SETS)]
        idx = [sb(f"idx{b}", [P, GROUP], I32) for b in range(SETS)]
        hot = [sb(f"hot{b}", [P, GROUP, P]) for b in range(2)]
        psO = [ps(f"psO{b}", [P, 512]) for b in range(BANKS)]
        if kind == "conv":
            attr = [sb(f"attr{b}", [RADIAL, GROUP, P]) for b in range(2)]
            prod = sb("prod", [P, GROUP, K])
            msg = [sb(f"msg{b}", [P, GROUP, K]) for b in range(2)]
            psF = [ps(f"psF{b}", [P, GROUP, K]) for b in range(2)]
        with nc.Block() as block:
            @block.gpsimd
            def _(pool):
                def gather(g, b, reused):
                    if reused and kind == "conv":
                        pool.wait_ge(prod_ready, g - SETS + 3)
                    elif reused:
                        pool.wait_ge(o_ready, (g - SETS + 1) * GROUP)
                    else:
                        pool.wait_ge(zeroed, 2)
                    nc.gpsimd.tensor_copy(idx[b][:], slot_rows[:, bass.ds(g * GROUP, GROUP)]).then_inc(idx_ready, 1)
                    pool.wait_ge(idx_ready, g + 1)
                    pool.sem_inc(idx_pass, 1)
                    for j in range(GROUP):
                        pool.indirect_dma_start(x[b][:, j, 0:WIDE], None, table,
                                                bass.IndirectOffsetOnAxis(ap=idx[b][:, j:j + 1], axis=0)).then_inc(x_ready[b], 16)
                for b in range(SETS):
                    gather(b, b, False)
                with pool.Fori(1, NTURN) as it:
                    for b in range(SETS):
                        gather(it * SETS + b, b, True)
                gather(NG, 0, True)
                pool.wait_ge(x_ready[0], 16 * GROUP * (NTURN + 1))

            if kind == "conv":
                @block.sync
                def _(sp):
                    regs = [sp.alloc_register(f"sp_t_{j}") for j in range(GROUP)]

                    def load_attr(g, b, pair):
                        sp.load(regs, m.trow[0:1, bass.ds(g * GROUP, GROUP)])
                        ts = [sp.snap(r, min_val=0, max_val=TP - 1) for r in regs]
                        sp.wait_ge(f_ready, g + 1)
                        for j in range(GROUP):
                            sp.dma_start(attr[b][:, j, :], d.attr12_T[:, bass.ds(ts[j] * P, P)]).then_inc(attr_ready[b], 16)
                    with sp.Fori(0, NG // 2) as it:
                        for b in range(2):
                            load_attr(it * 2 + b, b, it)
                    load_attr(NG, 0, NG // 2)

            else:
                @block.sync
                def _(sp):
                    for k in range(K_ACC):
                        sp.dma_start(d.acc[k].rearrange("(c p) k -> p c k", p=P), m.zeros[:].unsqueeze(1).to_broadcast([P, NT + 1, D + 1])).then_inc(acc_zeroed, 16)
                    sp.wait_ge(acc_zeroed, 16 * K_ACC)

            @block.tensor
            def _(pe):
                if kind == "conv":
                    pe.sem_inc(f_ready, 2)

                def filters(g, b, turn):
                    pair = turn * 2 + b // 2
                    pe.wait_ge(attr_ready[b % 2], pair * (16 * GROUP) + 16 * GROUP)
                    pe.wait_ge(prod_ready, g + 1)
                    for j in range(GROUP):
                        ins = nc.tensor.matmul(psF[b % 2][:, j, :], attr[b % 2][:, j, :], m.w_radial[:], start=True, stop=True)
                    ins.then_inc(f_ready, 1)

                def sums(g, b, turn, j):
                    i = g * GROUP + j
                    if j == 0:
                        pe.wait_ge(hot_ready, g + 1)
                        if kind == "conv":
                            pe.wait_ge(msg_ready, g + 1)
                        else:
                            pe.wait_ge(x_ready[b], turn * (16 * GROUP) + 16 * GROUP)
                    pe.wait_ge(acc_done, i + 1)
                    rhs = msg[b % 2] if kind == "conv" else x[b]
                    nc.tensor.matmul(psO[j % BANKS][:, 0:K], hot[b % 2][:, j, :], rhs[:, j, :], start=True, stop=True).then_inc(o_ready, 1)
                if kind == "conv":
                    filters(0, 0, 0)
                with pe.Fori(0, NTURN) as it:
                    for b in range(SETS):
                        b1 = (b + 1) % SETS
                        if kind == "conv":
                            filters(it * SETS + b + 1, b1, it + 1 if b1 == 0 else it)
                        for j in range(GROUP):
                            sums(it * SETS + b, b, it, j)
                pe.wait_ge(o_ready, S)

            @block.vector
            def _(dve):
                regs = [dve.alloc_register(f"dve_{kind}_{j}") for j in range(GROUP)]
                nc.vector.memset(m.sums[:], 0.0).then_inc(zeroed, 1)
                if kind == "rel":
                    for b in range(SETS - 1):
                        nc.vector.memset(x[b][:, :, D:D + 1], 1.0)
                    nc.vector.memset(x[SETS - 1][:, :, D:D + 1], 1.0).then_inc(zeroed, 1)
                else:
                    dve.sem_inc(zeroed, 1)
                    dve.sem_inc(prod_ready, 2)
                dve.sem_inc(acc_done, BANKS)
                dve.wait_ge(zeroed, 2)

                def onehots(g, b):
                    at = bass.ds(g * GROUP, GROUP)
                    nc.vector.tensor_tensor(hot[b % 2][:], m.iota[:, 0:P].unsqueeze(1).to_broadcast([P, GROUP, P]),
                                            m.loc[:, at].unsqueeze(2).to_broadcast([P, GROUP, P]), ALU.is_equal).then_inc(hot_ready, 1)

                def messages(g, b, turn):
                    at = bass.ds(g * GROUP, GROUP)
                    dve.wait_ge(x_ready[b], turn * (16 * GROUP) + 16 * GROUP)
                    dve.wait_ge(f_ready, g + 3)
                    nc.vector.tensor_tensor(prod[:], psF[b % 2][:], x[b][:], ALU.mult).then_inc(prod_ready, 1)
                    dve.wait_ge(prod_ready, g + 3)
                    nc.vector.tensor_tensor(msg[b % 2][:], prod[:], m.cut[:, at].unsqueeze(2).to_broadcast([P, GROUP, K]), ALU.mult).then_inc(msg_ready, 1)
                    dve.wait_ge(msg_ready, g + 1)

                def add(g, b, j, ns):
                    i = g * GROUP + j
                    dve.wait_ge(o_ready, i + 1)
                    dve.wait_ge(acc_done, i + BANKS)
                    to = m.sums[:, bass.ds(ns[j] * K, K)]
                    nc.vector.tensor_tensor(to, to, psO[j % BANKS][:, 0:K], ALU.add).then_inc(acc_done, 1)
                onehots(0, 0)
                if kind == "conv":
                    messages(0, 0, 0)
                with dve.Fori(0, NTURN) as it:
                    for b in range(SETS):
                        g = it * SETS + b
                        b1 = (b + 1) % SETS
                        dve.load(regs, m.nrow[0:1, bass.ds(g * GROUP, GROUP)])
                        ns = [dve.snap(r, min_val=0, max_val=NT - 1) for r in regs]
                        onehots(g + 1, b1)
                        for j in range(GROUP // 2):
                            add(g, b, j, ns)
                        if kind == "conv":
                            messages(g + 1, b1, it + 1 if b1 == 0 else it)
                        for j in range(GROUP // 2, GROUP):
                            add(g, b, j, ns)
                dve.wait_ge(acc_done, S + BANKS)


def phase_conv_out(nc, m, d, sem):
    in_ready = [sem(f"x_loaded{b}") for b in range(2)]
    a_ready = sem("sums_copied")
    t_ready = sem("sumsT_ready")
    t_copied = sem("sumsT_copied")
    o_ready = sem("out_ready")
    taken = sem("out_taken")
    y_done = sem("y_done")
    step = sem("norm_step")
    stored = [sem(f"h_stored{b}") for b in range(2)]
    eps_ready = sem("var_eps")
    sd_ready = sem("deviation")
    held = sem("held")
    PER = 3
    with ExitStack() as ctx:
        sb, ps = buf_maker(nc, ctx, "co")
        x = [sb(f"x{b}", [P, D]) for b in range(2)]
        y = [sb(f"y{b}", [P, D]) for b in range(2)]
        a = [sb(f"a{b}", [P, FILT]) for b in range(2)]
        aT = [sb(f"aT{b}", [FILT, P]) for b in range(2)]
        st = sb("st", [P, 6])
        mv = sb("mv", [P, 2])
        sd = sb("sd", [P, 2])
        psT = [ps(f"psT{b}", [FILT, P]) for b in range(2)]
        psO = [ps(f"psO{b}", [P, D]) for b in range(2)]
        with nc.Block() as block:
            @block.sync
            def _(sp):
                for b in range(2):
                    sp.sem_inc(stored[b], 16)

                def load(n, b, turn):
                    sp.wait_ge(y_done, n + 1)
                    sp.dma_start(x[b][:], tile_of(d.h, n)).then_inc(in_ready[b], 16)

                def store(n, b, turn):
                    sp.wait_ge(y_done, n + 3)
                    sp.dma_start(tile_of(d.h2, n), y[b][:]).then_inc(stored[b], 16)
                load_and_store(sp, load, store)
                for b in range(2):
                    sp.wait_ge(stored[b], 16 * (NT // 2 + 1))

            @block.tensor
            def _(pe):
                pe.sem_inc(t_ready, 2)
                pe.sem_inc(o_ready, 2)
                with pe.Fori(0, NT // 2) as it:
                    for b in range(2):
                        n = it * 2 + b
                        pe.wait_ge(a_ready, n + 1)
                        pe.wait_ge(t_copied, n + 1)
                        nc.tensor.matmul(psT[b][:], a[b][:], m.ident[:], start=True, stop=True).then_inc(t_ready, 1)
                        pe.wait_ge(t_copied, n + 3)
                        pe.wait_ge(taken, n + 1)
                        nc.tensor.matmul(psO[b][:], m.ones[0:1, :], m.b_conv_out[:], start=True, stop=False)
                        nc.tensor.matmul(psO[b][:], aT[b][:], m.w_conv_out[:], start=False, stop=True).then_inc(o_ready, 1)

            @block.scalar
            def _(act):
                act.sem_inc(t_copied, 2)

                def copies(n, b):
                    act.wait_ge(t_ready, n + 1)
                    nc.scalar.copy(a[b][:], m.sums[:, bass.ds(n * FILT, FILT)]).then_inc(a_ready, 1)
                    act.wait_ge(t_ready, n + 3)
                    act.wait_ge(o_ready, n + 1)
                    nc.scalar.copy(aT[b][:], psT[b][:]).then_inc(t_copied, 1)

                def root(n):
                    act.wait_ge(eps_ready, n + 1)
                    nc.scalar.activation(sd[:, 1:2], sd[:, 0:1], ACT.Sqrt).then_inc(sd_ready, 1)
                copies(0, 0)
                with act.Fori(0, NT // 2 - 1) as it:
                    copies(it * 2 + 1, 1)
                    root(it * 2)
                    copies(it * 2 + 2, 0)
                    root(it * 2 + 1)
                copies(NT - 1, 1)
                root(NT - 2)
                root(NT - 1)

            @block.vector
            def _(dve):
                v = nc.vector
                ch = Chain(dve, step, PER)
                dve.sem_inc(taken, 2)
                dve.sem_inc(y_done, 2)
                with dve.Fori(0, NT // 2) as it:
                    for b in range(2):
                        n = it * 2 + b
                        ch.turn(n)
                        dve.wait_ge(o_ready, n + 3)
                        dve.wait_ge(in_ready[b], it * 16 + 16)
                        dve.wait_ge(stored[b], it * 16 + 16)
                        v.tensor_tensor(y[b][:], psO[b][:], x[b][:], ALU.add).then_inc(taken, 1)
                        dve.wait_ge(taken, n + 3)
                        layer_norm(v, dve, ch, y[b], st, mv, sd, eps_ready, sd_ready, y_done, held, n)
                        ch.close()
                dve.wait_ge(y_done, NT + 2)


def phase_rel_tables(nc, m, d, w, sem):
    w_ready = sem("weights_loaded")
    in_ready = [sem(f"h_loaded{b}") for b in range(2)]
    t_ready = sem("hT_ready")
    t_copied = sem("hT_copied")
    o_ready = sem("product_ready")
    o_copied = [sem(f"product_copied{b}") for b in range(2)]
    base_ready = sem("base_ready")
    base_done = sem("base_done")
    stored = [sem(f"rows_stored{b}") for b in range(2)]
    base_stored = [sem(f"base_stored{b}") for b in range(2)]
    PAIRS = N_REL // 2
    with ExitStack() as ctx:
        sb, ps = buf_maker(nc, ctx, "rt")
        wr = sb("wr", [P, 2, N_REL, D])
        ws = sb("ws", [P, 2, D])
        bs = sb("bs", [1, D])
        h = [sb(f"h{b}", [P, D]) for b in range(2)]
        hT = [sb(f"hT{b}", [P, 2, P]) for b in range(2)]
        rows = [sb(f"rows{b}", [P, N_REL, D]) for b in range(2)]
        base = [sb(f"base{b}", [P, D]) for b in range(2)]
        psT = ps("psT", [P, 2, P])
        psB = ps("psB", [P, D])
        psO = [ps(f"psO{q}", [P, 2, D]) for q in range(PAIRS)]
        with nc.Block() as block:
            @block.sync
            def _(sp):
                sp.dma_start(bs[:], w["r_sl_b"].rearrange("(o n) -> o n", o=1)).then_inc(w_ready, 16)
                sp.dma_start(ws[:], w["r_sl_w_T"].rearrange("(k p) n -> p k n", p=P)).then_inc(w_ready, 16)
                for k in range(2):
                    sp.dma_start(wr[:, k, :, :], w["r_weight"][:, k * P:(k + 1) * P, :].rearrange("r p n -> p r n")).then_inc(w_ready, 16)
                for b in range(2):
                    sp.sem_inc(stored[b], 16)
                    sp.sem_inc(base_stored[b], 16)

                def load(n, b, turn):
                    sp.wait_ge(base_done, n + 1)
                    sp.dma_start(h[b][:], tile_of(d.h2, n)).then_inc(in_ready[b], 16)

                def store(n, b, turn):
                    sp.wait_ge(base_done, n + 3)
                    sp.dma_start(tile_of(d.base, n), base[b][:]).then_inc(base_stored[b], 16)
                    for e in range(2):
                        sp.wait_ge(o_copied[e], n * 2 + 4)
                    sp.dma_start(d.rel_table.rearrange("(r n) k -> n r k", r=N_REL)[bass.ds(n * P, P), :, :], rows[b][:]).then_inc(stored[b], 16)
                load_and_store(sp, load, store)
                for b in range(2):
                    sp.wait_ge(stored[b], 16 * (NT // 2 + 1))
                    sp.wait_ge(base_stored[b], 16 * (NT // 2 + 1))

            @block.tensor
            def _(pe):
                pe.wait_ge(w_ready, 4 * 16)
                pe.sem_inc(t_ready, 1)
                pe.sem_inc(o_ready, 1)
                pe.sem_inc(base_ready, 1)
                with pe.Fori(0, NT // 2) as it:
                    for b in range(2):
                        n = it * 2 + b
                        pe.wait_ge(in_ready[b], it * 16 + 16)
                        pe.wait_ge(t_copied, n + 1)
                        for k in range(2):
                            ins = nc.tensor.transpose(psT[:, k, :], h[b][:, k * P:(k + 1) * P], m.ident[:])
                        ins.then_inc(t_ready, 1)
                        pe.wait_ge(t_copied, n + 2)
                        pe.wait_ge(base_done, n + 2)
                        nc.tensor.matmul(psB[:], m.ones[0:1, :], bs[:], start=True, stop=False)
                        for k in range(2):
                            ins = nc.tensor.matmul(psB[:], hT[b][:, k, :], ws[:, k, :], start=False, stop=(k == 1))
                        ins.then_inc(base_ready, 1)
                        for q in range(PAIRS):
                            pe.wait_ge(o_copied[q % 2], n * 2 + q // 2 + 1)
                            for k in range(2):
                                ins = nc.tensor.matmul(psO[q][:].rearrange("p a n -> p (a n)"), hT[b][:, k, :],
                                                       wr[:, k, 2 * q:2 * q + 2, :].rearrange("p a n -> p (a n)"), start=(k == 0), stop=(k == 1))
                            ins.then_inc(o_ready, 1)

            def copy_pair(eng, copy, n, b, turn, q):
                eng.wait_ge(o_ready, n * PAIRS + q + 2)
                copy(rows[b][:, 2 * q:2 * q + 2, :], psO[q][:]).then_inc(o_copied[q % 2], 1)

            @block.scalar
            def _(act):
                act.sem_inc(t_copied, 1)
                act.sem_inc(o_copied[1], 2)
                with act.Fori(0, NT // 2) as it:
                    for b in range(2):
                        n = it * 2 + b
                        act.wait_ge(t_ready, n + 2)
                        act.wait_ge(o_copied[1], n * 2 + 1)
                        nc.scalar.copy(hT[b][:], psT[:]).then_inc(t_copied, 1)
                        act.wait_ge(stored[b], it * 16 + 16)
                        copy_pair(act, nc.scalar.copy, n, b, it, 1)
                        copy_pair(act, nc.scalar.copy, n, b, it, 3)

            @block.vector
            def _(dve):
                dve.sem_inc(base_done, 2)
                dve.sem_inc(o_copied[0], 2)
                with dve.Fori(0, NT // 2) as it:
                    for b in range(2):
                        n = it * 2 + b
                        dve.wait_ge(base_ready, n + 2)
                        dve.wait_ge(base_stored[b], it * 16 + 16)
                        nc.vector.tensor_tensor(base[b][:], psB[:], h[b][:], ALU.add).then_inc(base_done, 1)
                        dve.wait_ge(stored[b], it * 16 + 16)
                        copy_pair(dve, nc.vector.tensor_copy, n, b, it, 0)
                        copy_pair(dve, nc.vector.tensor_copy, n, b, it, 2)


def chunk_of(dram, c):
    return dram[bass.ds(c * CT, CT), :, :].rearrange("t p k -> p t k")


def norm_chunk(v, dve, ch, y, st, mv, sd, eps_ready, sd_ready, done, held, c):
    for t in range(CT):
        ch.do(v.bn_stats(st[:, t, :], y[:, t, :]))
    ch.wait()
    dve.sem_inc(held, 1)
    for t in range(CT):
        ch.do(v.bn_aggr(mv[:, t, :], st[:, t, :]))
    ch.wait()
    v.tensor_scalar(sd[:, 0, :], mv[:, :, 1], EPS, None, ALU.add).then_inc(eps_ready, 1)
    dve.wait_ge(sd_ready, c + 1)
    ch.link(v.reciprocal(sd[:, 1, :], sd[:, 1, :]))
    for t in range(CT):
        ins = v.tensor_scalar(y[:, t, :], y[:, t, :], mv[:, t, 0:1], sd[:, 1, t:t + 1], ALU.subtract, ALU.mult)
    ins.then_inc(done, 1)


def phase_gate(nc, m, d, w, sem):
    w_ready = sem("weights_loaded")
    ws_ready = sem("weights_ready")
    wstep = sem("weight_step")
    step = sem("norm_step")
    in_ready = [sem(f"base_loaded{b}") for b in range(2)]
    added = sem("base_added")
    y_done = sem("x3_ready")
    stored = [sem(f"x3_stored{b}") for b in range(2)]
    eps_ready = sem("var_eps")
    sd_ready = sem("deviation")
    held = sem("held")
    t_ready = sem("x3T_ready")
    t_copied = sem("x3T_copied")
    o_ready = sem("support_ready")
    o_copied = sem("support_copied")
    gate_ready = sem("gate")
    with ExitStack() as ctx:
        sb, ps = buf_maker(nc, ctx, "ga")
        wsup = sb("wsup", [P, 2, D + 1])
        a2 = sb("a2", [P, D])
        wa = sb("wa", [P, 2, D])
        base = [sb(f"base{b}", [P, CT, D]) for b in range(2)]
        y = [sb(f"y{b}", [P, CT, D]) for b in range(2)]
        deg = sb("deg", [P, CT])
        st = sb("st", [P, CT, 6])
        mv = sb("mv", [P, CT, 2])
        sd = sb("sd", [P, 2, CT])
        yT = [sb(f"yT{b}", [P, 2, P]) for b in range(2)]
        gate = sb("gate", [P, NT])
        psT = [ps(f"psT{b}", [P, 2, P]) for b in range(2)]
        psO = [ps(f"psO{b}", [P, 512]) for b in range(2)]
        sums = m.sums[:].rearrange("p (n k) -> p n k", k=D + 1)
        gated = m.gated[:].rearrange("p (n k) -> p n k", k=D + 1)

        order = [(True, 0)] + [x for t in range(1, CT) for x in ((True, t), (False, t - 1))] + [(False, CT - 1)]
        with nc.Block() as block:
            @block.sync
            def _(sp):
                sp.dma_start(wsup[:, :, 0:D], w["s_W"].rearrange("(k p) n -> p k n", p=P)).then_inc(w_ready, 16)
                sp.dma_start(a2[:], w["s_a2"].rearrange("k o -> o k").to_broadcast([P, D])).then_inc(w_ready, 16)
                with sp.Fori(0, NCK // 2) as it:
                    for b in range(2):
                        c = it * 2 + b
                        sp.wait_ge(added, c + 1)
                        sp.dma_start(base[b][:], chunk_of(d.base, c)).then_inc(in_ready[b], 16)

            @block.gpsimd
            def _(pool):
                with pool.Fori(0, NCK // 2) as it:
                    for b in range(2):
                        c = it * 2 + b
                        pool.wait_ge(y_done, c + 1)
                        pool.sem_inc(held, 1)
                        pool.dma_start(chunk_of(d.h, c), y[b][:]).then_inc(stored[b], 16)
                for b in range(2):
                    pool.wait_ge(stored[b], 16 * (NCK // 2))

            @block.tensor
            def _(pe):
                pe.wait_ge(ws_ready, 1)
                pe.sem_inc(t_ready, 2 * CT)
                pe.sem_inc(o_ready, 2)
                with pe.Fori(0, NCK // 2) as it:
                    for b in range(2):
                        c = it * 2 + b
                        pe.wait_ge(y_done, c + 1)
                        for turned, t in order:
                            q = (b * CT + t) % 2
                            n = c * CT + t
                            if turned:
                                pe.wait_ge(t_copied, n + 1)
                                for k in range(2):
                                    ins = nc.tensor.transpose(psT[q][:, k, :], y[b][:, t, k * P:(k + 1) * P], m.ident[:])
                                ins.then_inc(t_ready, 1)
                            else:
                                pe.wait_ge(t_copied, n + 3)
                                pe.wait_ge(o_copied, n + 1)
                                for k in range(2):
                                    ins = nc.tensor.matmul(psO[q][:, 0:D + 1], yT[q][:, k, :], wsup[:, k, :], start=(k == 0), stop=(k == 1))
                                ins.then_inc(o_ready, 1)

            @block.scalar
            def _(act):
                act.sem_inc(t_copied, 2)
                act.sem_inc(o_copied, 2)
                with act.Fori(0, NCK // 2) as it:
                    for b in range(2):
                        c = it * 2 + b
                        act.wait_ge(eps_ready, c + 1)
                        nc.scalar.activation(sd[:, 1, :], sd[:, 0, :], ACT.Sqrt).then_inc(sd_ready, 1)
                        for turned, t in order:
                            q = (b * CT + t) % 2
                            n = c * CT + t
                            if turned:
                                act.wait_ge(t_ready, n + 1 + 2 * CT)
                                act.wait_ge(o_ready, n + 1)
                                nc.scalar.copy(yT[q][:], psT[q][:]).then_inc(t_copied, 1)
                            else:
                                act.wait_ge(o_ready, n + 3)
                                nc.scalar.copy(m.gated[:, bass.ds(n * (D + 1), D + 1)], psO[q][:, 0:D + 1]).then_inc(o_copied, 1)
                act.wait_ge(o_copied, NT + 2)
                nc.scalar.activation(gate[:].unsqueeze(2), gated[:, :, D:D + 1], ACT.Sigmoid).then_inc(gate_ready, 1)

            @block.vector
            def _(dve):
                v = nc.vector
                wch = Chain(dve, wstep)
                dve.sem_inc(added, 2)
                dve.wait_ge(w_ready, 32)
                wch.link(v.tensor_tensor(wa[:], wsup[:, :, 0:D], a2[:].unsqueeze(1).to_broadcast([P, 2, D]), ALU.mult))
                v.tensor_reduce(wsup[:, :, D:D + 1], wa[:], AX_X, ALU.add).then_inc(ws_ready, 1)
                ch = Chain(dve, step, NORM_STEPS + 3)

                def chunk(c, b, turn, reused):
                    ch.turn(c)
                    cs = bass.ds(c * CT, CT)
                    if reused:
                        dve.wait_ge(stored[b], turn * 16)
                    dve.wait_ge(t_ready, c * CT + CT)
                    ch.link(v.tensor_scalar(deg[:].unsqueeze(2), sums[:, cs, D:D + 1], 1.0, None, ALU.max))
                    ch.link(v.reciprocal(deg[:], deg[:]))
                    ch.link(v.tensor_tensor(y[b][:], sums[:, cs, 0:D], deg[:].unsqueeze(2).to_broadcast([P, CT, D]), ALU.mult))
                    dve.wait_ge(in_ready[b], turn * 16 + 16)
                    v.tensor_tensor(y[b][:], y[b][:], base[b][:], ALU.add).then_inc(added, 1)
                    dve.wait_ge(added, c + 3)
                    norm_chunk(v, dve, ch, y[b], st, mv, sd, eps_ready, sd_ready, y_done, held, c)
                    ch.close()
                for b in range(2):
                    chunk(b, b, 0, False)
                with dve.Fori(1, NCK // 2) as it:
                    for b in range(2):
                        chunk(it * 2 + b, b, it, True)
                dve.wait_ge(gate_ready, 1)
                for t in range(0, NT, NT // 2):
                    ts = slice(t, t + NT // 2)
                    wch.do(v.tensor_tensor(gated[:, ts, 0:D], gated[:, ts, 0:D], gate[:, ts].unsqueeze(2).to_broadcast([P, NT // 2, D]), ALU.mult))
                wch.do(v.tensor_copy(gated[:, :, D:D + 1], gate[:].unsqueeze(2)))
                wch.wait()


def phase_scatter(nc, m, d, sem):
    K = D + 1
    HALF = GROUP // 2
    step = sem("prepare_step")
    diag_ready = sem("diagonals")
    s_ready = sem("sources_spread")
    hot_ready = sem("weighted_onehots")
    same_ready = sem("same_source")
    gstep = sem("index_step")
    idx_ready = sem("index_ready")
    b_ready = sem("pickers")
    b_copied = sem("pickers_copied")
    r_ready = sem("rows_ready")
    r_copied = sem("rows_copied")
    passed = sem("scatter_passed")
    bank_free = sem("rows_bank_free")
    idxf_ready = sem("index_value")
    done = [sem(f"scattered{k}") for k in range(K_ACC)]
    NTURN = NG // SETS
    PER = 2
    with ExitStack() as ctx:
        sb, ps = buf_maker(nc, ctx, "sc")
        srcv = sb("srcv", [P, S + GROUP])
        delta = sb("delta", [P, S + GROUP])
        valid = sb("valid", [P, S + GROUP])
        own = sb("own", [P, 2])
        later = sb("later", [P, P])
        diag = sb("diag", [P, GROUP, P])
        hot = sb("hot", [P, GROUP, P])
        same = sb("same", [P, GROUP, P])
        low = sb("low", [P, GROUP, P])
        count = sb("count", [P, GROUP])
        idxf = sb("idxf", [P, GROUP])
        idx = [sb(f"idx{b}", [P, GROUP], I32) for b in range(SETS)]
        pick = [sb(f"pick{b}", [P, GROUP, P]) for b in range(2)]
        rows = [sb(f"rows{b}", [P, GROUP, K]) for b in range(2)]
        psS = [ps(f"psS{h}", [P, HALF, P]) for h in range(2)]
        psB = [ps(f"psB{h}", [P, HALF, P]) for h in range(2)]
        psR = [ps(f"psR{q}", [P, 512]) for q in range(4)]
        with nc.Block() as block:
            @block.gpsimd
            def _(pool):
                def scatter(g, b, first):
                    pool.wait_ge(idx_ready, g + 1)
                    for j in range(GROUP):
                        i = g * GROUP + j
                        k = j % K_ACC
                        pool.wait_ge(r_copied, i + 1)
                        if not (first and j < K_ACC):
                            pool.wait_ge(done[k], (g * (GROUP // K_ACC) + j // K_ACC) * 16)
                        pool.sem_inc(passed, 1)
                        pool.indirect_dma_start(d.acc[k][0:NR + P, :], bass.IndirectOffsetOnAxis(ap=idx[b][:, j:j + 1], axis=0),
                                                rows[b % 2][:, j, :], None, compute_op=ALU.add).then_inc(done[k], 16)
                for b in range(SETS):
                    scatter(b, b, b == 0)
                with pool.Fori(1, NTURN) as it:
                    for b in range(SETS):
                        scatter(it * SETS + b, b, False)
                for k in range(K_ACC):
                    pool.wait_ge(done[k], 16 * (S // K_ACC))

            @block.tensor
            def _(pe):
                regs = [pe.alloc_register(f"pe_sc_{j}") for j in range(GROUP)]
                pe.sem_inc(b_ready, 2)
                pe.sem_inc(s_ready, 1)

                def spread(g):
                    pe.wait_ge(diag_ready, g + 1)
                    pe.wait_ge(same_ready, g + 1)
                    for h in range(2):
                        ins = nc.tensor.matmul(psS[h][:].rearrange("p j e -> p (j e)"), m.ones[:], diag[:, h * HALF:(h + 1) * HALF, :].rearrange("p j e -> p (j e)"), start=True, stop=True)
                    ins.then_inc(s_ready, 1)

                def pickers(g, h):
                    if h == 0:
                        pe.wait_ge(hot_ready, g + 1)
                        pe.wait_ge(same_ready, g + 2)
                    pe.wait_ge(b_copied, g * 2 + h + 1)
                    for j in range(h * HALF, (h + 1) * HALF):
                        ins = nc.tensor.matmul(psB[h][:, j - h * HALF, :], hot[:, j, :], same[:, j, :], start=True, stop=True)
                    ins.then_inc(b_ready, 1)

                def row(g, b, j, ns):
                    i = g * GROUP + j
                    if j % HALF == 0:
                        pe.wait_ge(b_copied, g * 2 + j // HALF + 3)
                    pe.wait_ge(bank_free, i + 1)
                    nc.tensor.matmul(psR[j % 4][:, 0:K], pick[b % 2][:, j, :], m.gated[:, bass.ds(ns[j] * K, K)], start=True, stop=True).then_inc(r_ready, 1)
                spread(0)
                pickers(0, 0)
                pickers(0, 1)
                with pe.Fori(0, NTURN) as it:
                    for b in range(SETS):
                        g = it * SETS + b
                        pe.load(regs, m.nrow[0:1, bass.ds(g * GROUP, GROUP)])
                        ns = [pe.snap(r, min_val=0, max_val=NT - 1) for r in regs]
                        spread(g + 1)
                        for j in range(4):
                            row(g, b, j, ns)
                        pickers(g + 1, 0)
                        row(g, b, 4, ns)
                        row(g, b, 5, ns)
                        pickers(g + 1, 1)
                        row(g, b, 6, ns)
                        row(g, b, 7, ns)

            @block.scalar
            def _(act):
                act.sem_inc(b_copied, 2)
                act.sem_inc(passed, 2 * GROUP)
                act.sem_inc(bank_free, 4)

                def copy_pick(g, b, h):
                    act.wait_ge(b_ready, g * 2 + h + 3)
                    nc.scalar.copy(pick[b % 2][:, h * HALF:(h + 1) * HALF, :], psB[h][:]).then_inc(b_copied, 1)

                def copy_row(g, b, j):
                    i = g * GROUP + j
                    act.wait_ge(r_ready, i + 1)
                    act.wait_ge(passed, i + K_ACC + 1)
                    nc.scalar.copy(rows[b % 2][:, j, :], psR[j % 4][:, 0:K]).then_inc(r_copied, 1)
                    act.wait_ge(r_copied, i + 1)
                    act.sem_inc(bank_free, 1)
                for h in range(2):
                    copy_pick(0, 0, h)
                with act.Fori(0, NTURN) as it:
                    for b in range(SETS):
                        g = it * SETS + b
                        b1 = (b + 1) % SETS
                        for j in range(4):
                            copy_row(g, b, j)
                        copy_pick(g + 1, b1, 0)
                        copy_row(g, b, 4)
                        copy_row(g, b, 5)
                        copy_pick(g + 1, b1, 1)
                        copy_row(g, b, 6)
                        copy_row(g, b, 7)

            @block.vector
            def _(dve):
                v = nc.vector
                ch = Chain(dve, step)
                gch = Chain(dve, gstep, PER)
                ch.do(v.tensor_scalar(own[:, 0:1], m.pidx[:], -1.0, -1.0, ALU.mult, ALU.add))
                ch.do(v.tensor_scalar(own[:, 1:2], m.pidx[:], float(NR), None, ALU.add))
                ch.do(v.tensor_scalar(later[:], m.iota[:, 0:P], m.pidx[:, 0:1], None, ALU.is_lt))
                ch.do(v.tensor_scalar(valid[:], m.loc[:], 0.0, None, ALU.is_ge))
                ch.do(v.tensor_scalar(delta[:], m.loc[:], float(P), None, ALU.is_lt))
                ch.do(v.tensor_copy(srcv[:], m.src_slot[:]))
                ch.wait()
                ch.link(v.tensor_tensor(valid[:], valid[:], delta[:], ALU.mult))
                ch.link(v.tensor_scalar(delta[:], srcv[:], own[:, 1:2], None, ALU.subtract))
                ch.do(v.tensor_tensor(delta[:], delta[:], valid[:], ALU.mult))
                ch.link(v.tensor_scalar(srcv[:], srcv[:], own[:, 0:1], None, ALU.subtract))
                ch.link(v.tensor_tensor(srcv[:], srcv[:], valid[:], ALU.mult))
                ch.link(v.tensor_scalar(srcv[:], srcv[:], own[:, 0:1], None, ALU.add))
                dve.sem_inc(same_ready, 1)
                dve.sem_inc(gstep, PER)

                def prepare(g, b):
                    gch.turn(g + 1)
                    gs = bass.ds(g * GROUP, GROUP)
                    src = srcv[:, gs]
                    dve.wait_ge(s_ready, g + 1)
                    v.tensor_tensor(diag[:], m.ident[:].unsqueeze(1).to_broadcast([P, GROUP, P]), src.unsqueeze(2).to_broadcast([P, GROUP, P]), ALU.mult).then_inc(diag_ready, 1)
                    dve.wait_ge(b_ready, g * 2 + 2)
                    for j in range(GROUP):
                        i = g * GROUP + j
                        ins = v.tensor_scalar(hot[:, j, :], m.iota[:, 0:P], m.loc[:, bass.ds(i, 1)], m.w_slot[:, bass.ds(i, 1)], ALU.is_equal, ALU.mult)
                    ins.then_inc(hot_ready, 1)
                    dve.wait_ge(s_ready, g + 2)
                    dve.wait_ge(gstep, g * PER + PER)
                    for h in range(2):
                        hs = slice(h * HALF, (h + 1) * HALF)
                        ins = v.tensor_tensor(same[:, hs, :], psS[h][:], srcv[:, bass.ds(g * GROUP + h * HALF, HALF)].unsqueeze(2).to_broadcast([P, HALF, P]), ALU.is_equal)
                    ins.then_inc(same_ready, 1)
                    dve.wait_ge(same_ready, g + 2)
                    gch.link(v.tensor_tensor(low[:], same[:], later[:].unsqueeze(1).to_broadcast([P, GROUP, P]), ALU.mult))
                    gch.link(v.tensor_reduce(count[:], low[:], AX_X, ALU.add))
                    dve.wait_ge(passed, g * GROUP)
                    v.scalar_tensor_tensor(out=idxf[:], in0=count[:], scalar=0.0, in1=delta[:, gs], op0=ALU.is_equal, op1=ALU.mult).then_inc(idxf_ready, 1)
                    dve.wait_ge(idxf_ready, g + 1)
                    v.tensor_scalar(idx[b][:], idxf[:], own[:, 1:2], None, ALU.add).then_inc(idx_ready, 1)
                    gch.close()
                prepare(0, 0)
                with dve.Fori(0, NTURN) as it:
                    for b in range(SETS):
                        prepare(it * SETS + b + 1, (b + 1) % SETS)


def phase_last(nc, m, d, w, out, sem):
    K = D + 1
    a_ready = sem("a1_loaded")
    t_ready = [sem(f"tables_loaded{b}") for b in range(2)]
    added = sem("tables_added")
    step = sem("sum_step")
    nstep = sem("norm_step")
    abs_ready = sem("abs")
    exp_ready = sem("exp")
    log_arg = sem("one_plus_exp")
    log_ready = sem("log")
    soft_step = sem("softplus_step")
    x_ready = [sem(f"x3_loaded{b}") for b in range(2)]
    neg_ready = sem("negative_part")
    elu_ready = sem("elu")
    y_done = sem("out_ready")
    stored = [sem(f"out_stored{b}") for b in range(2)]
    eps_ready = sem("var_eps")
    sd_ready = sem("deviation")
    held = sem("held")
    with ExitStack() as ctx:
        sb, _ = buf_maker(nc, ctx, "la")
        a1 = sb("a1", [P, D])
        o = sb("o", [P, NT, D])
        t = [sb(f"t{b}", [P, K_ACC, CT, K]) for b in range(2)]
        norm = sb("norm", [P, CT])
        no_node = sb("no_node", [P, NT])
        prod = sb("prod", [P, CT, D])
        z = sb("z", [P, NT])
        e = sb("e", [P, NT])
        x = [sb(f"x{b}", [P, CT, D]) for b in range(2)]
        y = [sb(f"y{b}", [P, CT, D]) for b in range(2)]
        st = sb("st", [P, CT, 6])
        mv = sb("mv", [P, CT, 2])
        sd = sb("sd", [P, 2, CT])
        with nc.Block() as block:
            @block.sync
            def _(sp):
                sp.dma_start(a1[:], w["s_a1"].rearrange("k o -> o k").to_broadcast([P, D])).then_inc(a_ready, 16)
                with sp.Fori(0, NCK // 2) as it:
                    for b in range(2):
                        c = it * 2 + b
                        sp.wait_ge(added, c + 1)
                        for k in range(K_ACC):
                            sp.dma_start(t[b][:, k, :, :], d.acc[k][bass.ds(c * (CT * P), CT * P), :].rearrange("(t p) k -> p t k", p=P)).then_inc(t_ready[b], 16)
                with sp.Fori(0, NCK // 2) as it:
                    for b in range(2):
                        c = it * 2 + b
                        sp.wait_ge(y_done, c + 1)
                        sp.dma_start(x[b][:], chunk_of(d.h, c)).then_inc(x_ready[b], 16)

            @block.gpsimd
            def _(pool):
                with pool.Fori(0, NCK // 2) as it:
                    for b in range(2):
                        c = it * 2 + b
                        pool.wait_ge(y_done, c + 3)
                        pool.sem_inc(held, 1)
                        pool.dma_start(chunk_of(out, c), y[b][:]).then_inc(stored[b], 16)
                for b in range(2):
                    pool.wait_ge(stored[b], 16 * (NCK // 2))

            @block.scalar
            def _(act):
                act.wait_ge(abs_ready, 1)
                nc.scalar.activation(e[:], e[:], ACT.Exp).then_inc(exp_ready, 1)
                act.wait_ge(log_arg, 1)
                nc.scalar.activation(e[:], e[:], ACT.Ln).then_inc(log_ready, 1)
                with act.Fori(0, NCK // 2) as it:
                    for b in range(2):
                        c = it * 2 + b
                        act.wait_ge(neg_ready, c + 1)
                        nc.scalar.activation(prod[:], y[b][:], ACT.Exp).then_inc(elu_ready, 1)
                        act.wait_ge(eps_ready, c + 1)
                        nc.scalar.activation(sd[:, 1, :], sd[:, 0, :], ACT.Sqrt).then_inc(sd_ready, 1)

            @block.vector
            def _(dve):
                v = nc.vector
                ch = Chain(dve, step, K_ACC + 3)
                dve.sem_inc(added, 2)
                sch = Chain(dve, soft_step)
                sch.do(v.tensor_scalar(no_node[:, 0:NT - 1], m.mask[:, 0:1].to_broadcast([P, NT - 1]), -1.0, 1.0, ALU.mult, ALU.add))
                sch.do(v.tensor_scalar(no_node[:, NT - 1:NT], m.mask[:, 1:2], -1.0, 1.0, ALU.mult, ALU.add))
                sch.wait()
                dve.wait_ge(a_ready, 16)
                with dve.Fori(0, NCK // 2) as it:
                    for b in range(2):
                        c = it * 2 + b
                        cs = bass.ds(c * CT, CT)
                        ch.turn(c)
                        dve.wait_ge(t_ready[b], it * (16 * K_ACC) + 16 * K_ACC)
                        for k in range(1, K_ACC):
                            ch.link(v.tensor_tensor(t[b][:, 0, :, :], t[b][:, 0, :, :], t[b][:, k, :, :], ALU.add))
                        ch.link(v.tensor_tensor(norm[:].unsqueeze(2), t[b][:, 0, :, D:K], no_node[:, cs].unsqueeze(2), ALU.add))
                        ch.link(v.reciprocal(norm[:], norm[:]))
                        v.tensor_tensor(o[:, cs, :], t[b][:, 0, :, 0:D], norm[:].unsqueeze(2).to_broadcast([P, CT, D]), ALU.mult).then_inc(added, 1)
                        dve.wait_ge(added, c + 3)
                        ch.link(v.tensor_tensor(prod[:], o[:, cs, :], a1[:].unsqueeze(1).to_broadcast([P, CT, D]), ALU.mult))
                        ch.link(v.tensor_reduce(z[:, cs], prod[:], AX_X, ALU.add))
                        ch.close()
                sch.link(v.scalar_tensor_tensor(out=e[:], in0=z[:], scalar=-1.0, in1=z[:], op0=ALU.mult, op1=ALU.min))
                dve.sem_inc(abs_ready, 1)
                dve.wait_ge(exp_ready, 1)
                v.tensor_scalar(e[:], e[:], 1.0, None, ALU.add).then_inc(log_arg, 1)
                dve.wait_ge(log_ready, 1)
                sch.link(v.scalar_tensor_tensor(out=z[:], in0=z[:], scalar=0.0, in1=e[:], op0=ALU.max, op1=ALU.add))
                nch = Chain(dve, nstep, NORM_STEPS + 2)
                dve.sem_inc(y_done, 2)

                def finish(c, b, turn, reused):
                    nch.turn(c)
                    cs = bass.ds(c * CT, CT)
                    if reused:
                        dve.wait_ge(stored[b], turn * 16)
                    v.scalar_tensor_tensor(out=y[b][:], in0=o[:, cs, :], scalar=0.0, in1=z[:, cs].unsqueeze(2).to_broadcast([P, CT, D]), op0=ALU.min, op1=ALU.mult).then_inc(neg_ready, 1)
                    dve.wait_ge(elu_ready, c + 1)
                    nch.link(v.scalar_tensor_tensor(out=y[b][:], in0=o[:, cs, :], scalar=0.0, in1=prod[:], op0=ALU.max, op1=ALU.add))
                    dve.wait_ge(x_ready[b], turn * 16 + 16)
                    nch.link(v.scalar_tensor_tensor(out=y[b][:], in0=y[b][:], scalar=-1.0, in1=x[b][:], op0=ALU.add, op1=ALU.add))
                    norm_chunk(v, dve, nch, y[b], st, mv, sd, eps_ready, sd_ready, y_done, held, c)
                    nch.close()
                for b in range(2):
                    finish(b, b, 0, False)
                with dve.Fori(1, NCK // 2) as it:
                    for b in range(2):
                        finish(it * 2 + b, b, it, True)


def build(nc, d, w, out):
    m = Mem()
    with ExitStack() as ctx:
        def sb(name, shape, dt=F32):
            return ctx.enter_context(nc.sbuf_tensor(name, shape, dt))
        SX = S + GROUP
        m.iota_i = sb("iota_i", [P, S], I32)
        m.pidx_i = sb("pidx_i", [P, 1], I32)
        m.iota = sb("iota", [P, S])
        m.pidx = sb("pidx", [P, 1])
        m.ones = sb("ones", [P, P])
        m.zeros = sb("zeros", [P, D + 1])
        m.minus_one = sb("minus_one", [1, P])
        m.ident = sb("ident", [P, P])
        m.mask = sb("mask", [P, 2])
        m.is_p0 = sb("is_p0", [P, 1])
        m.node_mask = sb("node_mask", [P, 2, P])
        m.src_slot = sb("src_slot", [P, SX], I32)
        m.rel_slot = sb("rel_slot", [P, SX], I32)
        m.w_slot = sb("w_slot", [P, SX])
        m.first = sb("first", [P, SX])
        m.loc = sb("loc", [P, SX])
        m.loc_m = sb("loc_m", [P, SX])
        m.trow = sb("trow", [1, SX], I32)
        m.nrow = sb("nrow", [1, SX], I32)
        m.carry_b = sb("carry_b", [H, S])
        m.carry_col = sb("carry_col", [P, SCH])

        sems = []

        def phase(name):
            def sem(s):
                sems.append(nc.alloc_semaphore(name=f"{name}_{s}"))
                return sems[-1]
            return sem

        def recycle():
            nc.clear_and_free_semaphores(sems)
            nc.all_engine_barrier()
            sems.clear()
        phase_constants(nc, m, phase("const"))
        gat_ctx = ExitStack()
        m.self_term = gat_ctx.enter_context(nc.sbuf_tensor("self_term", [P, 2 * H], F32))
        m.fold = gat_ctx.enter_context(nc.sbuf_tensor("fold", [39, 2 * H], F32))
        m.type_row = gat_ctx.enter_context(nc.sbuf_tensor("type_row", [P, 1], F32))
        m.w_table = gat_ctx.enter_context(nc.sbuf_tensor("w_table", [P, 2, D + 2 * H], F32))
        m.a_i = gat_ctx.enter_context(nc.sbuf_tensor("a_i", [P, NT * H], F32))
        m.a_j = gat_ctx.enter_context(nc.sbuf_tensor("a_j", [P, NT * H], F32))
        with ExitStack() as terms_ctx:
            m.sel = terms_ctx.enter_context(nc.sbuf_tensor("sel", [TCP, TCH, S], F32))
            phase_index(nc, m, d, phase("index"))
            phase_edge_weights(nc, m, d, w, phase("ew"))
            phase_edge_terms(nc, m, d, phase("et"))
            phase_slot_terms(nc, m, d, phase("st"))
        h_in = d.x
        for l in (1, 2):
            phase_table_weights(nc, m, w, l, phase(f"tw{l}"))
            phase_table(nc, m, d, h_in, l, phase(f"tb{l}"))
            with ExitStack() as layer_ctx:
                m.agg = layer_ctx.enter_context(nc.sbuf_tensor(f"agg{l}", [P, NT * AGG], F32))
                with nc.sbuf_tensor(f"slot_terms{l}", [P, H, S + GROUP], F32) as m.slot_terms:
                    phase_load_terms(nc, m, d, l, phase(f"lt{l}"))
                    phase_attention(nc, m, d, l, phase(f"at{l}"))
                mv = layer_ctx.enter_context(nc.sbuf_tensor(f"mv{l}", [P, NT * 2], F32))
                bn = layer_ctx.enter_context(nc.sbuf_tensor(f"bn{l}", [P, 2, D], F32))
                with ExitStack() as merge_ctx:
                    cagg = merge_ctx.enter_context(nc.sbuf_tensor(f"cagg{l}", [P, NT * AGG], F32))
                    fac = merge_ctx.enter_context(nc.sbuf_tensor(f"fac{l}", [P, 3, NT, H], F32))
                    phase_carry(nc, m, d, l, cagg, phase(f"cy{l}"))
                    phase_factors(nc, m, d, l, cagg, fac, phase(f"fa{l}"))
                    phase_project(nc, m, d, w, l, cagg, fac, mv, phase(f"pj{l}"))
                phase_norm(nc, m, d, w, l, h_in, mv, bn, phase(f"nm{l}"))
                phase_apply(nc, m, d, l, bn, phase(f"ap{l}"))
            h_in = d.h
            recycle()
        gat_ctx.close()

        with ExitStack() as conv_ctx:
            m.cut = conv_ctx.enter_context(nc.sbuf_tensor("cut", [P, SX], F32))
            m.w_conv_in = conv_ctx.enter_context(nc.sbuf_tensor("w_conv_in", [P, 2, FILT], F32))
            m.w_conv_out = conv_ctx.enter_context(nc.sbuf_tensor("w_conv_out", [FILT, D], F32))
            m.b_conv_out = conv_ctx.enter_context(nc.sbuf_tensor("b_conv_out", [1, D], F32))
            m.w_radial = conv_ctx.enter_context(nc.sbuf_tensor("w_radial", [RADIAL, FILT], F32))
            m.sums = conv_ctx.enter_context(nc.sbuf_tensor("conv_sums", [P, NT * FILT], F32))
            phase_cutoff(nc, m, phase("cut"))
            phase_conv_weights(nc, m, w, phase("cw"))
            phase_conv_table(nc, m, d, phase("ct"))
            phase_sum_messages(nc, m, d, "conv", d.conv_table[:, :], m.src_slot, phase("conv"))
            phase_conv_out(nc, m, d, phase("co"))
        recycle()
        phase_rel_tables(nc, m, d, w, phase("rt"))
        m.gated = sb("gated", [P, NT * (D + 1)])
        with nc.sbuf_tensor("rel_sums", [P, NT * (D + 1)], F32) as m.sums:
            phase_sum_messages(nc, m, d, "rel", d.rel_table[:, :], m.rel_slot, phase("rel"))
            phase_gate(nc, m, d, w, phase("gate"))
        recycle()
        phase_scatter(nc, m, d, phase("scatter"))
        phase_last(nc, m, d, w, out, phase("last"))


def kernel(**inputs):
    import numpy as np
    import concourse.bacc as bacc
    from concourse.bass_utils import run_bass_kernel_spmd

    nc = bacc.Bacc("TRN2", target_bir_lowering=False, num_devices=1)
    a = {k: np.asarray(v) for k, v in inputs.items()}

    def edge_tiles(v, pad):
        out = np.full((TP * P,) + v.shape[1:], pad, v.dtype)
        out[:N_EDGES] = v
        return out
    dst_ext = np.full((TP + 2) * P, PAD_DST, np.int32)
    dst_ext[:P] = -1
    dst_ext[P:P + N_EDGES] = a["dst"]
    x_tiles = np.zeros((NT, P, D), np.float32)
    padded = np.zeros((NT * NPT, D), np.float32)
    padded[:N_NODES] = a["x"]
    x_tiles[:, 1:, :] = padded.reshape(NT, NPT, D)
    arrays = {
        "dst_ext": dst_ext.reshape(TP + 2, P),
        "src": edge_tiles(a["src"], 0).reshape(TP, P),
        "type8": edge_tiles(a["edge_type_8"], 0).reshape(TP, P),
        "type7": edge_tiles(a["edge_type_7"], 0).reshape(1, TP * P),
        "weight": edge_tiles(a["edge_weight"], 0.0).reshape(TP, P),
        "attr16_T": np.ascontiguousarray(edge_tiles(a["edge_attr_16"], 0.0).T),
        "attr12_T": np.ascontiguousarray(edge_tiles(a["edge_attr_12"], 0.0).T),
        "x": x_tiles,
    }
    for name, v in a.items():
        for l, short in (("L0_gnn_", "g_"), ("L1_gnn_", "c_"), ("L2_gnn_", "r_"), ("L3_gnn_", "s_")):
            if name.startswith(l):
                arrays[short + name[len(l):]] = v
    for k in ("c_W_radial_to_message", "c_W_lin1", "c_W_message_to_node", "r_sl_w"):
        arrays[k + "_T"] = np.ascontiguousarray(arrays[k].T)
    d, w = Mem(), {}
    handles = {}
    for k, v in arrays.items():
        handles[k] = nc.dram_tensor("in_" + k, v.shape, mybir.dt.from_np(v.dtype), kind="ExternalInput").ap()
    d.dst_ext, d.src, d.type8, d.type7, d.weight = (handles[k] for k in ("dst_ext", "src", "type8", "type7", "weight"))
    d.attr16_T, d.attr12_T, d.x = handles["attr16_T"], handles["attr12_T"], handles["x"]
    for k, h in handles.items():
        if k[1:2] == "_":
            w[k if k[0] != "g" else k[2:]] = h

    def dram(name, shape):
        return nc.dram_tensor(name, shape, F32, kind="Internal").ap()
    d.carry_rows = dram("carry_rows", (1, SCH * P))
    d.edge_terms = dram("edge_terms", (TP, P, 2 * H))
    d.terms = [dram(f"terms{l}", (P, H, S + GROUP)) for l in (1, 2)]
    d.table = dram("table", (NR, TABW))
    d.h = dram("h", (NT, P, D))
    d.h2 = dram("h2", (NT, P, D))
    d.base = dram("base", (NT, P, D))
    d.conv_table = dram("conv_table", (NR, FILT))
    d.acc = [dram(f"acc{k}", (NR + P, D + 1)) for k in range(K_ACC)]
    d.rel_table = dram("rel_table", (N_REL * NR, D))
    d.carry = dram("carry", (S, AGG))
    out = nc.dram_tensor("out", (NT, P, D), F32, kind="ExternalOutput").ap()
    build(nc, d, w, out)
    r = run_bass_kernel_spmd(nc, [{"in_" + k: v for k, v in arrays.items()}], core_ids=[0])
    got = r.results[0]["out"]
    return np.ascontiguousarray(got[:, 1:, :].reshape(NT * NPT, D)[:N_NODES])
```

```python
from contextlib import ExitStack

import numpy as np
import concourse.bass as bass
from concourse import mybir

F32 = mybir.dt.float32
I32 = mybir.dt.int32
BF16 = mybir.dt.bfloat16
ALU = mybir.AluOpType
ACT = mybir.ActivationFunctionType
AX_X = mybir.AxisListType.X

P = 128
N_NODES = 6250
N_EDGES = 100000
D = 256
H = 8
C = D // H
N_TYPES = 7
SELF_TYPE = 6
N_REL = 8
EDIM = 16
RADIAL = 12
FILT = 64
NEG_SLOPE = 0.2
EPS = 1e-5
BIG = 1e30
CUTOFF = 5.0

NPT = P - 1
NT = -(-N_NODES // NPT)
NR = NT * P
LAST_ROWS = N_NODES - (NT - 1) * NPT + 1
assert NT % 2 == 0

TE = -(-N_EDGES // P)
TCH = 7
TCP = 112
TP = TCH * TCP
assert TP >= TE + 1
GROUP = 8
SETS = 4
BODY = GROUP * SETS
S = -(-(TE + NT - 1) // BODY) * BODY
NG = S // GROUP
SH = S // 2
SCH = -(-S // P)
KS = SCH + NT - 1
assert KS % GROUP == 0
assert SH <= 512
PAD_DST = NT * NPT - 1
TX = S + 2 * GROUP - (NT - 1)
assert TX >= TP

AGG = D + 2 * H + 1
XW = AGG + 1
TABW = D + H

CT = 5
NCK = NT // CT
assert NT % CT == 0 and NCK % 2 == 0
NORM_STEPS = 2 * CT + 1
CHUNK_ORDER = [(True, 0)] + [x for t in range(1, CT) for x in ((True, t), (False, t - 1))] + [(False, CT - 1)]
PAIR_ORDER = [(True, 0)] + [x for t in range(1, 2 * CT) for x in ((True, t), (False, t - 1))] + [(False, 2 * CT - 1)]
K_ACC = 4
assert GROUP % K_ACC == 0


class Mem:
    pass


class Chain:

    def __init__(self, eng, sem, per=0):
        self.eng, self.sem, self.per = eng, sem, per
        self.base, self.k = 0, 0

    def turn(self, n):
        self.base, self.k = n * self.per, 0

    def do(self, ins):
        ins.then_inc(self.sem, 1)
        self.k += 1

    def wait(self):
        self.eng.wait_ge(self.sem, self.base + self.k)

    def link(self, ins):
        self.do(ins)
        self.wait()

    def close(self):
        assert self.k == self.per, (self.k, self.per)


def buf_maker(nc, ctx, prefix):
    def sb(name, shape, dt=F32):
        return ctx.enter_context(nc.sbuf_tensor(f"{prefix}_{name}", shape, dt))

    def ps(name, shape):
        return ctx.enter_context(nc.psum_tensor(f"{prefix}_{name}", shape, F32))
    return sb, ps


def phase_constants(nc, m, sem):
    ready = sem("iota_ready")
    step = sem("const_step")
    with ExitStack() as ctx:
        sb, _ = buf_maker(nc, ctx, "const")
        iota_i = sb("iota_i", [P, S], I32)
        pidx_i = sb("pidx_i", [P, 1], I32)
        with nc.Block() as block:
            @block.gpsimd
            def _(pool):
                nc.gpsimd.iota(iota_i[:], pattern=[[1, S]], base=0, channel_multiplier=0).then_inc(ready, 1)
                nc.gpsimd.iota(pidx_i[:], pattern=[[1, 1]], base=0, channel_multiplier=1).then_inc(ready, 1)

            @block.vector
            def _(dve):
                ch = Chain(dve, step)
                dve.wait_ge(ready, 2)
                ch.do(nc.vector.tensor_copy(m.iota[:], iota_i[:]))
                ch.do(nc.vector.tensor_copy(m.pidx[:], pidx_i[:]))
                ch.do(nc.vector.memset(m.ones[:], 1.0))
                ch.do(nc.vector.memset(m.minus_one[:], -1.0))
                ch.link(nc.vector.memset(m.zeros[:], 0.0))
                ch.do(nc.vector.tensor_scalar(m.ident[:], m.iota[:, 0:P], m.pidx[:, 0:1], None, ALU.is_equal))
                ch.do(nc.vector.tensor_scalar(m.mask[:, 0:1], m.pidx[:], 0.0, None, ALU.is_gt))
                ch.do(nc.vector.tensor_scalar(m.is_p0[:], m.pidx[:], 0.0, None, ALU.is_equal))
                ch.link(nc.vector.tensor_scalar(m.mask[:, 1:2], m.pidx[:], float(LAST_ROWS), None, ALU.is_lt))
                ch.link(nc.vector.tensor_tensor(m.mask[:, 1:2], m.mask[:, 1:2], m.mask[:, 0:1], ALU.mult))
                ch.do(nc.vector.tensor_scalar(m.node_mask[:, 0, :], m.ones[:], m.mask[:, 0:1], None, ALU.mult))
                ch.link(nc.vector.tensor_scalar(m.node_mask[:, 1, :], m.ones[:], m.mask[:, 1:2], None, ALU.mult))


def phase_index(nc, m, d, sem):
    loaded = sem("edges_loaded")
    tiles_ready = sem("edge_rows_ready")
    step = sem("index_step")
    moved = sem("slot_moved")
    taken = sem("slot_taken")
    qrow_ready = sem("carried_row_ready")
    qb_ready = sem("carried_spread")
    n_ready = sem("node_tile_ready")
    stored = sem("carried_stored")
    with ExitStack() as ctx:
        sb, ps = buf_maker(nc, ctx, "ix")
        raw = {n: sb(f"{n}_raw", [TCP, TCH, P], I32) for n in ("dst", "dprev", "src", "rel")}
        dnext_raw = sb("dnext_raw", [TCP, TCH], I32)
        rows = sb("rows", [TCP, 6, TCH, P])
        wide = sb("wide", [TCP, 3, TCH * P])
        wide_i = sb("wide_i", [TCP, TCH * P], I32)
        q = sb("q", [TCP, TCH, P])
        qn = sb("qn", [TCP, TCH])
        small = sb("small", [TCP, 4, TCH])
        small_i = sb("small_i", [TCP, TCH], I32)
        tcol = sb("tcol", [TCP, TCH])
        sel = sb("sel", [TCP, TCH, S])
        slot = sb("slot", [P, 6, S])
        qrow = sb("qrow", [1, 3, S])
        tmp = sb("tmp", [P, S])
        start = sb("start", [P, SCH])
        step_tile = sb("step_tile", [P, KS])
        psum = [ps(f"ps{b}", [P, 2, 512]) for b in range(2)]

        with nc.Block() as block:
            @block.sync
            def _(sp):
                flat = d.dst_ext.rearrange("t p -> (t p)")
                for name, at in (("dst", P), ("dprev", P - 1)):
                    sp.dma_start(raw[name][:], flat[at:at + TP * P].rearrange("(c t p) -> t c p", c=TCH, p=P)).then_inc(loaded, 16)
                sp.dma_start(raw["src"][:], d.src.rearrange("(c t) p -> t c p", c=TCH)).then_inc(loaded, 16)
                sp.dma_start(raw["rel"][:], d.type8.rearrange("(c t) p -> t c p", c=TCH)).then_inc(loaded, 16)
                sp.dma_start(rows[:, 3, :, :], d.weight.rearrange("(c t) p -> t c p", c=TCH)).then_inc(loaded, 16)
                with nc.allow_non_contiguous_dma(reason="one word per edge tile"):
                    sp.dma_start(dnext_raw[:], d.dst_ext[2:2 + TP, 0:1].rearrange("(c t) p -> t (c p)", c=TCH)).then_inc(loaded, 16)

            @block.vector
            def _(dve):
                ch = Chain(dve, step)

                def floor_npt(out, x, t0, t1, ti):
                    ch.link(nc.vector.tensor_scalar(t0, x, float(NPT // 2), 1.0 / NPT, ALU.subtract, ALU.mult))
                    ch.link(nc.vector.tensor_copy(ti, t0))
                    ch.link(nc.vector.tensor_copy(out, ti))
                    ch.link(nc.vector.scalar_tensor_tensor(out=t0, in0=out, scalar=-float(NPT), in1=x, op0=ALU.mult, op1=ALU.add))
                    ch.do(nc.vector.tensor_scalar(t1, t0, float(NPT), None, ALU.is_ge))
                    ch.link(nc.vector.tensor_scalar(t0, t0, 0.0, None, ALU.is_lt))
                    ch.link(nc.vector.tensor_tensor(t1, t1, t0, ALU.subtract))
                    ch.link(nc.vector.tensor_tensor(out, out, t1, ALU.add))

                def flat(a):
                    return a.rearrange("t c p -> t (c p)")
                for v, pad in ((m.src_slot, 0), (m.rel_slot, 0), (m.w_slot, 0.0), (m.trow, 0), (m.nrow, NT - 1), (m.first, 0.0), (m.loc, -1.0), (m.loc_m, -1.0)):
                    ch.do(nc.vector.memset(v[:, S:S + 2 * GROUP], pad))
                dve.wait_ge(loaded, 6 * 16)
                t0, t1, x = wide[:, 0, :], wide[:, 1, :], wide[:, 2, :]
                for name, to in (("src", 1), ("dst", 0)):
                    ch.link(nc.vector.tensor_copy(x, flat(raw[name][:])))
                    floor_npt(flat(q[:]), x, t0, t1, wide_i[:])
                    ch.link(nc.vector.scalar_tensor_tensor(out=flat(rows[:, to, :, :]), in0=x, scalar=1.0, in1=flat(q[:]), op0=ALU.add, op1=ALU.add))
                ch.link(nc.vector.tensor_copy(t0, flat(raw["rel"][:])))
                ch.link(nc.vector.scalar_tensor_tensor(out=flat(rows[:, 2, :, :]), in0=t0, scalar=float(NR), in1=flat(rows[:, 1, :, :]), op0=ALU.mult, op1=ALU.add))
                ch.link(nc.vector.tensor_copy(t0, flat(raw["dprev"][:])))
                ch.link(nc.vector.tensor_tensor(flat(rows[:, 4, :, :]), x, t0, ALU.not_equal))
                ch.link(nc.vector.tensor_copy(small[:, 2, :], dnext_raw[:]))
                floor_npt(qn[:], small[:, 2, :], small[:, 0, :], small[:, 1, :], small_i[:])
                for c in range(TCH):
                    ch.do(nc.vector.tensor_scalar(tcol[:, c:c + 1], m.pidx[0:TCP, :], float(c * TCP), None, ALU.add))
                ch.wait()
                ch.link(nc.vector.tensor_tensor(small[:, 0, :], qn[:], tcol[:], ALU.add))
                ch.link(nc.vector.scalar_tensor_tensor(out=small[:, 1, :], in0=tcol[:], scalar=-1.0, in1=q[:, :, 0], op0=ALU.add, op1=ALU.add))
                ch.link(nc.vector.memset(small[0:1, 1, 0:1], -1.0))
                for c in range(TCH):
                    ch.do(nc.vector.tensor_scalar(rows[:, 5, c, :], m.ones[0:TCP, :], tcol[:, c:c + 1], None, ALU.mult))
                    ch.do(nc.vector.tensor_scalar(sel[:, c, :], m.iota[0:TCP, :], small[:, 0, c:c + 1], None, ALU.is_le))
                ch.wait()
                for c in range(TCH):
                    ins = nc.vector.scalar_tensor_tensor(out=sel[:, c, :], in0=m.iota[0:TCP, :], scalar=small[:, 1, c:c + 1], in1=sel[:, c, :], op0=ALU.is_gt, op1=ALU.mult)
                ins.then_inc(tiles_ready, 1)
                for a in range(6):
                    dve.wait_ge(moved, a + 1)
                    nc.vector.tensor_copy(slot[:, a, :].rearrange("p (h s) -> p h s", h=2), psum[a % 2][:, :, 0:SH]).then_inc(taken, 1)
                dve.wait_ge(taken, 6)
                ch.do(nc.vector.tensor_copy(m.src_slot[:, 0:S], slot[:, 1, :]))
                ch.do(nc.vector.tensor_copy(m.rel_slot[:, 0:S], slot[:, 2, :]))
                ch.do(nc.vector.tensor_copy(m.w_slot[:, 0:S], slot[:, 3, :]))
                ch.do(nc.vector.tensor_copy(m.trow[:, 0:S], slot[0:1, 5, :]))
                ch.do(nc.vector.tensor_scalar(m.first[:, 0:S], slot[:, 4, :], m.is_p0[:, 0:1], None, ALU.max))
                ch.link(nc.vector.tensor_tensor(tmp[:], m.iota[:], slot[:, 5, :], ALU.subtract))
                ch.do(nc.vector.tensor_copy(m.nrow[:, 0:S], tmp[0:1, :]))
                ch.do(nc.vector.tensor_copy(start[:], tmp[:, 0:S:P]))
                ch.link(nc.vector.memset(m.step_chunk_f[:], 0.0))
                for c in range(1, SCH):
                    ch.link(nc.vector.tensor_scalar(start[:, c:c + 1], start[:, c:c + 1], float(c), None, ALU.add))
                    ch.link(nc.vector.scalar_tensor_tensor(out=m.step_chunk_f[:], in0=m.iota[:, 0:KS], scalar=start[:, c:c + 1], in1=m.step_chunk_f[:], op0=ALU.is_ge, op1=ALU.add))
                ch.link(nc.vector.tensor_tensor(step_tile[:], m.iota[:, 0:KS], m.step_chunk_f[:], ALU.subtract))
                ch.do(nc.vector.tensor_copy(m.step_chunk[:], m.step_chunk_f[0:1, :]))
                ch.do(nc.vector.tensor_copy(m.step_tile[:], step_tile[0:1, :]))
                ch.do(nc.vector.tensor_scalar(m.step_rel[:], step_tile[:], -float(P), None, ALU.mult))
                ch.link(nc.vector.scalar_tensor_tensor(out=m.loc[:, 0:S], in0=tmp[:], scalar=-float(P), in1=slot[:, 0, :], op0=ALU.mult, op1=ALU.add))
                ch.link(nc.vector.tensor_scalar(qrow[:, 0, :], m.loc[0:1, 0:S], 1.0, None, ALU.is_ge))
                ch.link(nc.vector.tensor_scalar(qrow[:, 1, :], m.loc[0:1, 0:S], float(P), None, ALU.is_lt))
                ch.link(nc.vector.tensor_tensor(qrow[:, 0, :], qrow[:, 0, :], qrow[:, 1, :], ALU.mult))
                ch.link(nc.vector.tensor_scalar(qrow[:, 1, :], slot[0:1, 4, :], 0.0, None, ALU.is_equal))
                ch.link(nc.vector.tensor_tensor(qrow[:, 0, :], qrow[:, 0, :], qrow[:, 1, :], ALU.mult))
                ch.link(nc.vector.scalar_tensor_tensor(out=qrow[:, 1, :], in0=slot[0:1, 0, :], scalar=1.0, in1=qrow[:, 0, :], op0=ALU.add, op1=ALU.mult))
                ch.link(nc.vector.scalar_tensor_tensor(out=qrow[:, 2, :], in0=m.loc[0:1, 0:S], scalar=0.5, in1=qrow[:, 0, :], op0=ALU.add, op1=ALU.mult))
                ch.do(nc.vector.tensor_scalar(qrow[:, 1, :], qrow[:, 1, :], 1.0, None, ALU.subtract))
                ch.do(nc.vector.tensor_scalar(qrow[:, 2, :], qrow[:, 2, :], 0.5, None, ALU.subtract))
                ch.wait()
                nc.vector.memset(tmp[0:1, 0:1], 0.0).then_inc(qrow_ready, 1)
                dve.wait_ge(qb_ready, 2)
                psq = psum[1][:, :, 0:SH]
                ch.link(nc.vector.tensor_tensor(tmp[:].rearrange("p (h s) -> p h s", h=2), m.loc[:, 0:S].rearrange("p (h s) -> p h s", h=2), psq, ALU.is_equal))
                ch.do(nc.vector.tensor_copy(m.carry_b[:].rearrange("p (h s) -> p h s", h=2), psum[0][0:H, :, 0:SH]))
                ch.link(nc.vector.tensor_tensor(tmp[:], tmp[:], m.loc[:, 0:S], ALU.mult))
                ch.link(nc.vector.tensor_tensor(m.loc_m[:, 0:S], m.loc[:, 0:S], tmp[:], ALU.subtract))

            @block.tensor
            def _(pe):
                pe.wait_ge(tiles_ready, 1)
                for a in range(6):
                    if a >= 2:
                        pe.wait_ge(taken, a - 1)
                    for h in range(2):
                        for c in range(TCH):
                            ins = nc.tensor.matmul(psum[a % 2][:, h, 0:SH], rows[:, a, c, :], sel[:, c, h * SH:(h + 1) * SH], start=(c == 0), stop=(c == TCH - 1))
                    ins.then_inc(moved, 1)
                pe.wait_ge(qrow_ready, 1)
                for a in range(2):
                    for h in range(2):
                        ins = nc.tensor.matmul(psum[a][:, h, 0:SH], m.ones[0:1, :], qrow[:, 1 + a, h * SH:(h + 1) * SH], start=True, stop=True)
                    ins.then_inc(qb_ready, 1)

            @block.scalar
            def _(act):
                act.wait_ge(qrow_ready, 1)
                act.dma_start(d.carry_rows[:, 0:S], qrow[:, 1, :]).then_inc(stored, 16)
                act.dma_start(d.carry_rows[:, S:SCH * P], m.minus_one[0:1, 0:SCH * P - S]).then_inc(stored, 16)
                act.wait_ge(stored, 32)
                with nc.allow_non_contiguous_dma(reason="832 words, once"):
                    act.dma_start(m.carry_col[:], d.carry_rows.rearrange("o (c p) -> p (o c)", p=P)).then_inc(stored, 16)
                act.wait_ge(stored, 48)


def phase_edge_weights(nc, m, d, w, sem):
    loaded = sem("weights_loaded")
    zeroed = sem("zeroed")
    step = sem("ew_step")
    folded = sem("folded")
    self_ready = sem("self_ready")
    with ExitStack() as ctx:
        sb, ps = buf_maker(nc, ctx, "ew")
        wt = sb("wt", [39, 2, D])
        ae = sb("ae", [39, 2, D])
        pick = sb("pick", [39, P])
        pk = sb("pk", [39, 3])
        psum = ps("self", [P, 2 * H])
        with nc.Block() as block:
            @block.sync
            def _(sp):
                sp.wait_ge(zeroed, 1)
                for l in range(2):
                    sp.dma_start(wt[0:EDIM, l, :], w[f"We{l + 1}"]).then_inc(loaded, 16)
                    sp.dma_start(wt[32:39, l, :], w[f"te{l + 1}"]).then_inc(loaded, 16)
                    sp.dma_start(ae[:, l, :], w[f"ae{l + 1}"].rearrange("h (o c) -> o (h c)", o=1).to_broadcast([39, D])).then_inc(loaded, 16)

            @block.vector
            def _(dve):
                ch = Chain(dve, step)
                nc.vector.memset(wt[:], 0.0).then_inc(zeroed, 1)
                dve.wait_ge(zeroed, 1)
                dve.wait_ge(loaded, 6 * 16)
                ch.link(nc.vector.tensor_tensor(wt[:], wt[:], ae[:], ALU.mult))
                ch.link(nc.vector.memset(m.fold[:], 0.0))
                ch.do(nc.vector.tensor_reduce(m.fold[:, 0:2 * H], wt[:].rearrange("p l (h c) -> p (l h) c", c=C), AX_X, ALU.add))
                ch.do(nc.vector.tensor_scalar(pk[:, 0:1], m.pidx[0:39, :], float(EDIM), None, ALU.is_lt))
                ch.link(nc.vector.tensor_scalar(pk[:, 1:2], m.pidx[0:39, :], float(32 + SELF_TYPE), None, ALU.is_equal))
                ch.link(nc.vector.tensor_tensor(pk[:, 2:3], pk[:, 0:1], pk[:, 1:2], ALU.add))
                ch.link(nc.vector.tensor_scalar(pick[:], m.ones[0:39, :], pk[:, 2:3], None, ALU.mult))
                nc.vector.tensor_scalar(m.type_row[:], m.pidx[:], 32.0, None, ALU.subtract).then_inc(folded, 1)
                dve.wait_ge(self_ready, 1)
                ch.link(nc.vector.tensor_copy(m.self_term[:], psum[:]))

            @block.tensor
            def _(pe):
                pe.wait_ge(folded, 1)
                nc.tensor.matmul(psum[:], pick[:], m.fold[:, 0:2 * H], start=True, stop=True).then_inc(self_ready, 1)


def phase_edge_terms(nc, m, d, sem):
    CH = 28
    HALF = CH // 2
    NCH = TP // CH
    Q = P // 4
    assert TP % CH == 0 and NCH % 2 == 0
    in_ready = [sem(f"attr_loaded{b}") for b in range(2)]
    hot_ready = sem("type_onehot_ready")
    mm_ready = sem("terms_ready")
    turned = sem("terms_turned")
    copied = sem("terms_copied")
    stored = sem("terms_stored")
    zeroed = sem("attr_zeroed")
    held = sem("held")
    with ExitStack() as ctx:
        sb, ps = buf_maker(nc, ctx, "et")
        attr = [sb(f"attr{b}", [39, CH * P]) for b in range(2)]
        terms = [sb(f"terms{l}", [P, TX * H]) for l in range(2)]
        ty = [sb(f"ty{b}", [39, CH * P], I32) for b in range(2)]
        turn = [sb(f"turn{h}", [P, HALF * Q]) for h in range(2)]
        psum = [ps(f"ps{h}", [P, HALF * Q]) for h in range(2)]
        with nc.Block() as block:
            @block.sync
            def _(sp):
                sp.wait_ge(zeroed, 2)
                with sp.Fori(0, NCH // 2) as it:
                    for b in range(2):
                        n = it * 2 + b
                        sp.wait_ge(mm_ready, n * 2 + 2)
                        sp.dma_start(attr[b][0:EDIM, :], d.attr16_T[:, bass.ds(n * (CH * P), CH * P)]).then_inc(in_ready[b], 16)
                        sp.dma_start(ty[b][32:39, :], d.type7[0:1, bass.ds(n * (CH * P), CH * P)].to_broadcast([N_TYPES, CH * P])).then_inc(in_ready[b], 16)
                sp.wait_ge(copied, NCH * 2 + 2)
                for l in range(2):
                    sp.dma_start(d.terms[l], terms[l][:]).then_inc(stored, 16)
                sp.wait_ge(stored, 32)

            @block.vector
            def _(dve):
                for l in range(2):
                    nc.vector.memset(terms[l][:, TP * H:TX * H], 0.0)
                for b in range(2):
                    nc.vector.memset(attr[b][:], 0.0).then_inc(zeroed, 1)

                def types(b, turn_no):
                    dve.wait_ge(in_ready[b], turn_no * 32 + 32)
                    nc.vector.tensor_scalar(attr[b][32:39, :], ty[b][32:39, :], m.type_row[32:39, 0:1], None, ALU.is_equal).then_inc(hot_ready, 1)

                def transposes(n):
                    for h in range(2):
                        dve.wait_ge(mm_ready, n * 2 + h + 5)
                        dve.wait_ge(copied, n * 2 + h + 1)
                        nc.vector.transpose(turn[h][:], psum[h][:]).then_inc(turned, 1)
                types(0, 0)
                with dve.Fori(0, NCH // 2 - 1) as it:
                    types(1, it)
                    transposes(it * 2)
                    types(0, it + 1)
                    transposes(it * 2 + 1)
                types(1, NCH // 2 - 1)
                transposes(NCH - 2)
                transposes(NCH - 1)

            @block.tensor
            def _(pe):
                pe.sem_inc(mm_ready, 4)
                with pe.Fori(0, NCH // 2) as it:
                    for b in range(2):
                        n = it * 2 + b
                        pe.wait_ge(hot_ready, n + 1)
                        quarters = attr[b][:].rearrange("k (t q e) -> k t q e", q=4, e=Q)
                        for h in range(2):
                            pe.wait_ge(turned, n * 2 + h + 1)
                            pe.sem_inc(held, 1)
                            for q in range(4):
                                ins = nc.tensor.matmul(psum[h][q * Q:(q + 1) * Q, :], m.fold[:], quarters[:, h * HALF:(h + 1) * HALF, q, :], start=True, stop=True)
                            ins.then_inc(mm_ready, 1)

            @block.scalar
            def _(act):
                act.sem_inc(copied, 2)
                act.sem_inc(turned, 2)
                with act.Fori(0, NCH // 2) as it:
                    for b in range(2):
                        for h in range(2):
                            n = it * 2 + b
                            act.wait_ge(turned, n * 2 + h + 3)
                            for l in range(2):
                                ins = nc.scalar.copy(terms[l][:, bass.ds(n * (CH * H) + h * (HALF * H), HALF * H)].rearrange("p (t h) -> p t h", h=H),
                                                     turn[h][:].rearrange("p (t k) -> p t k", k=Q)[:, :, l * H:(l + 1) * H])
                            ins.then_inc(copied, 1)


def phase_table_weights(nc, m, w, l, sem):
    loaded = sem("weights_loaded")
    step = sem("tw_step")
    with ExitStack() as ctx:
        sb, ps = buf_maker(nc, ctx, f"tw{l}")
        wd = sb("wd", [P, 2, D])
        av = sb("av", [P, 2, D])
        prod = sb("prod", [P, 2, 2, D])
        with nc.Block() as block:
            @block.sync
            def _(sp):
                sp.dma_start(m.w_table[:, :, 0:D], w[f"Ws{l}"].rearrange("(k p) n -> p k n", p=P)).then_inc(loaded, 16)
                sp.dma_start(wd[:], w[f"Wd{l}"].rearrange("(k p) n -> p k n", p=P)).then_inc(loaded, 16)
                sp.dma_start(av[:, 0, :], w[f"ad{l}"].rearrange("h (o c) -> o (h c)", o=1).to_broadcast([P, D])).then_inc(loaded, 16)
                sp.dma_start(av[:, 1, :], w[f"as{l}"].rearrange("h (o c) -> o (h c)", o=1).to_broadcast([P, D])).then_inc(loaded, 16)

            @block.vector
            def _(dve):
                ch = Chain(dve, step)
                dve.wait_ge(loaded, 4 * 16)
                for k in range(2):
                    ch.do(nc.vector.tensor_tensor(prod[:, k, 0, :], m.w_table[:, k, 0:D], av[:, 0, :], ALU.mult))
                    ch.do(nc.vector.tensor_tensor(prod[:, k, 1, :], wd[:, k, :], av[:, 1, :], ALU.mult))
                ch.wait()
                for k in range(2):
                    ch.do(nc.vector.tensor_reduce(m.w_table[:, k, D:D + 2 * H], prod[:, k, :, :].rearrange("p a (h c) -> p (a h) c", c=C), AX_X, ALU.add))
                ch.wait()


def tile_of(dram, n):
    return dram[bass.ds(n, 1), :, :].rearrange("o p k -> p (o k)")


def load_and_store(eng, load, store, count):
    half = count // 2
    load(0, 0, 0)
    with eng.Fori(0, half - 1) as it:
        load(it * 2 + 1, 1, it)
        store(it * 2, 0, it)
        load(it * 2 + 2, 0, it + 1)
        store(it * 2 + 1, 1, it)
    load(count - 1, 1, half - 1)
    store(count - 2, 0, half - 1)
    store(count - 1, 1, half - 1)


def phase_attention(nc, m, d, l, sem):
    x_ready = [sem(f"rows_gathered{b}") for b in range(SETS)]
    idx_ready = sem("index_ready")
    idx_pass = sem("index_pass")
    loc_ready = [sem(f"places_loaded{b}") for b in range(2)]
    terms_ready = sem("edge_terms_loaded")
    terms_picked = sem("slot_terms_picked")
    full_ready = sem("onehotT_ready")
    ai_ready = sem("dst_and_edge_terms")
    z_ready = sem("logit_sum")
    al_ready = sem("logits")
    pre_ready = sem("src_and_edge_terms")
    xT_ready = sem("logitsT")
    mT_step = sem("maxT_step")
    mT_ready = sem("maxT")
    m_ready = sem("max_back")
    shift_ready = sem("shifted")
    cols_ready = sem("max_columns")
    ex_ready = sem("exps")
    rhs_ready = sem("messages")
    o_ready = sem("slot_sums")
    copied = sem("sums_copied")
    acc_done = sem("added")
    row_stored = [sem(f"carry_stored{b}") for b in range(2)]
    zeroed = sem("agg_zeroed")
    acc_zeroed = sem("tables_zeroed")
    BANKS = 4
    with ExitStack() as ctx:
        sb, ps = buf_maker(nc, ctx, f"at{l}")
        x = [sb(f"x{b}", [P, GROUP, XW]) for b in range(SETS)]
        idx = [sb(f"idx{b}", [P, GROUP], I32) for b in range(SETS)]
        place = [sb(f"place{b}", [P, GROUP * P], BF16) for b in range(2)]
        terms = sb("terms", [P, TX * H])
        slot_terms = [sb(f"slot_terms{b}", [P, GROUP, H]) for b in range(2)]
        fullT = sb("fullT", [P, GROUP, P])
        main = [sb(f"main{b}", [P, GROUP, P]) for b in range(2)]
        sums = [sb(f"sums{b}", [P, GROUP, AGG]) for b in range(2)]
        first = [sb(f"first{b}", [P, GROUP, H]) for b in range(2)]
        z = sb("z", [P, GROUP, H])
        al = sb("al", [P, GROUP, H])
        shifted = sb("shifted", [P, GROUP, H])
        flag = sb("flag", [GROUP * H, P + 1])
        fwd = sb("fwd", [GROUP * H, P])
        mx = sb("mx", [GROUP * H, P])
        psA = ps("psA", [P, GROUP, H])
        psX = ps("psX", [GROUP * H, 2, P])
        psM = ps("psM", [P, GROUP, H])
        psO = [ps(f"psO{q}", [P, 512]) for q in range(BANKS)]
        NTURN = NG // SETS

        with nc.Block() as block:
            @block.gpsimd
            def _(pool):
                def gather(g, b, reused):
                    if reused:
                        pool.wait_ge(o_ready, (g - SETS + 1) * GROUP)
                    nc.gpsimd.tensor_copy(idx[b][:], m.src_slot[:, bass.ds(g * GROUP, GROUP)]).then_inc(idx_ready, 1)
                    pool.wait_ge(idx_ready, g + 1)
                    pool.sem_inc(idx_pass, 1)
                    for j in range(GROUP):
                        pool.indirect_dma_start(x[b][:, j, 0:TABW], None, d.table[0:NR, :],
                                                bass.IndirectOffsetOnAxis(ap=idx[b][:, j:j + 1], axis=0)).then_inc(x_ready[b], 16)
                for b in range(SETS):
                    gather(b, b, False)
                with pool.Fori(1, NTURN) as it:
                    for b in range(SETS):
                        gather(it * SETS + b, b, True)
                gather(NG, 0, True)
                pool.wait_ge(x_ready[0], 16 * GROUP * (NTURN + 1))

            @block.sync
            def _(sp):
                def load_places(g, b):
                    sp.wait_ge(full_ready, g + 1)
                    sp.dma_start(place[b % 2][:], d.places[bass.ds(g * GROUP, GROUP), :].rearrange("(o s) p -> o (s p)", o=1).to_broadcast([P, GROUP * P])).then_inc(loc_ready[b % 2], 16)
                load_places(0, 0)
                load_places(1, 1)
                sp.dma_start(terms[:], d.terms[l - 1]).then_inc(terms_ready, 16)
                with sp.Fori(0, NG // 2 - 1) as it:
                    for b in range(2):
                        g = it * 2 + b
                        load_places(g + 2, b)
                        sp.wait_ge(copied, g * GROUP + GROUP + BANKS)
                        sp.dma_start(d.carry[bass.ds(g * GROUP, GROUP), :].rearrange("(o j) k -> o (j k)", o=1),
                                     sums[b][0:1, :, :].rearrange("o j k -> o (j k)")).then_inc(row_stored[b], 16)
                load_places(NG, 0)
                load_places(NG + 1, 1)
                for b in range(2):
                    g = NG - 2 + b
                    sp.wait_ge(copied, g * GROUP + GROUP + BANKS)
                    sp.dma_start(d.carry[g * GROUP:(g + 1) * GROUP, :].rearrange("(o j) k -> o (j k)", o=1),
                                 sums[b][0:1, :, :].rearrange("o j k -> o (j k)")).then_inc(row_stored[b], 16)
                for b in range(2):
                    sp.wait_ge(row_stored[b], 16 * (NG // 2 + 1))

            @block.tensor
            def _(pe):
                regs = [pe.alloc_register(f"pe_n{l}_{j}") for j in range(GROUP)]
                pe.sem_inc(ai_ready, 1)

                def dst_terms(g, b):
                    pe.load(regs, m.nrow[0:1, bass.ds(g * GROUP, GROUP)])
                    ns = [pe.snap(r, min_val=0, max_val=NT - 1) for r in regs]
                    pe.wait_ge(z_ready, g + 1)
                    pe.wait_ge(full_ready, g + 3)
                    for j in range(GROUP):
                        ins = nc.tensor.matmul(psA[:, j, :], fullT[:, j, :], m.a_ij[:, bass.ds(ns[j] * (2 * H) + H, H)], start=True, stop=True)
                    ins.then_inc(ai_ready, 1)

                def turn_logits(g, b):
                    pe.wait_ge(al_ready, g + 2)
                    pe.wait_ge(mT_ready, g + 1)
                    nc.tensor.matmul(psX[:, 0, :], al[:].rearrange("p j h -> p (j h)"), m.ident[:], start=True, stop=True)
                    nc.tensor.matmul(psX[:, 1, :], first[b % 2][:].rearrange("p j h -> p (j h)"), m.ident[:], start=True, stop=True).then_inc(xT_ready, 1)

                def turn_max(g, b):
                    pe.wait_ge(mT_ready, g + 2)
                    pe.wait_ge(cols_ready, g + 1)
                    nc.tensor.matmul(psM[:].rearrange("p j h -> p (j h)"), mx[:], m.ident[0:GROUP * H, 0:GROUP * H], start=True, stop=True).then_inc(m_ready, 1)

                def slot_sums(g, b, j):
                    i = g * GROUP + j
                    pe.wait_ge(rhs_ready, g * (GROUP // 2) + j // 2 + 1)
                    pe.wait_ge(copied, i + 1)
                    nc.tensor.matmul(psO[j % BANKS][:, 0:AGG], main[b % 2][:, j, :], x[b][:, j, 0:AGG], start=True, stop=True).then_inc(o_ready, 1)

                dst_terms(0, 0)
                turn_logits(0, 0)
                turn_max(0, 0)
                dst_terms(1, 1)
                with pe.Fori(0, NTURN) as it:
                    for b in range(SETS):
                        g = it * SETS + b
                        g1, b1 = g + 1, (b + 1) % SETS
                        slot_sums(g, b, 0)
                        turn_logits(g1, b1)
                        slot_sums(g, b, 1)
                        slot_sums(g, b, 2)
                        slot_sums(g, b, 3)
                        turn_max(g1, b1)
                        slot_sums(g, b, 4)
                        slot_sums(g, b, 5)
                        dst_terms(g + 2, (b + 2) % SETS)
                        slot_sums(g, b, 6)
                        slot_sums(g, b, 7)

            @block.scalar
            def _(act):
                act.sem_inc(copied, BANKS)
                for b in range(2):
                    act.sem_inc(row_stored[b], 16)

                if l == 1:
                    for k in range(K_ACC):
                        act.dma_start(d.acc[k].rearrange("(c p) k -> p c k", p=P), m.zeros[:].unsqueeze(1).to_broadcast([P, NT + 1, D + 1])).then_inc(acc_zeroed, 16)
                regs = [act.alloc_register(f"act_n{l}_{j}") for j in range(GROUP)]
                act.wait_ge(terms_ready, 16)

                def tiles_of(g):
                    act.load(regs, m.nrow[0:1, bass.ds(g * GROUP, GROUP)])
                    ns = [act.snap(r, min_val=0, max_val=NT - 1) for r in regs]
                    return [nc.s_assert_within(g * GROUP + j - ns[j], 0, TX - 1, skip_runtime_bounds_check_because="node tiles are numbered so that this is an edge tile's number") for j in range(GROUP)]

                def pick_term(g, b, j, ts):
                    if j == 0:
                        act.wait_ge(pre_ready, g + 1)
                    ins = nc.scalar.copy(slot_terms[b % 2][:, j, :], terms[:, bass.ds(ts[j] * H, H)])
                    if j == GROUP - 1:
                        ins.then_inc(terms_picked, 1)

                def exps(g, b):
                    act.wait_ge(shift_ready, g + 1)
                    nc.scalar.activation(x[b][:, :, D:D + H], shifted[:], ACT.Exp).then_inc(ex_ready, 1)

                def copy_sums(g, b, j):
                    i = g * GROUP + j
                    act.wait_ge(o_ready, i + 1)
                    act.wait_ge(acc_done, i + 1)
                    nc.scalar.copy(sums[b % 2][:, j, :], psO[j % BANKS][:, 0:AGG]).then_inc(copied, 1)

                for g in range(2):
                    ts = tiles_of(g)
                    for j in range(GROUP):
                        pick_term(g, g, j, ts)
                exps(0, 0)
                with act.Fori(0, NTURN) as it:
                    for b in range(SETS):
                        g = it * SETS + b
                        act.wait_ge(row_stored[b % 2], it * 32 + (b // 2) * 16 + 16)
                        ts = tiles_of(g + 2)
                        for j in range(GROUP):
                            if j == 6:
                                exps(g + 1, (b + 1) % SETS)
                            copy_sums(g, b, j)
                            if j < 2:
                                for k in range(j * GROUP // 2, (j + 1) * GROUP // 2):
                                    pick_term(g + 2, b + 2, k, ts)

                if l == 1:
                    act.wait_ge(acc_zeroed, 16 * K_ACC)

            @block.vector
            def _(dve):
                regs = [dve.alloc_register(f"dve_n{l}_{j}") for j in range(GROUP)]
                nc.vector.memset(m.agg[:], 0.0).then_inc(zeroed, 1)
                nc.vector.memset(flag[:], 0.0).then_inc(zeroed, 1)
                dve.sem_inc(full_ready, 2)
                dve.sem_inc(z_ready, 1)
                dve.sem_inc(al_ready, 1)
                dve.sem_inc(pre_ready, 2)
                dve.sem_inc(mT_ready, 1)
                dve.sem_inc(cols_ready, 1)
                dve.sem_inc(acc_done, 2 * GROUP)
                mT_ch = Chain(dve, mT_step, 2)
                dve.wait_ge(zeroed, 2)

                def tiles_of(g):
                    dve.load(regs, m.nrow[0:1, bass.ds(g * GROUP, GROUP)])
                    return [dve.snap(r, min_val=0, max_val=NT - 1) for r in regs]

                def onehotT(g, b, pair):
                    dve.wait_ge(loc_ready[b % 2], pair * 16 + 16)
                    dve.wait_ge(ai_ready, g + 1)
                    nc.vector.tensor_scalar(fullT[:].rearrange("p j e -> p (j e)"), place[b % 2][:], m.pidx[:, 0:1], None, ALU.is_equal).then_inc(full_ready, 1)

                def onehot(g, b):
                    at = bass.ds(g * GROUP, GROUP)
                    nc.vector.tensor_tensor(main[b % 2][:], m.iota[:, 0:P].unsqueeze(1).to_broadcast([P, GROUP, P]),
                                            m.loc_m[:, at].unsqueeze(2).to_broadcast([P, GROUP, P]), ALU.is_equal)

                def logits_1(g, b, turn):
                    nc.vector.tensor_copy(first[b % 2][:], m.first[:, bass.ds(g * GROUP, GROUP)].unsqueeze(2).to_broadcast([P, GROUP, H]))
                    dve.wait_ge(x_ready[b], turn * (16 * GROUP) + 16 * GROUP)
                    dve.wait_ge(terms_picked, g + 1)
                    dve.wait_ge(al_ready, g + 1)
                    nc.vector.tensor_tensor(z[:], x[b][:, :, D:D + H], slot_terms[b % 2][:], ALU.add).then_inc(pre_ready, 1)

                def logits_2(g, b):
                    dve.wait_ge(pre_ready, g + 3)
                    dve.wait_ge(ai_ready, g + 2)
                    nc.vector.tensor_tensor(z[:], psA[:], z[:], ALU.add).then_inc(z_ready, 1)

                def logits_3(g, b):
                    dve.wait_ge(z_ready, g + 2)
                    dve.wait_ge(cols_ready, g + 1)
                    nc.vector.scalar_tensor_tensor(out=al[:], in0=z[:], scalar=NEG_SLOPE, in1=z[:], op0=ALU.mult, op1=ALU.max).then_inc(al_ready, 1)

                def scans(g, b, step):
                    mT_ch.turn(g)
                    mT_ch.k = step
                    if step == 0:
                        dve.wait_ge(xT_ready, g + 1)
                        mT_ch.do(nc.vector.tensor_scalar(flag[:, 0:P], psX[:, 1, :], -BIG, None, ALU.mult))
                    elif step == 1:
                        mT_ch.wait()
                        mT_ch.do(nc.vector.tensor_tensor_scan(fwd[:], flag[:, 0:P], psX[:, 0, :], -BIG, ALU.add, ALU.max))
                    else:
                        mT_ch.wait()
                        nc.vector.tensor_tensor_scan(mx[:, ::-1], flag[:, P:0:-1], fwd[:, ::-1], -BIG, ALU.add, ALU.max).then_inc(mT_ready, 1)

                def shifts(g, b):
                    dve.wait_ge(m_ready, g + 1)
                    nc.vector.tensor_tensor(shifted[:], al[:], psM[:], ALU.subtract).then_inc(shift_ready, 1)
                    nc.vector.tensor_copy(x[b][:, :, D + 2 * H:AGG], first[b % 2][:, :, 0:1])
                    nc.vector.tensor_tensor(x[b][:, :, D + H:D + 2 * H], psM[:], first[b % 2][:], ALU.mult).then_inc(cols_ready, 1)

                def messages(g, b, j):
                    if j == 0:
                        dve.wait_ge(ex_ready, g + 1)
                    v = x[b][:, j:j + 2, 0:D].rearrange("p j (h c) -> p j h c", c=C)
                    nc.vector.tensor_tensor(v, v, x[b][:, j:j + 2, D:D + H].unsqueeze(3).to_broadcast([P, 2, H, C]), ALU.mult).then_inc(rhs_ready, 1)

                def add(g, b, j, ns):
                    i = g * GROUP + j
                    dve.wait_ge(copied, i + 1 + BANKS)
                    dve.wait_ge(acc_done, i + 2 * GROUP)
                    to = m.agg[:, bass.ds(ns[j] * AGG, AGG)]
                    nc.vector.tensor_tensor(to, to, sums[b % 2][:, j, :], ALU.add).then_inc(acc_done, 1)

                def period(g, b, turn, last_added):
                    g1, b1 = g + 1, (b + 1) % SETS
                    t1 = turn + 1 if b1 == 0 else turn
                    b0 = (b - 1) % SETS
                    if last_added:
                        ns = tiles_of(g - 1)

                    def add_before(*js):
                        if last_added:
                            for j in js:
                                add(g - 1, b0, j, ns)
                    messages(g, b, 0)
                    logits_1(g1, b1, t1)
                    add_before(0)
                    logits_2(g1, b1)
                    messages(g, b, 2)
                    logits_3(g1, b1)
                    add_before(1)
                    messages(g, b, 4)
                    add_before(2)
                    scans(g1, b1, 0)
                    add_before(3)
                    scans(g1, b1, 1)
                    scans(g1, b1, 2)
                    messages(g, b, 6)
                    add_before(4)
                    shifts(g1, b1)
                    add_before(5)
                    onehotT(g + 2, b + 2, turn * 2 + (b + 2) // 2)
                    add_before(6)
                    add_before(7)
                    onehot(g1, b1)

                onehotT(0, 0, 0)
                onehot(0, 0)
                logits_1(0, 0, 0)
                logits_2(0, 0)
                logits_3(0, 0)
                onehotT(1, 1, 0)
                for step in range(3):
                    scans(0, 0, step)
                shifts(0, 0)
                for b in range(SETS):
                    period(b, b, 0, b > 0)
                with dve.Fori(1, NTURN) as it:
                    for b in range(SETS):
                        period(it * SETS + b, b, it, True)
                ns = tiles_of(NG - 1)
                for j in range(GROUP):
                    add(NG - 1, SETS - 1, j, ns)
                dve.wait_ge(acc_done, S + 2 * GROUP)


def phase_places(nc, m, d, sem):
    turned = sem("places_turned")
    copied = sem("places_copied")
    stored = sem("places_stored")
    with ExitStack() as ctx:
        sb, ps = buf_maker(nc, ctx, "pl")
        rows = sb("rows", [P, SCH, P], BF16)
        psum = [ps(f"ps{b}", [P, 4, P]) for b in range(2)]
        FULL = (S + 2 * GROUP) // P
        REST = (S + 2 * GROUP) % P
        with nc.Block() as block:
            @block.tensor
            def _(pe):
                for c in range(SCH):
                    n = P if c < FULL else REST
                    ins = nc.tensor.matmul(psum[c // 4][0:n, c % 4, :], m.loc[:, c * P:c * P + n], m.ident[:], start=True, stop=True)
                ins.then_inc(turned, 1)

            @block.vector
            def _(dve):
                dve.wait_ge(turned, 1)
                nc.vector.tensor_copy(rows[:, 0:4, :], psum[0][:])
                nc.vector.tensor_copy(rows[:, 4:FULL, :], psum[1][:, 0:FULL - 4, :])
                nc.vector.tensor_copy(rows[0:REST, FULL, :], psum[1][0:REST, FULL - 4, :]).then_inc(copied, 1)

            @block.sync
            def _(sp):
                sp.wait_ge(copied, 1)
                sp.dma_start(d.places[0:FULL * P, :].rearrange("(c p) e -> p c e", p=P), rows[:, 0:FULL, :]).then_inc(stored, 16)
                sp.dma_start(d.places[FULL * P:S + 2 * GROUP, :], rows[0:REST, FULL, :]).then_inc(stored, 16)
                sp.wait_ge(stored, 32)


def phase_carry(nc, m, d, l, cagg, sem):
    zeroed = sem("tail_zeroed")
    loaded = sem("carry_loaded")
    step = sem("carry_step")
    turned = sem("maxima_turned")
    mT_ready = sem("node_maxima")
    back = sem("maxima_back")
    diff_ready = sem("diff_ready")
    ex_ready = sem("factors_ready")
    rows_ready = sem("rows_scaled")
    o_ready = sem("step_summed")
    acc_done = sem("step_added")
    W = SCH * P
    FULL = S // P
    BANKS = 4
    with ExitStack() as ctx:
        sb, ps = buf_maker(nc, ctx, f"cy{l}")
        rows = sb("rows", [P, SCH, AGG])
        mT = sb("mT", [H, W])
        flag = sb("flag", [H, W + 1])
        firstT = sb("firstT", [H, W])
        f8 = sb("f8", [P, SCH, H])
        diff = sb("diff", [P, SCH, H])
        ex = sb("ex", [P, SCH, H])
        rel = sb("rel", [P, 2, KS])
        hot = sb("hot", [P, KS, P])
        psT = [ps(f"psT{b}", [H, 4, P]) for b in range(2)]
        psB = [ps(f"psB{b}", [P, SCH, H]) for b in range(2)]
        psO = [ps(f"psO{b}", [P, 512]) for b in range(BANKS)]
        with nc.Block() as block:
            @block.sync
            def _(sp):
                sp.wait_ge(zeroed, 1)
                sp.dma_start(rows[:, 0:FULL, :], d.carry[0:FULL * P, :].rearrange("(c p) k -> p c k", p=P)).then_inc(loaded, 16)
                if S % P:
                    sp.dma_start(rows[0:S % P, FULL, :], d.carry[FULL * P:S, :]).then_inc(loaded, 16)

            @block.tensor
            def _(pe):
                regs = [pe.alloc_register(f"pe_cy{l}_{j}") for j in range(GROUP)]
                pe.wait_ge(loaded, 16 * (1 + (S % P > 0)))
                for c in range(SCH):
                    ins = nc.tensor.transpose(psT[c // 4][:, c % 4, :], rows[:, c, D + H:D + 2 * H], m.ident[:])
                ins.then_inc(turned, 1)
                pe.wait_ge(mT_ready, 1)
                for c in range(SCH):
                    nc.tensor.transpose(psB[0][:, c, :], mT[:, c * P:(c + 1) * P], m.ident[0:H, 0:H])
                    ins = nc.tensor.transpose(psB[1][:, c, :], firstT[:, c * P:(c + 1) * P], m.ident[0:H, 0:H])
                ins.then_inc(back, 1)
                pe.wait_ge(rows_ready, 1)
                for g in range(KS // GROUP):
                    pe.load(regs, m.step_chunk[0:1, g * GROUP:(g + 1) * GROUP])
                    cs = [pe.snap(r, min_val=0, max_val=SCH - 1) for r in regs]
                    for j in range(GROUP):
                        k = g * GROUP + j
                        if k >= BANKS:
                            pe.wait_ge(acc_done, k - BANKS + 1)
                        nc.tensor.matmul(psO[k % BANKS][:, 0:AGG], hot[:, k, :], rows[:].rearrange("p c k -> p (c k)")[:, bass.ds(cs[j] * AGG, AGG)], start=True, stop=True).then_inc(o_ready, 1)

            @block.scalar
            def _(act):
                act.wait_ge(diff_ready, 1)
                nc.scalar.activation(ex[:], diff[:], ACT.Exp).then_inc(ex_ready, 1)

            @block.vector
            def _(dve):
                regs = [dve.alloc_register(f"dve_cy{l}_{j}") for j in range(GROUP)]
                ch = Chain(dve, step)
                nc.vector.memset(rows[:, FULL:SCH, :], 0.0).then_inc(zeroed, 1)
                ch.do(nc.vector.memset(flag[:], 0.0))
                ch.do(nc.vector.memset(mT[:], 0.0))
                ch.link(nc.vector.memset(firstT[:], 1.0))
                ch.link(nc.vector.tensor_tensor(firstT[:, 1:S], m.carry_b[:, 1:S], m.carry_b[:, 0:S - 1], ALU.not_equal))
                ch.link(nc.vector.tensor_scalar(flag[:, 0:S], firstT[:, 0:S], -BIG, None, ALU.mult))
                dve.wait_ge(turned, 1)
                for b, (c0, c1) in enumerate(((0, 4), (4, SCH))):
                    ch.do(nc.vector.tensor_copy(mT[:, c0 * P:c1 * P].rearrange("p (c q) -> p c q", q=P), psT[b][:, 0:c1 - c0, :]))
                ch.wait()
                ch.link(nc.vector.tensor_tensor_scan(mT[:, 0:S], flag[:, 0:S], mT[:, 0:S], -BIG, ALU.add, ALU.max))
                nc.vector.tensor_tensor_scan(mT[:, S - 1::-1], flag[:, S:0:-1], mT[:, S - 1::-1], -BIG, ALU.add, ALU.max).then_inc(mT_ready, 1)
                ch.do(nc.vector.memset(cagg[:], 0.0))
                ch.do(nc.vector.tensor_copy(rel[:, 0, :], m.step_rel[:]))
                for c in range(SCH):
                    ch.link(nc.vector.tensor_scalar(rel[:, 1, :], m.step_chunk_f[:], float(c), m.carry_col[:, c:c + 1], ALU.is_equal, ALU.mult))
                    ch.link(nc.vector.tensor_tensor(rel[:, 0, :], rel[:, 0, :], rel[:, 1, :], ALU.add))
                ch.do(nc.vector.tensor_tensor(hot[:], m.iota[:, 0:P].unsqueeze(1).to_broadcast([P, KS, P]), rel[:, 0, :].unsqueeze(2).to_broadcast([P, KS, P]), ALU.is_equal))
                dve.wait_ge(back, 1)
                ch.do(nc.vector.tensor_copy(f8[:], psB[1][:]))
                nc.vector.tensor_tensor(diff[:], rows[:, :, D + H:D + 2 * H], psB[0][:], ALU.subtract).then_inc(diff_ready, 1)
                dve.wait_ge(ex_ready, 1)
                ch.wait()
                dve.wait_ge(diff_ready, 1)
                for c in range(SCH):
                    v = rows[:, c, 0:D].rearrange("p (h k) -> p h k", k=C)
                    ch.do(nc.vector.tensor_tensor(v, v, ex[:, c, :].unsqueeze(2).to_broadcast([P, H, C]), ALU.mult))
                ch.do(nc.vector.tensor_tensor(rows[:, :, D:D + H], rows[:, :, D:D + H], ex[:], ALU.mult))
                ch.do(nc.vector.tensor_tensor(rows[:, :, D + H:D + 2 * H], psB[0][:], f8[:], ALU.mult))
                nc.vector.tensor_copy(rows[:, :, D + 2 * H:AGG], f8[:, :, 0:1]).then_inc(rows_ready, 1)
                ch.wait()
                for g in range(KS // GROUP):
                    dve.load(regs, m.step_tile[0:1, g * GROUP:(g + 1) * GROUP])
                    ns = [dve.snap(r, min_val=0, max_val=NT - 1) for r in regs]
                    for j in range(GROUP):
                        k = g * GROUP + j
                        dve.wait_ge(o_ready, k + 1)
                        if k:
                            dve.wait_ge(acc_done, k)
                        to = cagg[:, bass.ds(ns[j] * AGG, AGG)]
                        nc.vector.tensor_tensor(to, to, psO[k % BANKS][:, 0:AGG], ALU.add).then_inc(acc_done, 1)
                dve.wait_ge(acc_done, KS)


def phase_factors(nc, m, d, l, cagg, fac, sem):
    step = sem("factor_step")
    diff_ready = sem("diff_ready")
    ex_ready = sem("exp_ready")
    with ExitStack() as ctx:
        sb, ps = buf_maker(nc, ctx, f"fa{l}")
        a = sb("self", [P, NT, H])
        mm = sb("max", [P, 3, NT, H])
        t = sb("t", [P, NT, H])
        den = sb("den", [P, NT, H])
        agg = m.agg[:].rearrange("p (n k) -> p n k", k=AGG)
        cg = cagg[:].rearrange("p (n k) -> p n k", k=AGG)

        def bc(v):
            return v.to_broadcast([P, NT, H])
        with nc.Block() as block:
            @block.vector
            def _(dve):
                ch = Chain(dve, step)
                v = nc.vector
                a_ij = m.a_ij[:].rearrange("p (n a h) -> p n a h", a=2, h=H)
                ch.link(v.tensor_tensor(a[:], a_ij[:, :, 0, :], a_ij[:, :, 1, :], ALU.add))
                ch.link(v.tensor_tensor(a[:], a[:], bc(m.self_term[:, (l - 1) * H:l * H].unsqueeze(1)), ALU.add))
                ch.link(v.scalar_tensor_tensor(out=mm[:, 2, :, :], in0=a[:], scalar=NEG_SLOPE, in1=a[:], op0=ALU.mult, op1=ALU.max))
                for k, src in enumerate((agg, cg)):
                    ch.link(v.tensor_scalar(t[:], bc(src[:, :, D + 2 * H:AGG]), 1.0, BIG, ALU.subtract, ALU.mult))
                    ch.link(v.tensor_tensor(mm[:, k, :, :], t[:], src[:, :, D + H:D + 2 * H], ALU.add))
                ch.link(v.tensor_tensor(a[:], mm[:, 0, :, :], mm[:, 1, :, :], ALU.max))
                ch.link(v.tensor_tensor(a[:], a[:], mm[:, 2, :, :], ALU.max))
                for k in range(3):
                    ins = v.tensor_tensor(mm[:, k, :, :], mm[:, k, :, :], a[:], ALU.subtract)
                ins.then_inc(diff_ready, 1)
                dve.wait_ge(ex_ready, 1)
                ch.do(v.tensor_tensor(den[:], agg[:, :, D:D + H], fac[:, 0, :, :], ALU.mult))
                ch.link(v.tensor_tensor(t[:], cg[:, :, D:D + H], fac[:, 1, :, :], ALU.mult))
                ch.link(v.tensor_tensor(den[:], den[:], t[:], ALU.add))
                ch.link(v.scalar_tensor_tensor(out=den[:], in0=den[:], scalar=1e-16, in1=fac[:, 2, :, :], op0=ALU.add, op1=ALU.add))
                ch.link(v.reciprocal(t[:], den[:]))
                for k in range(3):
                    ch.do(v.tensor_tensor(fac[:, k, :, :], fac[:, k, :, :], t[:], ALU.mult))
                ch.wait()

            @block.scalar
            def _(act):
                act.wait_ge(diff_ready, 1)
                nc.scalar.activation(fac[:].rearrange("p a n h -> p (a n h)"), mm[:].rearrange("p a n h -> p (a n h)"), ACT.Exp).then_inc(ex_ready, 1)


def phase_project(nc, m, d, w, l, cagg, fac, mv, sem):
    w_ready = sem("wo_loaded")
    bias_ready = sem("bias_ready")
    in_ready = [sem(f"xs_loaded{b}") for b in range(2)]
    step = sem("weigh_step")
    sum_ready = sem("weighed")
    t_ready = sem("turned")
    t_copied = sem("turned_copied")
    o_ready = sem("projected")
    kept = sem("kept")
    sstep = sem("stats_step")
    held = sem("held")
    PER = 4
    with ExitStack() as ctx:
        sb, ps = buf_maker(nc, ctx, f"pj{l}")
        wo = sb("wo", [P, 2, D])
        bias = sb("bias", [1, 2, D])
        x = [sb(f"x{b}", [P, CT, D]) for b in range(2)]
        s1 = [sb(f"s1{b}", [P, CT, D]) for b in range(2)]
        s2 = sb("s2", [P, CT, D])
        sT = [sb(f"sT{b}", [P, 2, P]) for b in range(2)]
        st = sb("st", [P, CT, 6])
        mv1 = sb("mv1", [P, CT, 2])
        psT = [ps(f"psT{b}", [P, 2, P]) for b in range(2)]
        psO = [ps(f"psO{b}", [P, D]) for b in range(2)]
        agg = m.agg[:].rearrange("p (n k) -> p n k", k=AGG)
        cg = cagg[:].rearrange("p (n k) -> p n k", k=AGG)
        with nc.Block() as block:
            @block.sync
            def _(sp):
                sp.dma_start(wo[:], w[f"Wo{l}"].rearrange("(k p) n -> p k n", p=P)).then_inc(w_ready, 16)
                sp.dma_start(bias[:, 0, :], w[f"bo{l}"].rearrange("(o n) -> o n", o=1)).then_inc(w_ready, 16)
                sp.dma_start(bias[:, 1, :], w[f"b{l}"].rearrange("(o n) -> o n", o=1)).then_inc(w_ready, 16)
                with sp.Fori(0, NCK // 2) as it:
                    for b in range(2):
                        c = it * 2 + b
                        sp.wait_ge(sum_ready, c + 1)
                        sp.dma_start(x[b][:], d.table[bass.ds(c * (CT * P), CT * P), 0:D].rearrange("(t p) k -> p t k", p=P)).then_inc(in_ready[b], 16)

            @block.vector
            def _(dve):
                v = nc.vector
                ch = Chain(dve, step, PER)
                sch = Chain(dve, sstep, 2 * CT + 1)
                dve.wait_ge(w_ready, 48)
                v.tensor_tensor(bias[:, 0, :], bias[:, 0, :], bias[:, 1, :], ALU.add).then_inc(bias_ready, 1)
                dve.sem_inc(sum_ready, 2)

                def heads(a):
                    return a.rearrange("p n (h c) -> p n h c", c=C)

                def weigh(c, b, turn):
                    cs = bass.ds(c * CT, CT)

                    def f(k):
                        return fac[:, k, cs, :].unsqueeze(3).to_broadcast([P, CT, H, C])
                    ch.turn(c)
                    dve.wait_ge(t_ready, c * CT + CT)
                    dve.wait_ge(sum_ready, c + 2)
                    ch.do(v.tensor_tensor(heads(s1[b][:]), heads(agg[:, cs, 0:D]), f(0), ALU.mult))
                    ch.do(v.tensor_tensor(heads(s2[:]), heads(cg[:, cs, 0:D]), f(1), ALU.mult))
                    dve.wait_ge(in_ready[b], turn * 16 + 16)
                    ch.link(v.tensor_tensor(heads(x[b][:]), heads(x[b][:]), f(2), ALU.mult))
                    ch.link(v.tensor_tensor(s1[b][:], s1[b][:], s2[:], ALU.add))
                    v.tensor_tensor(s1[b][:], s1[b][:], x[b][:], ALU.add).then_inc(sum_ready, 1)
                    ch.close()

                def stats(c):
                    sch.turn(c)
                    dve.wait_ge(kept, c * CT + CT + 2)
                    dve.sem_inc(held, 1)
                    for t in range(CT):
                        sch.do(v.bn_stats(st[:, t, :], agg[:, bass.ds(c * CT + t, 1), 0:D].rearrange("p o k -> p (o k)")))
                    sch.wait()
                    dve.sem_inc(held, 1)
                    for t in range(CT):
                        sch.do(v.bn_aggr(mv1[:, t, :], st[:, t, :]))
                    sch.wait()
                    sch.link(v.tensor_copy(mv[:, bass.ds(c * (2 * CT), 2 * CT)].rearrange("p (t k) -> p t k", k=2), mv1[:]))
                    sch.close()
                weigh(0, 0, 0)
                with dve.Fori(0, NCK // 2 - 1) as it:
                    weigh(it * 2 + 1, 1, it)
                    stats(it * 2)
                    weigh(it * 2 + 2, 0, it + 1)
                    stats(it * 2 + 1)
                weigh(NCK - 1, 1, NCK // 2 - 1)
                stats(NCK - 2)
                stats(NCK - 1)

            @block.tensor
            def _(pe):
                pe.wait_ge(bias_ready, 1)
                pe.sem_inc(t_ready, 2 * CT)
                pe.sem_inc(o_ready, 2)
                with pe.Fori(0, NCK // 2) as it:
                    for b in range(2):
                        c = it * 2 + b
                        pe.wait_ge(sum_ready, c + 3)
                        for turned, t in CHUNK_ORDER:
                            q = (b * CT + t) % 2
                            n = c * CT + t
                            if turned:
                                pe.wait_ge(t_copied, n + 1)
                                for k in range(2):
                                    ins = nc.tensor.transpose(psT[q][:, k, :], s1[b][:, t, k * P:(k + 1) * P], m.ident[:])
                                ins.then_inc(t_ready, 1)
                            else:
                                pe.wait_ge(t_copied, n + 3)
                                pe.wait_ge(kept, n + 1)
                                nc.tensor.matmul(psO[q][:], m.ones[0:1, :], bias[0:1, 0, :], start=True, stop=False)
                                for k in range(2):
                                    ins = nc.tensor.matmul(psO[q][:], sT[q][:, k, :], wo[:, k, :], start=False, stop=(k == 1))
                                ins.then_inc(o_ready, 1)

            @block.scalar
            def _(act):
                act.sem_inc(t_copied, 2)
                act.sem_inc(kept, 2)
                with act.Fori(0, NCK // 2) as it:
                    for b in range(2):
                        c = it * 2 + b
                        for turned, t in CHUNK_ORDER:
                            q = (b * CT + t) % 2
                            n = c * CT + t
                            if turned:
                                act.wait_ge(t_ready, n + 1 + 2 * CT)
                                act.wait_ge(o_ready, n + 1)
                                nc.scalar.copy(sT[q][:], psT[q][:]).then_inc(t_copied, 1)
                            else:
                                act.wait_ge(o_ready, n + 3)
                                nc.scalar.copy(m.agg[:, bass.ds(n * AGG, D)], psO[q][:]).then_inc(kept, 1)


def phase_norm(nc, m, d, w, l, h_dram, mv, bn, sem):
    w_ready = sem("rows_loaded")
    in_ready = [sem(f"h_loaded{b}") for b in range(2)]
    step = sem("norm_step")
    eps_ready = sem("var_eps")
    sd_ready = sem("deviation")
    y_step = sem("y_step")
    y_ready = sem("y_ready")
    sq_ready = sem("squared")
    summed = sem("summed")
    var_ready = sem("bn_var")
    bsd_ready = sem("bn_deviation")
    PER = 3
    with ExitStack() as ctx:
        sb, ps = buf_maker(nc, ctx, f"nm{l}")
        par = sb("par", [P, 4, D])
        h = [sb(f"h{b}", [P, CT, D]) for b in range(2)]
        sd = sb("sd", [P, NT])
        rs = sb("rs", [P, NT])
        sq = [sb(f"sq{b}", [P, CT, D]) for b in range(2)]
        mean = sb("mean", [P, D])
        var = sb("var", [P, D])
        psS = [ps(f"psS{b}", [P, D]) for b in range(2)]
        mvv = mv[:].rearrange("p (n k) -> p n k", k=2)
        agg = m.agg[:].rearrange("p (n k) -> p n k", k=AGG)

        def chunks(eng, body):
            body(0, 0, 0)
            body(1, 1, 0)
            with eng.Fori(1, NCK // 2 - 1) as it:
                for b in range(2):
                    body(it * 2 + b, b, it)
            body(NCK - 2, 0, NCK // 2 - 1)
            body(NCK - 1, 1, NCK // 2 - 1)
        with nc.Block() as block:
            @block.sync
            def _(sp):
                for k, name in enumerate((f"lg{l}", f"lb{l}", f"bng{l}", f"bnb{l}")):
                    sp.dma_start(par[:, k, :], w[name].rearrange("(o n) -> o n", o=1).to_broadcast([P, D])).then_inc(w_ready, 16)
                with sp.Fori(0, NCK // 2) as it:
                    for b in range(2):
                        c = it * 2 + b
                        sp.wait_ge(y_ready, c + 1)
                        sp.dma_start(h[b][:], chunk_of(h_dram, c)).then_inc(in_ready[b], 16)

            @block.scalar
            def _(act):
                act.wait_ge(eps_ready, 1)
                nc.scalar.activation(sd[:], rs[:], ACT.Sqrt).then_inc(sd_ready, 1)
                with act.Fori(0, NCK // 2) as it:
                    for b in range(2):
                        c = it * 2 + b
                        act.wait_ge(y_ready, c + 3)
                        act.wait_ge(summed, c + 1)
                        nc.scalar.activation(sq[b][:], agg[:, bass.ds(c * CT, CT), 0:D], ACT.Square).then_inc(sq_ready, 1)
                act.wait_ge(var_ready, 1)
                nc.scalar.activation(var[:], var[:], ACT.Sqrt).then_inc(bsd_ready, 1)

            @block.tensor
            def _(pe):
                pe.sem_inc(summed, 2)

                def sums(c, b, turn):
                    pe.wait_ge(sq_ready, c + 1)
                    for t in range(CT):
                        n = c * CT + t
                        first = isinstance(n, int) and n == 0
                        last = isinstance(n, int) and n == NT - 1
                        mask = m.node_mask[:, 1 if last else 0, :]
                        nc.tensor.matmul(psS[0][:], mask, m.agg[:, bass.ds(n * AGG, D)], start=first, stop=last, skip_group_check=True)
                        ins = nc.tensor.matmul(psS[1][:], mask, sq[b][:, t, :], start=first, stop=last, skip_group_check=True)
                    ins.then_inc(summed, 1)
                chunks(pe, sums)

            @block.vector
            def _(dve):
                v = nc.vector
                ch = Chain(dve, step)
                ych = Chain(dve, y_step, PER)
                dve.sem_inc(y_ready, 2)
                v.tensor_scalar(rs[:], mvv[:, :, 1], EPS, None, ALU.add).then_inc(eps_ready, 1)
                dve.wait_ge(sd_ready, 1)
                ch.link(v.reciprocal(rs[:], sd[:]))
                dve.wait_ge(w_ready, 64)
                with dve.Fori(0, NCK // 2) as it:
                    for b in range(2):
                        c = it * 2 + b
                        ych.turn(c)
                        y = agg[:, bass.ds(c * CT, CT), 0:D]
                        for t in range(CT):
                            n = c * CT + t
                            yt = m.agg[:, bass.ds(n * AGG, D)]
                            ins = v.tensor_scalar(yt, yt, mvv[:, bass.ds(n, 1), 0], rs[:, bass.ds(n, 1)], ALU.subtract, ALU.mult)
                        ych.link(ins)
                        ych.link(v.tensor_tensor(y, y, par[:, 0, :].unsqueeze(1).to_broadcast([P, CT, D]), ALU.mult))
                        dve.wait_ge(in_ready[b], it * 16 + 16)
                        ych.link(v.tensor_tensor(y, y, par[:, 1, :].unsqueeze(1).to_broadcast([P, CT, D]), ALU.add))
                        v.tensor_tensor(y, y, h[b][:], ALU.add).then_inc(y_ready, 1)
                        ych.close()
                dve.wait_ge(summed, NCK + 2)
                ch.do(v.tensor_scalar(mean[:], psS[0][:], 1.0 / N_NODES, None, ALU.mult))
                ch.link(v.tensor_scalar(var[:], psS[1][:], 1.0 / N_NODES, None, ALU.mult))
                ch.link(v.tensor_tensor(bn[:, 0, :], mean[:], mean[:], ALU.mult))
                ch.link(v.tensor_tensor(var[:], var[:], bn[:, 0, :], ALU.subtract))
                v.tensor_scalar(var[:], var[:], 0.0, EPS, ALU.max, ALU.add).then_inc(var_ready, 1)
                dve.wait_ge(bsd_ready, 1)
                ch.link(v.reciprocal(var[:], var[:]))
                ch.link(v.tensor_tensor(bn[:, 0, :], var[:], par[:, 2, :], ALU.mult))
                ch.link(v.tensor_tensor(mean[:], mean[:], bn[:, 0, :], ALU.mult))
                ch.link(v.tensor_tensor(bn[:, 1, :], par[:, 3, :], mean[:], ALU.subtract))


def phase_rows(nc, m, d, kind, bn, weights, table, width, sem):
    made, loads = kind != "x", kind != "h1"
    total = weights.shape[2]
    in_ready = [sem(f"x_loaded{b}") for b in range(2)]
    step = sem("apply_step")
    y_done = sem("rows_ready")
    y_stored = [sem(f"rows_stored{b}") for b in range(2)]
    t_ready = sem("turned")
    t_copied = sem("turned_copied")
    o_ready = sem("product_ready")
    o_copied = sem("product_copied")
    stored = [sem(f"table_stored{b}") for b in range(2)]
    eps_ready = sem("var_eps")
    sd_ready = sem("deviation")
    held = sem("held")
    PER = NORM_STEPS + 4 if kind == "x1" else 2
    with ExitStack() as ctx:
        sb, ps = buf_maker(nc, ctx, f"rw{kind}")
        y = [sb(f"y{b}", [P, CT, D]) for b in range(2)]
        x = [sb(f"x{b}", [P, CT, D]) for b in range(2)] if kind == "x1" else y
        row = [sb(f"row{b}", [P, CT, width]) for b in range(2)]
        yT = [sb(f"yT{b}", [P, 2, P]) for b in range(2)]
        st = sb("st", [P, CT, 6])
        mv = sb("mv", [P, CT, 2])
        sd = sb("sd", [P, 2, CT])
        psT = [ps(f"psT{b}", [P, 2, P]) for b in range(2)]
        psO = [ps(f"psO{b}", [P, total]) for b in range(2)]
        with nc.Block() as block:
            @block.sync
            def _(sp):
                for b in range(2):
                    sp.sem_inc(y_stored[b], 16)
                    sp.sem_inc(stored[b], 16)

                def load(c, b, turn):
                    if kind == "x":
                        sp.wait_ge(t_ready, c * CT + CT)
                    elif loads:
                        sp.wait_ge(y_done, c + 1)
                    if loads:
                        sp.dma_start(x[b][:], chunk_of(d.x, c)).then_inc(in_ready[b], 16)

                def store(c, b, turn):
                    if made:
                        sp.wait_ge(y_done, c + 3)
                        sp.dma_start(chunk_of(d.h, c), y[b][:]).then_inc(y_stored[b], 16)
                    sp.wait_ge(o_copied, c * CT + CT + 2)
                    sp.dma_start(table[bass.ds(c * (CT * P), CT * P), :].rearrange("(t p) k -> p t k", p=P), row[b][:]).then_inc(stored[b], 16)
                load_and_store(sp, load, store, NCK)
                for b in range(2):
                    if made:
                        sp.wait_ge(y_stored[b], 16 * (NCK // 2 + 1))
                    sp.wait_ge(stored[b], 16 * (NCK // 2 + 1))

            @block.vector
            def _(dve):
                if not made:
                    return
                v = nc.vector
                agg = m.agg[:].rearrange("p (n k) -> p n k", k=AGG)
                ch = Chain(dve, step, PER)
                dve.sem_inc(y_done, 2)

                def bc(k):
                    return bn[:, k, :].unsqueeze(1).to_broadcast([P, CT, D])
                with dve.Fori(0, NCK // 2) as it:
                    for b in range(2):
                        c = it * 2 + b
                        ch.turn(c)
                        dve.wait_ge(y_stored[b], it * 16 + 16)
                        dve.wait_ge(t_ready, c * CT + CT)
                        ch.link(v.tensor_tensor(y[b][:], agg[:, bass.ds(c * CT, CT), 0:D], bc(0), ALU.mult))
                        ch.link(v.tensor_tensor(y[b][:], y[b][:], bc(1), ALU.add))
                        if kind == "h1":
                            v.tensor_scalar(y[b][:], y[b][:], 0.0, None, ALU.max).then_inc(y_done, 1)
                            ch.close()
                            continue
                        dve.wait_ge(in_ready[b], it * 16 + 16)
                        ch.link(v.tensor_tensor(y[b][:], y[b][:], x[b][:], ALU.add))
                        ch.link(v.scalar_tensor_tensor(out=y[b][:], in0=y[b][:], scalar=0.0, in1=x[b][:], op0=ALU.max, op1=ALU.add))
                        norm_chunk(v, dve, ch, y[b], st, mv, sd, eps_ready, sd_ready, y_done, held, c)
                        ch.close()

            @block.tensor
            def _(pe):
                pe.sem_inc(t_ready, 2 * CT)
                pe.sem_inc(o_ready, 2)
                with pe.Fori(0, NCK // 2) as it:
                    for b in range(2):
                        c = it * 2 + b
                        if made:
                            pe.wait_ge(y_done, c + 3)
                        else:
                            pe.wait_ge(in_ready[b], it * 16 + 16)
                        for turned, t in CHUNK_ORDER:
                            q = (b * CT + t) % 2
                            n = c * CT + t
                            if turned:
                                pe.wait_ge(t_copied, n + 1)
                                for k in range(2):
                                    ins = nc.tensor.transpose(psT[q][:, k, :], y[b][:, t, k * P:(k + 1) * P], m.ident[:])
                                ins.then_inc(t_ready, 1)
                            else:
                                pe.wait_ge(t_copied, n + 3)
                                pe.wait_ge(o_copied, n + 1)
                                for k in range(2):
                                    ins = nc.tensor.matmul(psO[q][:], yT[q][:, k, :], weights[:, k, :], start=(k == 0), stop=(k == 1))
                                ins.then_inc(o_ready, 1)

            @block.scalar
            def _(act):
                act.sem_inc(t_copied, 2)
                act.sem_inc(o_copied, 2)
                with act.Fori(0, NCK // 2) as it:
                    for b in range(2):
                        c = it * 2 + b
                        if kind == "x1":
                            act.wait_ge(eps_ready, c + 1)
                            nc.scalar.activation(sd[:, 1, :], sd[:, 0, :], ACT.Sqrt).then_inc(sd_ready, 1)
                        act.wait_ge(stored[b], it * 16 + 16)
                        for turned, t in CHUNK_ORDER:
                            q = (b * CT + t) % 2
                            n = c * CT + t
                            if turned:
                                act.wait_ge(t_ready, n + 1 + 2 * CT)
                                act.wait_ge(o_ready, n + 1)
                                nc.scalar.copy(yT[q][:], psT[q][:]).then_inc(t_copied, 1)
                            else:
                                act.wait_ge(o_ready, n + 3)
                                ins = nc.scalar.copy(row[b][:, t, :], psO[q][:, 0:width])
                                if total > width:
                                    ins = nc.scalar.copy(m.a_ij[:, bass.ds(n * 2 * H, 2 * H)], psO[q][:, D:D + 2 * H])
                                ins.then_inc(o_copied, 1)


def phase_conv_weights(nc, m, w, sem):
    loaded = sem("weights_loaded")
    ready = sem("joined")
    step = sem("copied")
    with ExitStack() as ctx:
        sb, ps = buf_maker(nc, ctx, "cw")
        wn = sb("wn", [FILT, D])
        l1T = sb("l1T", [FILT, FILT])
        l2 = sb("l2", [FILT, FILT])
        b2 = sb("b2", [FILT, 1])
        wmT = sb("wmT", [FILT, D])
        psI = ps("psI", [P, 2, FILT])
        psO = ps("psO", [FILT, D])
        psB = ps("psB", [1, D])
        with nc.Block() as block:
            @block.sync
            def _(sp):
                sp.dma_start(wn[:], w["c_W_node_to_message"]).then_inc(loaded, 16)
                sp.dma_start(l1T[:], w["c_W_lin1_T"]).then_inc(loaded, 16)
                sp.dma_start(l2[:], w["c_W_lin2"]).then_inc(loaded, 16)
                sp.dma_start(b2[:], w["c_b_lin2"].rearrange("(k o) -> k o", o=1)).then_inc(loaded, 16)
                sp.dma_start(wmT[:], w["c_W_message_to_node_T"]).then_inc(loaded, 16)
                sp.dma_start(m.w_radial[:], w["c_W_radial_to_message_T"]).then_inc(loaded, 16)

            @block.tensor
            def _(pe):
                pe.wait_ge(loaded, 6 * 16)
                for k in range(2):
                    nc.tensor.matmul(psI[:, k, :], wn[:, k * P:(k + 1) * P], l1T[:], start=True, stop=True)
                nc.tensor.matmul(psB[:], b2[:], wmT[:], start=True, stop=True)
                nc.tensor.matmul(psO[:], l2[:], wmT[:], start=True, stop=True).then_inc(ready, 1)

            @block.vector
            def _(dve):
                ch = Chain(dve, step)
                dve.wait_ge(ready, 1)
                ch.do(nc.vector.tensor_copy(m.w_conv_in[:], psI[:]))
                ch.do(nc.vector.tensor_copy(m.w_conv_out[:], psO[:]))
                ch.do(nc.vector.tensor_copy(m.b_conv_out[:], psB[:]))
                dve.wait_ge(loaded, 6 * 16)
                ch.wait()


def phase_cutoff(nc, m, sem):
    step = sem("cut_step")
    arg_ready = sem("argument")
    sin_ready = sem("sine")
    turn = 2.0 * np.pi
    with ExitStack() as ctx:
        sb, _ = buf_maker(nc, ctx, "cut")
        u = sb("u", [P, S])
        r = sb("r", [P, S])
        whole = sb("whole", [P, S], I32)
        with nc.Block() as block:
            @block.vector
            def _(dve):
                ch = Chain(dve, step)
                v = nc.vector
                ch.do(v.memset(m.cut[:, S:S + 2 * GROUP], 0.0))
                ch.link(v.tensor_scalar(u[:], m.w_slot[:, 0:S], 0.5 / CUTOFF, None, ALU.mult))
                ch.link(v.tensor_copy(whole[:], u[:]))
                ch.link(v.tensor_copy(r[:], whole[:]))
                ch.link(v.tensor_tensor(r[:], u[:], r[:], ALU.subtract))
                ch.link(v.scalar_tensor_tensor(out=u[:], in0=r[:], scalar=-1.0, in1=r[:], op0=ALU.mult, op1=ALU.max))
                ch.link(v.tensor_scalar(r[:], u[:], -1.0, 1.0, ALU.mult, ALU.add))
                ch.link(v.tensor_tensor(r[:], u[:], r[:], ALU.min))
                v.tensor_scalar(u[:], r[:], -turn, turn / 4, ALU.mult, ALU.add).then_inc(arg_ready, 1)
                dve.wait_ge(sin_ready, 1)
                ch.link(v.tensor_scalar(m.cut[:, 0:S], r[:], 0.5, 0.5, ALU.mult, ALU.add))

            @block.scalar
            def _(act):
                act.wait_ge(arg_ready, 1)
                nc.scalar.activation(r[:], u[:], ACT.Sin).then_inc(sin_ready, 1)


def phase_sum_messages(nc, m, d, kind, table, slot_rows, sem):
    K = FILT if kind == "conv" else D + 1
    WIDE = FILT if kind == "conv" else D
    BANKS = 4
    x_ready = [sem(f"rows_gathered{b}") for b in range(SETS)]
    idx_ready = sem("index_ready")
    idx_pass = sem("index_pass")
    hot_ready = sem("onehot_ready")
    attr_ready = [sem(f"attr_loaded{b}") for b in range(2)]
    f_ready = sem("filters_ready")
    prod_ready = sem("products")
    msg_ready = sem("messages")
    o_ready = sem("slot_sums")
    acc_done = sem("added")
    zeroed = sem("zeroed")
    NTURN = NG // SETS
    with ExitStack() as ctx:
        sb, ps = buf_maker(nc, ctx, kind)
        x = [sb(f"x{b}", [P, GROUP, K]) for b in range(SETS)]
        idx = [sb(f"idx{b}", [P, GROUP], I32) for b in range(SETS)]
        hot = [sb(f"hot{b}", [P, GROUP, P]) for b in range(2)]
        psO = [ps(f"psO{b}", [P, 512]) for b in range(BANKS)]
        if kind == "conv":
            attr = [sb(f"attr{b}", [RADIAL, GROUP, P]) for b in range(2)]
            prod = sb("prod", [P, GROUP, K])
            msg = [sb(f"msg{b}", [P, GROUP, K]) for b in range(2)]
            psF = [ps(f"psF{b}", [P, GROUP, K]) for b in range(2)]
        with nc.Block() as block:
            @block.gpsimd
            def _(pool):
                def index(g, b, turn):
                    if not (isinstance(turn, int) and turn == 0):
                        pool.wait_ge(x_ready[b], turn * (16 * GROUP))
                        pool.sem_inc(idx_pass, 1)
                    nc.gpsimd.tensor_copy(idx[b][:], slot_rows[:, bass.ds(g * GROUP, GROUP)]).then_inc(idx_ready, 1)

                def gather(g, b, turn, reused=True, last=False):
                    if reused and kind == "conv":
                        pool.wait_ge(prod_ready, g - SETS + 3)
                    elif reused:
                        pool.wait_ge(o_ready, (g - SETS + 1) * GROUP)
                    else:
                        pool.wait_ge(zeroed, 2)
                    pool.wait_ge(idx_ready, g + 1)
                    pool.sem_inc(idx_pass, 1)
                    for j in range(GROUP):
                        if j == GROUP // 2 and not last:
                            index(g + 1, (b + 1) % SETS, turn + 1 if b == SETS - 1 else turn)
                        pool.indirect_dma_start(x[b][:, j, 0:WIDE], None, table,
                                                bass.IndirectOffsetOnAxis(ap=idx[b][:, j:j + 1], axis=0)).then_inc(x_ready[b], 16)
                index(0, 0, 0)
                for b in range(SETS):
                    gather(b, b, 0, reused=False)
                with pool.Fori(1, NTURN) as it:
                    for b in range(SETS):
                        gather(it * SETS + b, b, it)
                gather(NG, 0, NTURN, last=True)
                pool.wait_ge(x_ready[0], 16 * GROUP * (NTURN + 1))

            if kind == "conv":
                @block.sync
                def _(sp):
                    regs = [sp.alloc_register(f"sp_t_{j}") for j in range(GROUP)]

                    def load_attr(g, b, pair):
                        sp.load(regs, m.trow[0:1, bass.ds(g * GROUP, GROUP)])
                        ts = [sp.snap(r, min_val=0, max_val=TP - 1) for r in regs]
                        sp.wait_ge(f_ready, g + 1)
                        for j in range(GROUP):
                            sp.dma_start(attr[b][:, j, :], d.attr12_T[:, bass.ds(ts[j] * P, P)]).then_inc(attr_ready[b], 16)
                    with sp.Fori(0, NG // 2) as it:
                        for b in range(2):
                            load_attr(it * 2 + b, b, it)
                    load_attr(NG, 0, NG // 2)

            @block.tensor
            def _(pe):
                if kind == "conv":
                    pe.sem_inc(f_ready, 2)

                def filters(g, b, turn):
                    pair = turn * 2 + b // 2
                    pe.wait_ge(attr_ready[b % 2], pair * (16 * GROUP) + 16 * GROUP)
                    pe.wait_ge(prod_ready, g + 1)
                    for j in range(GROUP):
                        ins = nc.tensor.matmul(psF[b % 2][:, j, :], attr[b % 2][:, j, :], m.w_radial[:], start=True, stop=True)
                    ins.then_inc(f_ready, 1)

                def sums(g, b, turn, j):
                    i = g * GROUP + j
                    if j == 0:
                        pe.wait_ge(hot_ready, g + 1)
                        if kind == "conv":
                            pe.wait_ge(msg_ready, g + 1)
                        else:
                            pe.wait_ge(x_ready[b], turn * (16 * GROUP) + 16 * GROUP)
                    pe.wait_ge(acc_done, i + 1)
                    rhs = msg[b % 2] if kind == "conv" else x[b]
                    nc.tensor.matmul(psO[j % BANKS][:, 0:K], hot[b % 2][:, j, :], rhs[:, j, :], start=True, stop=True).then_inc(o_ready, 1)
                if kind == "conv":
                    filters(0, 0, 0)
                with pe.Fori(0, NTURN) as it:
                    for b in range(SETS):
                        b1 = (b + 1) % SETS
                        if kind == "conv":
                            filters(it * SETS + b + 1, b1, it + 1 if b1 == 0 else it)
                        for j in range(GROUP):
                            sums(it * SETS + b, b, it, j)
                pe.wait_ge(o_ready, S)

            @block.vector
            def _(dve):
                regs = [dve.alloc_register(f"dve_{kind}_{j}") for j in range(GROUP)]
                nc.vector.memset(m.sums[:], 0.0).then_inc(zeroed, 1)
                if kind == "rel":
                    for b in range(SETS - 1):
                        nc.vector.memset(x[b][:, :, D:D + 1], 1.0)
                    nc.vector.memset(x[SETS - 1][:, :, D:D + 1], 1.0).then_inc(zeroed, 1)
                else:
                    dve.sem_inc(zeroed, 1)
                    dve.sem_inc(prod_ready, 2)
                dve.sem_inc(acc_done, BANKS)
                dve.wait_ge(zeroed, 2)

                def onehots(g, b):
                    at = bass.ds(g * GROUP, GROUP)
                    nc.vector.tensor_tensor(hot[b % 2][:], m.iota[:, 0:P].unsqueeze(1).to_broadcast([P, GROUP, P]),
                                            m.loc[:, at].unsqueeze(2).to_broadcast([P, GROUP, P]), ALU.is_equal).then_inc(hot_ready, 1)

                def messages(g, b, turn):
                    at = bass.ds(g * GROUP, GROUP)
                    dve.wait_ge(x_ready[b], turn * (16 * GROUP) + 16 * GROUP)
                    dve.wait_ge(f_ready, g + 3)
                    nc.vector.tensor_tensor(prod[:], psF[b % 2][:], x[b][:], ALU.mult).then_inc(prod_ready, 1)
                    dve.wait_ge(prod_ready, g + 3)
                    nc.vector.tensor_tensor(msg[b % 2][:], prod[:], m.cut[:, at].unsqueeze(2).to_broadcast([P, GROUP, K]), ALU.mult).then_inc(msg_ready, 1)
                    dve.wait_ge(msg_ready, g + 1)

                def add(g, b, j, ns):
                    i = g * GROUP + j
                    dve.wait_ge(o_ready, i + 1)
                    dve.wait_ge(acc_done, i + BANKS)
                    to = m.sums[:, bass.ds(ns[j] * K, K)]
                    nc.vector.tensor_tensor(to, to, psO[j % BANKS][:, 0:K], ALU.add).then_inc(acc_done, 1)
                onehots(0, 0)
                if kind == "conv":
                    messages(0, 0, 0)
                with dve.Fori(0, NTURN) as it:
                    for b in range(SETS):
                        g = it * SETS + b
                        b1 = (b + 1) % SETS
                        dve.load(regs, m.nrow[0:1, bass.ds(g * GROUP, GROUP)])
                        ns = [dve.snap(r, min_val=0, max_val=NT - 1) for r in regs]
                        onehots(g + 1, b1)
                        for j in range(GROUP // 2):
                            add(g, b, j, ns)
                        if kind == "conv":
                            messages(g + 1, b1, it + 1 if b1 == 0 else it)
                        for j in range(GROUP // 2, GROUP):
                            add(g, b, j, ns)
                dve.wait_ge(acc_done, S + BANKS)


def phase_conv_out(nc, m, d, sem):
    in_ready = [sem(f"x_loaded{b}") for b in range(2)]
    a_ready = sem("sums_copied")
    t_ready = sem("sumsT_ready")
    t_copied = sem("sumsT_copied")
    o_ready = sem("out_ready")
    taken = sem("out_taken")
    y_done = sem("y_done")
    step = sem("norm_step")
    stored = [sem(f"h_stored{b}") for b in range(2)]
    eps_ready = sem("var_eps")
    sd_ready = sem("deviation")
    held = sem("held")
    with ExitStack() as ctx:
        sb, ps = buf_maker(nc, ctx, "co")
        x = [sb(f"x{b}", [P, CT, D]) for b in range(2)]
        y = [sb(f"y{b}", [P, CT, D]) for b in range(2)]
        a = [sb(f"a{b}", [P, FILT]) for b in range(2)]
        aT = [sb(f"aT{b}", [FILT, P]) for b in range(2)]
        st = sb("st", [P, CT, 6])
        mv = sb("mv", [P, CT, 2])
        sd = sb("sd", [P, 2, CT])
        psT = [ps(f"psT{b}", [FILT, P]) for b in range(2)]
        psO = [ps(f"psO{b}", [P, D]) for b in range(2)]
        with nc.Block() as block:
            @block.sync
            def _(sp):
                for b in range(2):
                    sp.sem_inc(stored[b], 16)

                def load(c, b, turn):
                    sp.wait_ge(y_done, c + 1)
                    sp.dma_start(x[b][:], chunk_of(d.h, c)).then_inc(in_ready[b], 16)

                def store(c, b, turn):
                    sp.wait_ge(y_done, c + 3)
                    sp.dma_start(chunk_of(d.h2, c), y[b][:]).then_inc(stored[b], 16)
                load_and_store(sp, load, store, NCK)
                for b in range(2):
                    sp.wait_ge(stored[b], 16 * (NCK // 2 + 1))

            @block.tensor
            def _(pe):
                pe.sem_inc(t_ready, 2)
                pe.sem_inc(o_ready, 2)
                with pe.Fori(0, NCK // 2) as it:
                    for turned, t in PAIR_ORDER:
                        n = it * (2 * CT) + t
                        q = t % 2
                        if turned:
                            pe.wait_ge(a_ready, n + 1)
                            pe.wait_ge(t_copied, n + 1)
                            nc.tensor.matmul(psT[q][:], a[q][:], m.ident[:], start=True, stop=True).then_inc(t_ready, 1)
                        else:
                            pe.wait_ge(t_copied, n + 3)
                            pe.wait_ge(taken, n + 1)
                            nc.tensor.matmul(psO[q][:], m.ones[0:1, :], m.b_conv_out[:], start=True, stop=False)
                            nc.tensor.matmul(psO[q][:], aT[q][:], m.w_conv_out[:], start=False, stop=True).then_inc(o_ready, 1)

            @block.scalar
            def _(act):
                act.sem_inc(t_copied, 2)

                def copies(n, q):
                    act.wait_ge(t_ready, n + 1)
                    nc.scalar.copy(a[q][:], m.sums[:, bass.ds(n * FILT, FILT)]).then_inc(a_ready, 1)
                    act.wait_ge(t_ready, n + 3)
                    act.wait_ge(o_ready, n + 1)
                    nc.scalar.copy(aT[q][:], psT[q][:]).then_inc(t_copied, 1)

                def root(c):
                    act.wait_ge(eps_ready, c + 1)
                    nc.scalar.activation(sd[:, 1, :], sd[:, 0, :], ACT.Sqrt).then_inc(sd_ready, 1)
                for t in range(CT + 1):
                    copies(t, t % 2)
                with act.Fori(0, NCK // 2 - 1) as it:
                    for b in range(2):
                        root(it * 2 + b)
                        for t in range(CT + 1, 2 * CT + 1):
                            copies((it * 2 + b) * CT + t, (b * CT + t) % 2)
                root(NCK - 2)
                for t in range(NT - CT + 1, NT):
                    copies(t, t % 2)
                root(NCK - 1)

            @block.vector
            def _(dve):
                v = nc.vector
                ch = Chain(dve, step, NORM_STEPS)
                dve.sem_inc(taken, 2)
                dve.sem_inc(y_done, 2)
                with dve.Fori(0, NCK // 2) as it:
                    for b in range(2):
                        c = it * 2 + b
                        ch.turn(c)
                        dve.wait_ge(in_ready[b], it * 16 + 16)
                        dve.wait_ge(stored[b], it * 16 + 16)
                        for t in range(CT):
                            n = c * CT + t
                            q = (b * CT + t) % 2
                            dve.wait_ge(o_ready, n + 3)
                            v.tensor_tensor(y[b][:, t, :], psO[q][:], x[b][:, t, :], ALU.add).then_inc(taken, 1)
                        dve.wait_ge(taken, c * CT + CT + 2)
                        norm_chunk(v, dve, ch, y[b], st, mv, sd, eps_ready, sd_ready, y_done, held, c)
                        ch.close()
                dve.wait_ge(y_done, NCK + 2)


def phase_rel_tables(nc, m, d, w, sem):
    w_ready = sem("weights_loaded")
    in_ready = [sem(f"h_loaded{b}") for b in range(2)]
    t_ready = sem("hT_ready")
    t_copied = sem("hT_copied")
    o_ready = sem("product_ready")
    o_copied = [sem(f"product_copied{b}") for b in range(2)]
    base_ready = sem("base_ready")
    base_done = sem("base_done")
    stored = [sem(f"rows_stored{b}") for b in range(2)]
    base_stored = [sem(f"base_stored{b}") for b in range(2)]
    PAIRS = N_REL // 2
    with ExitStack() as ctx:
        sb, ps = buf_maker(nc, ctx, "rt")
        wr = sb("wr", [P, 2, N_REL, D])
        ws = sb("ws", [P, 2, D])
        bs = sb("bs", [1, D])
        h = [sb(f"h{b}", [P, D]) for b in range(2)]
        hT = [sb(f"hT{b}", [P, 2, P]) for b in range(2)]
        rows = [sb(f"rows{b}", [P, N_REL, D]) for b in range(2)]
        base = [sb(f"base{b}", [P, D]) for b in range(2)]
        psT = ps("psT", [P, 2, P])
        psB = ps("psB", [P, D])
        psO = [ps(f"psO{q}", [P, 2, D]) for q in range(PAIRS)]
        with nc.Block() as block:
            @block.sync
            def _(sp):
                sp.dma_start(bs[:], w["r_sl_b"].rearrange("(o n) -> o n", o=1)).then_inc(w_ready, 16)
                sp.dma_start(ws[:], w["r_sl_w_T"].rearrange("(k p) n -> p k n", p=P)).then_inc(w_ready, 16)
                for k in range(2):
                    sp.dma_start(wr[:, k, :, :], w["r_weight"][:, k * P:(k + 1) * P, :].rearrange("r p n -> p r n")).then_inc(w_ready, 16)
                for b in range(2):
                    sp.sem_inc(stored[b], 16)
                    sp.sem_inc(base_stored[b], 16)

                def load(n, b, turn):
                    sp.wait_ge(base_done, n + 1)
                    sp.dma_start(h[b][:], tile_of(d.h2, n)).then_inc(in_ready[b], 16)

                def store(n, b, turn):
                    sp.wait_ge(base_done, n + 3)
                    sp.dma_start(tile_of(d.base, n), base[b][:]).then_inc(base_stored[b], 16)
                    for e in range(2):
                        sp.wait_ge(o_copied[e], n * 2 + 4)
                    sp.dma_start(d.rel_table.rearrange("(r n) k -> n r k", r=N_REL)[bass.ds(n * P, P), :, :], rows[b][:]).then_inc(stored[b], 16)
                load_and_store(sp, load, store, NT)
                for b in range(2):
                    sp.wait_ge(stored[b], 16 * (NT // 2 + 1))
                    sp.wait_ge(base_stored[b], 16 * (NT // 2 + 1))

            @block.tensor
            def _(pe):
                pe.wait_ge(w_ready, 4 * 16)
                pe.sem_inc(t_ready, 1)
                pe.sem_inc(o_ready, 1)
                pe.sem_inc(base_ready, 1)
                with pe.Fori(0, NT // 2) as it:
                    for b in range(2):
                        n = it * 2 + b
                        pe.wait_ge(in_ready[b], it * 16 + 16)
                        pe.wait_ge(t_copied, n + 1)
                        for k in range(2):
                            ins = nc.tensor.transpose(psT[:, k, :], h[b][:, k * P:(k + 1) * P], m.ident[:])
                        ins.then_inc(t_ready, 1)
                        pe.wait_ge(t_copied, n + 2)
                        pe.wait_ge(base_done, n + 2)
                        nc.tensor.matmul(psB[:], m.ones[0:1, :], bs[:], start=True, stop=False)
                        for k in range(2):
                            ins = nc.tensor.matmul(psB[:], hT[b][:, k, :], ws[:, k, :], start=False, stop=(k == 1))
                        ins.then_inc(base_ready, 1)
                        for q in range(PAIRS):
                            pe.wait_ge(o_copied[q % 2], n * 2 + q // 2 + 1)
                            for k in range(2):
                                ins = nc.tensor.matmul(psO[q][:].rearrange("p a n -> p (a n)"), hT[b][:, k, :],
                                                       wr[:, k, 2 * q:2 * q + 2, :].rearrange("p a n -> p (a n)"), start=(k == 0), stop=(k == 1))
                            ins.then_inc(o_ready, 1)

            def copy_pair(eng, copy, n, b, turn, q):
                eng.wait_ge(o_ready, n * PAIRS + q + 2)
                copy(rows[b][:, 2 * q:2 * q + 2, :], psO[q][:]).then_inc(o_copied[q % 2], 1)

            @block.scalar
            def _(act):
                act.sem_inc(t_copied, 1)
                act.sem_inc(o_copied[1], 2)
                with act.Fori(0, NT // 2) as it:
                    for b in range(2):
                        n = it * 2 + b
                        act.wait_ge(t_ready, n + 2)
                        act.wait_ge(o_copied[1], n * 2 + 1)
                        nc.scalar.copy(hT[b][:], psT[:]).then_inc(t_copied, 1)
                        act.wait_ge(stored[b], it * 16 + 16)
                        copy_pair(act, nc.scalar.copy, n, b, it, 1)
                        copy_pair(act, nc.scalar.copy, n, b, it, 3)

            @block.vector
            def _(dve):
                dve.sem_inc(base_done, 2)
                dve.sem_inc(o_copied[0], 2)
                with dve.Fori(0, NT // 2) as it:
                    for b in range(2):
                        n = it * 2 + b
                        dve.wait_ge(base_ready, n + 2)
                        dve.wait_ge(base_stored[b], it * 16 + 16)
                        nc.vector.tensor_tensor(base[b][:], psB[:], h[b][:], ALU.add).then_inc(base_done, 1)
                        dve.wait_ge(stored[b], it * 16 + 16)
                        copy_pair(dve, nc.vector.tensor_copy, n, b, it, 0)
                        copy_pair(dve, nc.vector.tensor_copy, n, b, it, 2)


def chunk_of(dram, c):
    return dram[bass.ds(c * CT, CT), :, :].rearrange("t p k -> p t k")


def norm_chunk(v, dve, ch, y, st, mv, sd, eps_ready, sd_ready, done, held, c):
    for t in range(CT):
        ch.do(v.bn_stats(st[:, t, :], y[:, t, :]))
    ch.wait()
    dve.sem_inc(held, 1)
    for t in range(CT):
        ch.do(v.bn_aggr(mv[:, t, :], st[:, t, :]))
    ch.wait()
    v.tensor_scalar(sd[:, 0, :], mv[:, :, 1], EPS, None, ALU.add).then_inc(eps_ready, 1)
    dve.wait_ge(sd_ready, c + 1)
    ch.link(v.reciprocal(sd[:, 1, :], sd[:, 1, :]))
    for t in range(CT):
        ins = v.tensor_scalar(y[:, t, :], y[:, t, :], mv[:, t, 0:1], sd[:, 1, t:t + 1], ALU.subtract, ALU.mult)
    ins.then_inc(done, 1)


def phase_gate(nc, m, d, w, sem):
    w_ready = sem("weights_loaded")
    ws_ready = sem("weights_ready")
    wstep = sem("weight_step")
    step = sem("norm_step")
    in_ready = [sem(f"base_loaded{b}") for b in range(2)]
    added = sem("base_added")
    y_done = sem("x3_ready")
    stored = [sem(f"x3_stored{b}") for b in range(2)]
    eps_ready = sem("var_eps")
    sd_ready = sem("deviation")
    held = sem("held")
    t_ready = sem("x3T_ready")
    t_copied = sem("x3T_copied")
    o_ready = sem("support_ready")
    o_copied = sem("support_copied")
    gate_ready = sem("gate")
    with ExitStack() as ctx:
        sb, ps = buf_maker(nc, ctx, "ga")
        wsup = sb("wsup", [P, 2, D + 1])
        a2 = sb("a2", [P, D])
        wa = sb("wa", [P, 2, D])
        base = [sb(f"base{b}", [P, CT, D]) for b in range(2)]
        y = [sb(f"y{b}", [P, CT, D]) for b in range(2)]
        deg = sb("deg", [P, CT])
        st = sb("st", [P, CT, 6])
        mv = sb("mv", [P, CT, 2])
        sd = sb("sd", [P, 2, CT])
        yT = [sb(f"yT{b}", [P, 2, P]) for b in range(2)]
        gate = sb("gate", [P, NT])
        psT = [ps(f"psT{b}", [P, 2, P]) for b in range(2)]
        psO = [ps(f"psO{b}", [P, 512]) for b in range(2)]
        sums = m.sums[:].rearrange("p (n k) -> p n k", k=D + 1)
        gated = m.gated[:].rearrange("p (n k) -> p n k", k=D + 1)

        with nc.Block() as block:
            @block.sync
            def _(sp):
                sp.dma_start(wsup[:, :, 0:D], w["s_W"].rearrange("(k p) n -> p k n", p=P)).then_inc(w_ready, 16)
                sp.dma_start(a2[:], w["s_a2"].rearrange("k o -> o k").to_broadcast([P, D])).then_inc(w_ready, 16)
                with sp.Fori(0, NCK // 2) as it:
                    for b in range(2):
                        c = it * 2 + b
                        sp.wait_ge(added, c + 1)
                        sp.dma_start(base[b][:], chunk_of(d.base, c)).then_inc(in_ready[b], 16)

            @block.gpsimd
            def _(pool):
                with pool.Fori(0, NCK // 2) as it:
                    for b in range(2):
                        c = it * 2 + b
                        pool.wait_ge(y_done, c + 1)
                        pool.sem_inc(held, 1)
                        pool.dma_start(chunk_of(d.h, c), y[b][:]).then_inc(stored[b], 16)
                for b in range(2):
                    pool.wait_ge(stored[b], 16 * (NCK // 2))

            @block.tensor
            def _(pe):
                pe.wait_ge(ws_ready, 1)
                pe.sem_inc(t_ready, 2 * CT)
                pe.sem_inc(o_ready, 2)
                with pe.Fori(0, NCK // 2) as it:
                    for b in range(2):
                        c = it * 2 + b
                        pe.wait_ge(y_done, c + 1)
                        for turned, t in CHUNK_ORDER:
                            q = (b * CT + t) % 2
                            n = c * CT + t
                            if turned:
                                pe.wait_ge(t_copied, n + 1)
                                for k in range(2):
                                    ins = nc.tensor.transpose(psT[q][:, k, :], y[b][:, t, k * P:(k + 1) * P], m.ident[:])
                                ins.then_inc(t_ready, 1)
                            else:
                                pe.wait_ge(t_copied, n + 3)
                                pe.wait_ge(o_copied, n + 1)
                                for k in range(2):
                                    ins = nc.tensor.matmul(psO[q][:, 0:D + 1], yT[q][:, k, :], wsup[:, k, :], start=(k == 0), stop=(k == 1))
                                ins.then_inc(o_ready, 1)

            @block.scalar
            def _(act):
                act.sem_inc(t_copied, 2)
                act.sem_inc(o_copied, 2)
                with act.Fori(0, NCK // 2) as it:
                    for b in range(2):
                        c = it * 2 + b
                        act.wait_ge(eps_ready, c + 1)
                        nc.scalar.activation(sd[:, 1, :], sd[:, 0, :], ACT.Sqrt).then_inc(sd_ready, 1)
                        for turned, t in CHUNK_ORDER:
                            q = (b * CT + t) % 2
                            n = c * CT + t
                            if turned:
                                act.wait_ge(t_ready, n + 1 + 2 * CT)
                                act.wait_ge(o_ready, n + 1)
                                nc.scalar.copy(yT[q][:], psT[q][:]).then_inc(t_copied, 1)
                            else:
                                act.wait_ge(o_ready, n + 3)
                                nc.scalar.copy(m.gated[:, bass.ds(n * (D + 1), D + 1)], psO[q][:, 0:D + 1]).then_inc(o_copied, 1)
                act.wait_ge(o_copied, NT + 2)
                nc.scalar.activation(gate[:].unsqueeze(2), gated[:, :, D:D + 1], ACT.Sigmoid).then_inc(gate_ready, 1)

            @block.vector
            def _(dve):
                v = nc.vector
                wch = Chain(dve, wstep)
                dve.sem_inc(added, 2)
                dve.wait_ge(w_ready, 32)
                wch.link(v.tensor_tensor(wa[:], wsup[:, :, 0:D], a2[:].unsqueeze(1).to_broadcast([P, 2, D]), ALU.mult))
                v.tensor_reduce(wsup[:, :, D:D + 1], wa[:], AX_X, ALU.add).then_inc(ws_ready, 1)
                ch = Chain(dve, step, NORM_STEPS + 3)

                def chunk(c, b, turn, reused):
                    ch.turn(c)
                    cs = bass.ds(c * CT, CT)
                    if reused:
                        dve.wait_ge(stored[b], turn * 16)
                    dve.wait_ge(t_ready, c * CT + CT)
                    ch.link(v.tensor_scalar(deg[:].unsqueeze(2), sums[:, cs, D:D + 1], 1.0, None, ALU.max))
                    ch.link(v.reciprocal(deg[:], deg[:]))
                    ch.link(v.tensor_tensor(y[b][:], sums[:, cs, 0:D], deg[:].unsqueeze(2).to_broadcast([P, CT, D]), ALU.mult))
                    dve.wait_ge(in_ready[b], turn * 16 + 16)
                    v.tensor_tensor(y[b][:], y[b][:], base[b][:], ALU.add).then_inc(added, 1)
                    dve.wait_ge(added, c + 3)
                    norm_chunk(v, dve, ch, y[b], st, mv, sd, eps_ready, sd_ready, y_done, held, c)
                    ch.close()
                for b in range(2):
                    chunk(b, b, 0, False)
                with dve.Fori(1, NCK // 2) as it:
                    for b in range(2):
                        chunk(it * 2 + b, b, it, True)
                dve.wait_ge(gate_ready, 1)
                for t in range(0, NT, NT // 2):
                    ts = slice(t, t + NT // 2)
                    wch.do(v.tensor_tensor(gated[:, ts, 0:D], gated[:, ts, 0:D], gate[:, ts].unsqueeze(2).to_broadcast([P, NT // 2, D]), ALU.mult))
                wch.do(v.tensor_copy(gated[:, :, D:D + 1], gate[:].unsqueeze(2)))
                wch.wait()


def phase_scatter(nc, m, d, sem):
    K = D + 1
    HALF = GROUP // 2
    step = sem("prepare_step")
    diag_ready = sem("diagonals")
    s_ready = sem("sources_spread")
    hot_ready = sem("weighted_onehots")
    same_ready = sem("same_source")
    gstep = sem("index_step")
    idx_ready = sem("index_ready")
    b_ready = sem("pickers")
    b_copied = sem("pickers_copied")
    r_ready = sem("rows_ready")
    r_copied = sem("rows_copied")
    passed = sem("scatter_passed")
    bank_free = sem("rows_bank_free")
    idxf_ready = sem("index_value")
    done = [sem(f"scattered{k}") for k in range(K_ACC)]
    NTURN = NG // SETS
    PER = 2
    with ExitStack() as ctx:
        sb, ps = buf_maker(nc, ctx, "sc")
        srcv = sb("srcv", [P, S + 2 * GROUP])
        delta = sb("delta", [P, S + 2 * GROUP])
        valid = sb("valid", [P, S + 2 * GROUP])
        own = sb("own", [P, 2])
        later = sb("later", [P, P])
        diag = sb("diag", [P, GROUP, P])
        hot = sb("hot", [P, GROUP, P])
        same = sb("same", [P, GROUP, P])
        low = sb("low", [P, GROUP, P])
        count = sb("count", [P, GROUP])
        idxf = sb("idxf", [P, GROUP])
        idx = [sb(f"idx{b}", [P, GROUP], I32) for b in range(SETS)]
        pick = [sb(f"pick{b}", [P, GROUP, P]) for b in range(2)]
        rows = [sb(f"rows{b}", [P, GROUP, K]) for b in range(2)]
        psS = [ps(f"psS{h}", [P, HALF, P]) for h in range(2)]
        psB = [ps(f"psB{h}", [P, HALF, P]) for h in range(2)]
        psR = [ps(f"psR{q}", [P, 512]) for q in range(4)]
        with nc.Block() as block:
            @block.gpsimd
            def _(pool):
                def scatter(g, b, first):
                    pool.wait_ge(idx_ready, g + 1)
                    for j in range(GROUP):
                        i = g * GROUP + j
                        k = j % K_ACC
                        pool.wait_ge(r_copied, i + 1)
                        if not (first and j < K_ACC):
                            pool.wait_ge(done[k], (g * (GROUP // K_ACC) + j // K_ACC) * 16)
                        pool.sem_inc(passed, 1)
                        pool.indirect_dma_start(d.acc[k][0:NR + P, :], bass.IndirectOffsetOnAxis(ap=idx[b][:, j:j + 1], axis=0),
                                                rows[b % 2][:, j, :], None, compute_op=ALU.add).then_inc(done[k], 16)
                for b in range(SETS):
                    scatter(b, b, b == 0)
                with pool.Fori(1, NTURN) as it:
                    for b in range(SETS):
                        scatter(it * SETS + b, b, False)
                for k in range(K_ACC):
                    pool.wait_ge(done[k], 16 * (S // K_ACC))

            @block.tensor
            def _(pe):
                regs = [pe.alloc_register(f"pe_sc_{j}") for j in range(GROUP)]
                pe.sem_inc(b_ready, 2)
                pe.sem_inc(s_ready, 1)

                def spread(g):
                    pe.wait_ge(diag_ready, g + 1)
                    pe.wait_ge(same_ready, g + 1)
                    for h in range(2):
                        ins = nc.tensor.matmul(psS[h][:].rearrange("p j e -> p (j e)"), m.ones[:], diag[:, h * HALF:(h + 1) * HALF, :].rearrange("p j e -> p (j e)"), start=True, stop=True)
                    ins.then_inc(s_ready, 1)

                def pickers(g, h):
                    if h == 0:
                        pe.wait_ge(hot_ready, g + 1)
                        pe.wait_ge(same_ready, g + 2)
                    pe.wait_ge(b_copied, g * 2 + h + 1)
                    for j in range(h * HALF, (h + 1) * HALF):
                        ins = nc.tensor.matmul(psB[h][:, j - h * HALF, :], hot[:, j, :], same[:, j, :], start=True, stop=True)
                    ins.then_inc(b_ready, 1)

                def row(g, b, j, ns):
                    i = g * GROUP + j
                    if j % HALF == 0:
                        pe.wait_ge(b_copied, g * 2 + j // HALF + 3)
                    pe.wait_ge(bank_free, i + 1)
                    nc.tensor.matmul(psR[j % 4][:, 0:K], pick[b % 2][:, j, :], m.gated[:, bass.ds(ns[j] * K, K)], start=True, stop=True).then_inc(r_ready, 1)
                spread(0)
                pickers(0, 0)
                pickers(0, 1)
                with pe.Fori(0, NTURN) as it:
                    for b in range(SETS):
                        g = it * SETS + b
                        pe.load(regs, m.nrow[0:1, bass.ds(g * GROUP, GROUP)])
                        ns = [pe.snap(r, min_val=0, max_val=NT - 1) for r in regs]
                        spread(g + 1)
                        for j in range(4):
                            row(g, b, j, ns)
                        pickers(g + 1, 0)
                        row(g, b, 4, ns)
                        row(g, b, 5, ns)
                        pickers(g + 1, 1)
                        row(g, b, 6, ns)
                        row(g, b, 7, ns)

            @block.scalar
            def _(act):
                act.sem_inc(b_copied, 2)
                act.sem_inc(passed, 2 * GROUP)
                act.sem_inc(bank_free, 4)

                def copy_pick(g, b, h):
                    act.wait_ge(b_ready, g * 2 + h + 3)
                    nc.scalar.copy(pick[b % 2][:, h * HALF:(h + 1) * HALF, :], psB[h][:]).then_inc(b_copied, 1)

                def copy_row(g, b, j):
                    i = g * GROUP + j
                    act.wait_ge(r_ready, i + 1)
                    act.wait_ge(passed, i + K_ACC + 1)
                    nc.scalar.copy(rows[b % 2][:, j, :], psR[j % 4][:, 0:K]).then_inc(r_copied, 1)
                    act.wait_ge(r_copied, i + 1)
                    act.sem_inc(bank_free, 1)
                for h in range(2):
                    copy_pick(0, 0, h)
                with act.Fori(0, NTURN) as it:
                    for b in range(SETS):
                        g = it * SETS + b
                        b1 = (b + 1) % SETS
                        for j in range(4):
                            copy_row(g, b, j)
                        copy_pick(g + 1, b1, 0)
                        copy_row(g, b, 4)
                        copy_row(g, b, 5)
                        copy_pick(g + 1, b1, 1)
                        copy_row(g, b, 6)
                        copy_row(g, b, 7)

            @block.vector
            def _(dve):
                v = nc.vector
                ch = Chain(dve, step)
                gch = Chain(dve, gstep, PER)
                ch.do(v.tensor_scalar(own[:, 0:1], m.pidx[:], -1.0, -1.0, ALU.mult, ALU.add))
                ch.do(v.tensor_scalar(own[:, 1:2], m.pidx[:], float(NR), None, ALU.add))
                ch.do(v.tensor_scalar(later[:], m.iota[:, 0:P], m.pidx[:, 0:1], None, ALU.is_lt))
                ch.do(v.tensor_scalar(valid[:], m.loc[:], 0.0, None, ALU.is_ge))
                ch.do(v.tensor_scalar(delta[:], m.loc[:], float(P), None, ALU.is_lt))
                ch.do(v.tensor_copy(srcv[:], m.src_slot[:]))
                ch.wait()
                ch.link(v.tensor_tensor(valid[:], valid[:], delta[:], ALU.mult))
                ch.link(v.tensor_scalar(delta[:], srcv[:], own[:, 1:2], None, ALU.subtract))
                ch.do(v.tensor_tensor(delta[:], delta[:], valid[:], ALU.mult))
                ch.link(v.tensor_scalar(srcv[:], srcv[:], own[:, 0:1], None, ALU.subtract))
                ch.link(v.tensor_tensor(srcv[:], srcv[:], valid[:], ALU.mult))
                ch.link(v.tensor_scalar(srcv[:], srcv[:], own[:, 0:1], None, ALU.add))
                dve.sem_inc(same_ready, 1)
                dve.sem_inc(gstep, PER)

                def prepare(g, b):
                    gch.turn(g + 1)
                    gs = bass.ds(g * GROUP, GROUP)
                    src = srcv[:, gs]
                    dve.wait_ge(s_ready, g + 1)
                    v.tensor_tensor(diag[:], m.ident[:].unsqueeze(1).to_broadcast([P, GROUP, P]), src.unsqueeze(2).to_broadcast([P, GROUP, P]), ALU.mult).then_inc(diag_ready, 1)
                    dve.wait_ge(b_ready, g * 2 + 2)
                    for j in range(GROUP):
                        i = g * GROUP + j
                        ins = v.tensor_scalar(hot[:, j, :], m.iota[:, 0:P], m.loc[:, bass.ds(i, 1)], m.w_slot[:, bass.ds(i, 1)], ALU.is_equal, ALU.mult)
                    ins.then_inc(hot_ready, 1)
                    dve.wait_ge(s_ready, g + 2)
                    dve.wait_ge(gstep, g * PER + PER)
                    for h in range(2):
                        hs = slice(h * HALF, (h + 1) * HALF)
                        ins = v.tensor_tensor(same[:, hs, :], psS[h][:], srcv[:, bass.ds(g * GROUP + h * HALF, HALF)].unsqueeze(2).to_broadcast([P, HALF, P]), ALU.is_equal)
                    ins.then_inc(same_ready, 1)
                    dve.wait_ge(same_ready, g + 2)
                    gch.link(v.tensor_tensor(low[:], same[:], later[:].unsqueeze(1).to_broadcast([P, GROUP, P]), ALU.mult))
                    gch.link(v.tensor_reduce(count[:], low[:], AX_X, ALU.add))
                    dve.wait_ge(passed, g * GROUP)
                    v.scalar_tensor_tensor(out=idxf[:], in0=count[:], scalar=0.0, in1=delta[:, gs], op0=ALU.is_equal, op1=ALU.mult).then_inc(idxf_ready, 1)
                    dve.wait_ge(idxf_ready, g + 1)
                    v.tensor_scalar(idx[b][:], idxf[:], own[:, 1:2], None, ALU.add).then_inc(idx_ready, 1)
                    gch.close()
                prepare(0, 0)
                with dve.Fori(0, NTURN) as it:
                    for b in range(SETS):
                        prepare(it * SETS + b + 1, (b + 1) % SETS)


def phase_last(nc, m, d, w, out, sem):
    K = D + 1
    a_ready = sem("a1_loaded")
    t_ready = [sem(f"tables_loaded{b}") for b in range(2)]
    added = sem("tables_added")
    step = sem("sum_step")
    nstep = sem("norm_step")
    abs_ready = sem("abs")
    exp_ready = sem("exp")
    log_arg = sem("one_plus_exp")
    log_ready = sem("log")
    soft_step = sem("softplus_step")
    x_ready = [sem(f"x3_loaded{b}") for b in range(2)]
    neg_ready = sem("negative_part")
    elu_ready = sem("elu")
    y_done = sem("out_ready")
    stored = [sem(f"out_stored{b}") for b in range(2)]
    eps_ready = sem("var_eps")
    sd_ready = sem("deviation")
    held = sem("held")
    with ExitStack() as ctx:
        sb, _ = buf_maker(nc, ctx, "la")
        a1 = sb("a1", [P, D])
        o = sb("o", [P, NT, D])
        t = [sb(f"t{b}", [P, K_ACC, CT, K]) for b in range(2)]
        norm = sb("norm", [P, CT])
        no_node = sb("no_node", [P, NT])
        prod = sb("prod", [P, CT, D])
        z = sb("z", [P, NT])
        e = sb("e", [P, NT])
        x = [sb(f"x{b}", [P, CT, D]) for b in range(2)]
        y = [sb(f"y{b}", [P, CT, D]) for b in range(2)]
        st = sb("st", [P, CT, 6])
        mv = sb("mv", [P, CT, 2])
        sd = sb("sd", [P, 2, CT])
        with nc.Block() as block:
            @block.sync
            def _(sp):
                sp.dma_start(a1[:], w["s_a1"].rearrange("k o -> o k").to_broadcast([P, D])).then_inc(a_ready, 16)
                with sp.Fori(0, NCK // 2) as it:
                    for b in range(2):
                        c = it * 2 + b
                        sp.wait_ge(added, c + 1)
                        for k in range(K_ACC):
                            sp.dma_start(t[b][:, k, :, :], d.acc[k][bass.ds(c * (CT * P), CT * P), :].rearrange("(t p) k -> p t k", p=P)).then_inc(t_ready[b], 16)
                with sp.Fori(0, NCK // 2) as it:
                    for b in range(2):
                        c = it * 2 + b
                        sp.wait_ge(y_done, c + 1)
                        sp.dma_start(x[b][:], chunk_of(d.h, c)).then_inc(x_ready[b], 16)

            @block.gpsimd
            def _(pool):
                with pool.Fori(0, NCK // 2) as it:
                    for b in range(2):
                        c = it * 2 + b
                        pool.wait_ge(y_done, c + 3)
                        pool.sem_inc(held, 1)
                        pool.dma_start(chunk_of(out, c), y[b][:]).then_inc(stored[b], 16)
                for b in range(2):
                    pool.wait_ge(stored[b], 16 * (NCK // 2))

            @block.scalar
            def _(act):
                act.wait_ge(abs_ready, 1)
                nc.scalar.activation(e[:], e[:], ACT.Exp).then_inc(exp_ready, 1)
                act.wait_ge(log_arg, 1)
                nc.scalar.activation(e[:], e[:], ACT.Ln).then_inc(log_ready, 1)
                with act.Fori(0, NCK // 2) as it:
                    for b in range(2):
                        c = it * 2 + b
                        act.wait_ge(neg_ready, c + 1)
                        nc.scalar.activation(prod[:], y[b][:], ACT.Exp).then_inc(elu_ready, 1)
                        act.wait_ge(eps_ready, c + 1)
                        nc.scalar.activation(sd[:, 1, :], sd[:, 0, :], ACT.Sqrt).then_inc(sd_ready, 1)

            @block.vector
            def _(dve):
                v = nc.vector
                ch = Chain(dve, step, K_ACC + 3)
                dve.sem_inc(added, 2)
                sch = Chain(dve, soft_step)
                sch.do(v.tensor_scalar(no_node[:, 0:NT - 1], m.mask[:, 0:1].to_broadcast([P, NT - 1]), -1.0, 1.0, ALU.mult, ALU.add))
                sch.do(v.tensor_scalar(no_node[:, NT - 1:NT], m.mask[:, 1:2], -1.0, 1.0, ALU.mult, ALU.add))
                sch.wait()
                dve.wait_ge(a_ready, 16)
                with dve.Fori(0, NCK // 2) as it:
                    for b in range(2):
                        c = it * 2 + b
                        cs = bass.ds(c * CT, CT)
                        ch.turn(c)
                        dve.wait_ge(t_ready[b], it * (16 * K_ACC) + 16 * K_ACC)
                        for k in range(1, K_ACC):
                            ch.link(v.tensor_tensor(t[b][:, 0, :, :], t[b][:, 0, :, :], t[b][:, k, :, :], ALU.add))
                        ch.link(v.tensor_tensor(norm[:].unsqueeze(2), t[b][:, 0, :, D:K], no_node[:, cs].unsqueeze(2), ALU.add))
                        ch.link(v.reciprocal(norm[:], norm[:]))
                        v.tensor_tensor(o[:, cs, :], t[b][:, 0, :, 0:D], norm[:].unsqueeze(2).to_broadcast([P, CT, D]), ALU.mult).then_inc(added, 1)
                        dve.wait_ge(added, c + 3)
                        ch.link(v.tensor_tensor(prod[:], o[:, cs, :], a1[:].unsqueeze(1).to_broadcast([P, CT, D]), ALU.mult))
                        ch.link(v.tensor_reduce(z[:, cs], prod[:], AX_X, ALU.add))
                        ch.close()
                sch.link(v.scalar_tensor_tensor(out=e[:], in0=z[:], scalar=-1.0, in1=z[:], op0=ALU.mult, op1=ALU.min))
                dve.sem_inc(abs_ready, 1)
                dve.wait_ge(exp_ready, 1)
                v.tensor_scalar(e[:], e[:], 1.0, None, ALU.add).then_inc(log_arg, 1)
                dve.wait_ge(log_ready, 1)
                sch.link(v.scalar_tensor_tensor(out=z[:], in0=z[:], scalar=0.0, in1=e[:], op0=ALU.max, op1=ALU.add))
                nch = Chain(dve, nstep, NORM_STEPS + 2)
                dve.sem_inc(y_done, 2)

                def finish(c, b, turn, reused):
                    nch.turn(c)
                    cs = bass.ds(c * CT, CT)
                    if reused:
                        dve.wait_ge(stored[b], turn * 16)
                    v.scalar_tensor_tensor(out=y[b][:], in0=o[:, cs, :], scalar=0.0, in1=z[:, cs].unsqueeze(2).to_broadcast([P, CT, D]), op0=ALU.min, op1=ALU.mult).then_inc(neg_ready, 1)
                    dve.wait_ge(elu_ready, c + 1)
                    nch.link(v.scalar_tensor_tensor(out=y[b][:], in0=o[:, cs, :], scalar=0.0, in1=prod[:], op0=ALU.max, op1=ALU.add))
                    dve.wait_ge(x_ready[b], turn * 16 + 16)
                    nch.link(v.scalar_tensor_tensor(out=y[b][:], in0=y[b][:], scalar=-1.0, in1=x[b][:], op0=ALU.add, op1=ALU.add))
                    norm_chunk(v, dve, nch, y[b], st, mv, sd, eps_ready, sd_ready, y_done, held, c)
                    nch.close()
                for b in range(2):
                    finish(b, b, 0, False)
                with dve.Fori(1, NCK // 2) as it:
                    for b in range(2):
                        finish(it * 2 + b, b, it, True)


def build(nc, d, w, out):
    m = Mem()
    with ExitStack() as ctx:
        def sb(name, shape, dt=F32):
            return ctx.enter_context(nc.sbuf_tensor(name, shape, dt))
        SX = S + 2 * GROUP
        m.iota = sb("iota", [P, S])
        m.pidx = sb("pidx", [P, 1])
        m.ones = sb("ones", [P, P])
        m.zeros = sb("zeros", [P, D + 1])
        m.minus_one = sb("minus_one", [1, P])
        m.ident = sb("ident", [P, P])
        m.mask = sb("mask", [P, 2])
        m.is_p0 = sb("is_p0", [P, 1])
        m.node_mask = sb("node_mask", [P, 2, P])
        m.src_slot = sb("src_slot", [P, SX], I32)
        m.rel_slot = sb("rel_slot", [P, SX], I32)
        m.w_slot = sb("w_slot", [P, SX])
        m.first = sb("first", [P, SX])
        m.loc = sb("loc", [P, SX])
        m.loc_m = sb("loc_m", [P, SX])
        m.trow = sb("trow", [1, SX], I32)
        m.nrow = sb("nrow", [1, SX], I32)
        m.carry_b = sb("carry_b", [H, S])
        m.carry_col = sb("carry_col", [P, SCH])
        m.step_chunk_f = sb("step_chunk_f", [P, KS])
        m.step_rel = sb("step_rel", [P, KS])
        m.step_chunk = sb("step_chunk", [1, KS], I32)
        m.step_tile = sb("step_tile", [1, KS], I32)

        sems = []

        def phase(name):
            def sem(s):
                sems.append(nc.alloc_semaphore(name=f"{name}_{s}"))
                return sems[-1]
            return sem

        def recycle():
            nc.clear_and_free_semaphores(sems)
            nc.all_engine_barrier()
            sems.clear()
        phase_constants(nc, m, phase("const"))
        m.w_conv_in = sb("w_conv_in", [P, 2, FILT])
        m.w_conv_out = sb("w_conv_out", [FILT, D])
        m.b_conv_out = sb("b_conv_out", [1, D])
        m.w_radial = sb("w_radial", [RADIAL, FILT])
        gat_ctx = ctx.enter_context(ExitStack())
        m.self_term = gat_ctx.enter_context(nc.sbuf_tensor("self_term", [P, 2 * H], F32))
        m.fold = gat_ctx.enter_context(nc.sbuf_tensor("fold", [39, P // 4], F32))
        m.type_row = gat_ctx.enter_context(nc.sbuf_tensor("type_row", [P, 1], F32))
        m.w_table = gat_ctx.enter_context(nc.sbuf_tensor("w_table", [P, 2, D + 2 * H], F32))
        m.a_ij = gat_ctx.enter_context(nc.sbuf_tensor("a_ij", [P, NT * 2 * H], F32))
        phase_index(nc, m, d, phase("index"))
        phase_places(nc, m, d, phase("pl"))
        phase_edge_weights(nc, m, d, w, phase("ew"))
        phase_edge_terms(nc, m, d, phase("et"))
        phase_conv_weights(nc, m, w, phase("cw"))
        phase_table_weights(nc, m, w, 1, phase("tw1"))
        phase_rows(nc, m, d, "x", None, m.w_table, d.table, TABW, phase("rwx"))
        for l in (1, 2):
            with ExitStack() as layer_ctx:
                m.agg = layer_ctx.enter_context(nc.sbuf_tensor(f"agg{l}", [P, NT * AGG], F32))
                phase_attention(nc, m, d, l, phase(f"at{l}"))
                mv = layer_ctx.enter_context(nc.sbuf_tensor(f"mv{l}", [P, NT * 2], F32))
                bn = layer_ctx.enter_context(nc.sbuf_tensor(f"bn{l}", [P, 2, D], F32))
                with ExitStack() as merge_ctx:
                    cagg = merge_ctx.enter_context(nc.sbuf_tensor(f"cagg{l}", [P, NT * AGG], F32))
                    fac = merge_ctx.enter_context(nc.sbuf_tensor(f"fac{l}", [P, 3, NT, H], F32))
                    phase_carry(nc, m, d, l, cagg, phase(f"cy{l}"))
                    phase_factors(nc, m, d, l, cagg, fac, phase(f"fa{l}"))
                    phase_project(nc, m, d, w, l, cagg, fac, mv, phase(f"pj{l}"))
                phase_norm(nc, m, d, w, l, d.x if l == 1 else d.h, mv, bn, phase(f"nm{l}"))
                if l == 1:
                    phase_table_weights(nc, m, w, 2, phase("tw2"))
                    phase_rows(nc, m, d, "h1", bn, m.w_table, d.table, TABW, phase("rwh1"))
                else:
                    phase_rows(nc, m, d, "x1", bn, m.w_conv_in, d.conv_table, FILT, phase("rwx1"))
            recycle()
        gat_ctx.close()

        with ExitStack() as conv_ctx:
            m.cut = conv_ctx.enter_context(nc.sbuf_tensor("cut", [P, SX], F32))
            m.sums = conv_ctx.enter_context(nc.sbuf_tensor("conv_sums", [P, NT * FILT], F32))
            phase_cutoff(nc, m, phase("cut"))
            phase_sum_messages(nc, m, d, "conv", d.conv_table[:, :], m.src_slot, phase("conv"))
            phase_conv_out(nc, m, d, phase("co"))
        recycle()
        phase_rel_tables(nc, m, d, w, phase("rt"))
        with nc.sbuf_tensor("gated", [P, NT * (D + 1)], F32) as m.gated:
            with nc.sbuf_tensor("rel_sums", [P, NT * (D + 1)], F32) as m.sums:
                phase_sum_messages(nc, m, d, "rel", d.rel_table[:, :], m.rel_slot, phase("rel"))
                phase_gate(nc, m, d, w, phase("gate"))
            recycle()
            phase_scatter(nc, m, d, phase("scatter"))
        phase_last(nc, m, d, w, out, phase("last"))


def kernel(**inputs):
    import numpy as np
    import concourse.bacc as bacc
    from concourse.bass_utils import run_bass_kernel_spmd

    nc = bacc.Bacc("TRN2", target_bir_lowering=False, num_devices=1)
    a = {k: np.asarray(v) for k, v in inputs.items()}

    def edge_tiles(v, pad):
        out = np.full((TP * P,) + v.shape[1:], pad, v.dtype)
        out[:N_EDGES] = v
        return out
    dst_ext = np.full((TP + 2) * P, PAD_DST, np.int32)
    dst_ext[:P] = -1
    dst_ext[P:P + N_EDGES] = a["dst"]
    x_tiles = np.zeros((NT, P, D), np.float32)
    padded = np.zeros((NT * NPT, D), np.float32)
    padded[:N_NODES] = a["x"]
    x_tiles[:, 1:, :] = padded.reshape(NT, NPT, D)
    arrays = {
        "dst_ext": dst_ext.reshape(TP + 2, P),
        "src": edge_tiles(a["src"], 0).reshape(TP, P),
        "type8": edge_tiles(a["edge_type_8"], 0).reshape(TP, P),
        "type7": edge_tiles(a["edge_type_7"], 0).reshape(1, TP * P),
        "weight": edge_tiles(a["edge_weight"], 0.0).reshape(TP, P),
        "attr16_T": np.ascontiguousarray(edge_tiles(a["edge_attr_16"], 0.0).T),
        "attr12_T": np.ascontiguousarray(edge_tiles(a["edge_attr_12"], 0.0).T),
        "x": x_tiles,
    }
    for name, v in a.items():
        for l, short in (("L0_gnn_", "g_"), ("L1_gnn_", "c_"), ("L2_gnn_", "r_"), ("L3_gnn_", "s_")):
            if name.startswith(l):
                arrays[short + name[len(l):]] = v
    for k in ("c_W_radial_to_message", "c_W_lin1", "c_W_message_to_node", "r_sl_w"):
        arrays[k + "_T"] = np.ascontiguousarray(arrays[k].T)
    d, w = Mem(), {}
    handles = {}
    for k, v in arrays.items():
        handles[k] = nc.dram_tensor("in_" + k, v.shape, mybir.dt.from_np(v.dtype), kind="ExternalInput").ap()
    d.dst_ext, d.src, d.type8, d.type7, d.weight = (handles[k] for k in ("dst_ext", "src", "type8", "type7", "weight"))
    d.attr16_T, d.attr12_T, d.x = handles["attr16_T"], handles["attr12_T"], handles["x"]
    for k, h in handles.items():
        if k[1:2] == "_":
            w[k if k[0] != "g" else k[2:]] = h

    def dram(name, shape):
        return nc.dram_tensor(name, shape, F32, kind="Internal").ap()
    d.carry_rows = dram("carry_rows", (1, SCH * P))
    d.places = nc.dram_tensor("places", (S + 2 * GROUP, P), BF16, kind="Internal").ap()
    d.terms = [dram(f"terms{l}", (P, TX * H)) for l in (1, 2)]
    d.table = dram("table", (NR, TABW))
    d.h = dram("h", (NT, P, D))
    d.h2 = dram("h2", (NT, P, D))
    d.base = dram("base", (NT, P, D))
    d.conv_table = dram("conv_table", (NR, FILT))
    d.acc = [dram(f"acc{k}", (NR + P, D + 1)) for k in range(K_ACC)]
    d.rel_table = dram("rel_table", (N_REL * NR, D))
    d.carry = dram("carry", (S, AGG))
    out = nc.dram_tensor("out", (NT, P, D), F32, kind="ExternalOutput").ap()
    build(nc, d, w, out)
    r = run_bass_kernel_spmd(nc, [{"in_" + k: v for k, v in arrays.items()}], core_ids=[0])
    got = r.results[0]["out"]
    return np.ascontiguousarray(got[:, 1:, :].reshape(NT * NPT, D)[:N_NODES])
```
